# Optimizing a Trainium2 kernel written in Bass

```python
import numpy as np
import jax
import jax.numpy as jnp

def _softmax(x, axis=-1):
    return jax.nn.softmax(x, axis=axis)

def _gelu(x):
    return jax.nn.gelu(x, approximate=True)

def _silu(x):
    return jax.nn.silu(x)

def _sigmoid(x):
    return jax.nn.sigmoid(x)

def _layernorm(x, axis=-1, eps=1e-05):
    m = jnp.mean(x, axis=axis, keepdims=True)
    v = jnp.var(x, axis=axis, keepdims=True)
    return (x - m) / jnp.sqrt(v + eps)

def _scatter_add(tgt, idx, src, axis=0):
    return tgt.at[idx].add(src)

def _segment_sum(src, seg, n):
    return jax.ops.segment_sum(src, seg, n)
kernel_name = 'mk_adaln_d2_jaxref_r8_1e3980'

def setup_inputs(seed: int=0):
    np.random.seed(seed)
    _w = jnp.asarray

    def _L0_attn_setup():
        import jax, jax.numpy as jnp
        import numpy as np
        import math
        B, L, H, D, HID = (2, 128, 16, 64, 128)

        def _rope_tables(seq_len, dim):
            inv_freq = 1.0 / 10000.0 ** (jnp.arange(0, dim, 2, dtype=jnp.float32) / dim)
            t = jnp.arange(seq_len, dtype=jnp.float32)
            freqs = jnp.outer(t, inv_freq)
            emb = jnp.concatenate([freqs, freqs], -1)
            return (jnp.cos(emb), jnp.sin(emb))

        def _rotate_half(x):
            x1, x2 = jnp.split(x, 2, axis=-1)
            return jnp.concatenate([-x2, x1], axis=-1)

        def _apply_rope(x, cos, sin):
            return x * cos + _rotate_half(x) * sin

        def _forward(x, w_qkv, w_o, log_p, log_a, w1, b1, w2, b2):
            Bx, Lx, _ = x.shape
            qkv = jnp.dot(x, w_qkv).reshape(Bx, Lx, 3, H, D)
            qkv = jnp.transpose(qkv, (2, 0, 3, 1, 4))
            q, k, v = (qkv[0], qkv[1], qkv[2])
            cos, sin = _rope_tables(Lx, D)
            cos, sin = (cos[None, None], sin[None, None])
            q = _apply_rope(q, cos, sin)
            k = _apply_rope(k, cos, sin)
            scale = 1.0 / math.sqrt(D)
            scores = jnp.einsum('bhid,bhjd->bhij', q, k) * scale
            pos = jnp.arange(Lx, dtype=jnp.float32)
            dist = jnp.abs(pos[None, :] - pos[:, None])
            p = jax.nn.softplus(log_p)
            a = jax.nn.softplus(log_a)
            kerple = -p * jnp.log1p(a * dist[None])
            attn_t = jnp.transpose(scores, (0, 2, 3, 1))
            kerple_t = jnp.broadcast_to(jnp.transpose(kerple, (1, 2, 0))[None], attn_t.shape)
            combined = jnp.concatenate([attn_t, kerple_t], axis=-1)
            hdn = jax.nn.gelu(jnp.dot(combined, w1) + b1, approximate=False)
            refined = jnp.dot(hdn, w2) + b2
            refined = jnp.transpose(refined, (0, 3, 1, 2))
            scores = scores + kerple[None] + refined
            causal = jnp.tril(jnp.ones((Lx, Lx), dtype=bool))
            scores = jnp.where(causal[None, None], scores, -jnp.inf)
            weights = jax.nn.softmax(scores, axis=-1)
            out = jnp.einsum('bhij,bhjd->bhid', weights, v)
            out = jnp.transpose(out, (0, 2, 1, 3)).reshape(Bx, Lx, H * D)
            return jnp.dot(out, w_o)
        key = jax.random.key(seed)
        ks = jax.random.split(key, 8)
        s = 0.02
        return {'x': jax.random.normal(ks[0], (B, L, HID), jnp.float32), 'w_qkv': jax.random.normal(ks[1], (HID, 3 * H * D), jnp.float32) * s, 'w_o': jax.random.normal(ks[2], (H * D, HID), jnp.float32) * s, 'log_p': jax.random.normal(ks[3], (H, 1, 1), jnp.float32) * 0.02, 'log_a': jax.random.normal(ks[4], (H, 1, 1), jnp.float32) * 0.02, 'w1': jax.random.normal(ks[5], (2 * H, 2 * H), jnp.float32) * s, 'b1': jnp.zeros((2 * H,), jnp.float32), 'w2': jax.random.normal(ks[6], (2 * H, H), jnp.float32) * s, 'b2': jnp.zeros((H,), jnp.float32)}
    _L0_attn_in = _L0_attn_setup()

    def _L0_ffn_setup():
        import jax, jax.numpy as jnp
        import numpy as np
        TOP_K = 2

        def _route(x2d, gate_w, num_experts, top_k):
            scores = jax.nn.softmax((x2d @ gate_w.T).astype(jnp.float32), axis=1)
            top_scores, sel = jax.lax.top_k(scores, top_k)
            sel_flat = sel.reshape(-1)
            counts = jnp.bincount(sel_flat, length=num_experts)
            order = jnp.argsort(sel_flat, stable=True)
            top_scores_sorted = top_scores.reshape(-1)[order]
            token_idx = order // top_k
            return (top_scores_sorted, token_idx, counts)

        def _grouped_swiglu(xr, w1, w2, w3, eid):
            out = jnp.zeros((xr.shape[0], w2.shape[-1]), dtype=xr.dtype)
            for e in range(w1.shape[0]):
                xe = jnp.where((eid == e)[:, None], xr, 0.0)
                h = jax.nn.silu(xe @ w1[e]) * (xe @ w3[e])
                out = out + h @ w2[e]
            return out
        key = jax.random.key(seed)
        ks = jax.random.split(key, 5)
        bs, slen, dim, hidden, E = (2, 256, 128, 352, 8)
        x = jax.random.normal(ks[0], (bs, slen, dim), dtype=jnp.float32)
        gate_w = jax.random.normal(ks[1], (E, dim), dtype=jnp.float32) * 0.02
        w1 = jax.random.normal(ks[2], (E, dim, hidden), dtype=jnp.float32) * 0.02
        w2 = jax.random.normal(ks[3], (E, hidden, dim), dtype=jnp.float32) * 0.02
        w3 = jax.random.normal(ks[4], (E, dim, hidden), dtype=jnp.float32) * 0.02
        return {'x': x, 'gate_w': gate_w, 'w1': w1, 'w2': w2, 'w3': w3}
    _L0_ffn_in = _L0_ffn_setup()
    _L0_c = _w((lambda *s: np.random.randn(*s).astype(np.float32) * 0.05)(8, 128))
    _L0_wmod = _w((lambda *s: np.random.randn(*s).astype(np.float32) * 0.05)(128, 6 * 128) * 128 ** (-0.5))

    def _L1_attn_setup():
        import jax, jax.numpy as jnp
        import numpy as np
        D_MODEL = 128
        N_HEADS = 16
        N_GROUPS = 4
        D_K = D_MODEL // N_HEADS
        HEADS_PER_GROUP = N_HEADS // N_GROUPS

        def rope(x):
            s, d = (x.shape[1], x.shape[2])
            theta = 1.0 / 10000.0 ** (jnp.arange(d // 2, dtype=jnp.float32) / (d // 2))
            ang = jnp.arange(s, dtype=jnp.float32)[:, None] * theta[None, :]
            cos, sin = (jnp.cos(ang), jnp.sin(ang))
            xe, xo = (x[..., 0::2], x[..., 1::2])
            return jnp.concatenate([xe * cos - xo * sin, xe * sin + xo * cos], axis=-1)
        key = jax.random.key(seed)
        k1, k2, k3, k4, k5 = jax.random.split(key, 5)
        b, s = (1, 256)
        scale = 0.02
        X = jax.random.normal(k1, (b, s, D_MODEL), dtype=jnp.float32)
        W_q = jax.random.normal(k2, (D_MODEL, D_MODEL), dtype=jnp.float32) * scale
        W_k = jax.random.normal(k3, (N_GROUPS * D_K, D_MODEL), dtype=jnp.float32) * scale
        W_v = jax.random.normal(k4, (N_GROUPS * D_K, D_MODEL), dtype=jnp.float32) * scale
        W_o = jax.random.normal(k5, (D_MODEL, D_MODEL), dtype=jnp.float32) * scale
        return {'X': X, 'W_q': W_q, 'W_k': W_k, 'W_v': W_v, 'W_o': W_o}
    _L1_attn_in = _L1_attn_setup()

    def _L1_ffn_setup():
        import jax, jax.numpy as jnp
        import numpy as np
        L, E, H, F, K = (4, 4, 128, 512, 2)
        B, S = (4, 256)
        EPS = 1e-05

        def _moe_layer(x, rw, rb, g, b, w1, b1, w2, b2):
            logits = jnp.einsum('bsh,he->bse', x, rw) + rb
            probs = jax.nn.softmax(logits, axis=-1)
            vals, idx = jax.lax.top_k(probs, K)
            vals = vals / vals.sum(axis=-1, keepdims=True)
            mu = x.mean(axis=-1, keepdims=True)
            xc = x - mu
            xhat = xc * jax.lax.rsqrt((xc * xc).mean(axis=-1, keepdims=True) + EPS)
            xe = xhat[None] * g[:, None, None, :] + b[:, None, None, :]
            h = jax.nn.gelu(jnp.einsum('ebsh,ehf->ebsf', xe, w1) + b1[:, None, None, :], approximate=False)
            y = jnp.einsum('ebsf,efh->ebsh', h, w2) + b2[:, None, None, :]
            expert_out = x[None] + y
            comb = jnp.einsum('bsk,bske->bse', vals, jax.nn.one_hot(idx, E, dtype=x.dtype))
            return jnp.einsum('bse,ebsh->bsh', comb, expert_out)
        key = jax.random.key(seed)
        ks = jax.random.split(key, 4)
        return {'hidden_states': jax.random.normal(ks[0], (B, S, H), jnp.float32), 'router_w': 0.02 * jax.random.normal(ks[1], (L, H, E), jnp.float32), 'router_b': jnp.zeros((L, E), jnp.float32), 'ln_g': jnp.ones((L, E, H), jnp.float32), 'ln_b': jnp.zeros((L, E, H), jnp.float32), 'w1': 0.02 * jax.random.normal(ks[2], (L, E, H, F), jnp.float32), 'b1': jnp.zeros((L, E, F), jnp.float32), 'w2': 0.02 * jax.random.normal(ks[3], (L, E, F, H), jnp.float32), 'b2': jnp.zeros((L, E, H), jnp.float32)}
    _L1_ffn_in = _L1_ffn_setup()
    _L1_c = _w((lambda *s: np.random.randn(*s).astype(np.float32) * 0.05)(8, 128))
    _L1_wmod = _w((lambda *s: np.random.randn(*s).astype(np.float32) * 0.05)(128, 6 * 128) * 128 ** (-0.5))
    _d = {'L0_attn_x': _L0_attn_in['x'], 'L0_attn_w_qkv': _L0_attn_in['w_qkv'], 'L0_attn_w_o': _L0_attn_in['w_o'], 'L0_attn_log_p': _L0_attn_in['log_p'], 'L0_attn_log_a': _L0_attn_in['log_a'], 'L0_attn_w1': _L0_attn_in['w1'], 'L0_attn_b1': _L0_attn_in['b1'], 'L0_attn_w2': _L0_attn_in['w2'], 'L0_attn_b2': _L0_attn_in['b2'], 'L0_ffn_gate_w': _L0_ffn_in['gate_w'], 'L0_ffn_w1': _L0_ffn_in['w1'], 'L0_ffn_w2': _L0_ffn_in['w2'], 'L0_ffn_w3': _L0_ffn_in['w3'], 'L0_c': _L0_c, 'L0_wmod': _L0_wmod, 'L1_attn_W_q': _L1_attn_in['W_q'], 'L1_attn_W_k': _L1_attn_in['W_k'], 'L1_attn_W_v': _L1_attn_in['W_v'], 'L1_attn_W_o': _L1_attn_in['W_o'], 'L1_ffn_router_w': _L1_ffn_in['router_w'], 'L1_ffn_router_b': _L1_ffn_in['router_b'], 'L1_ffn_ln_g': _L1_ffn_in['ln_g'], 'L1_ffn_ln_b': _L1_ffn_in['ln_b'], 'L1_ffn_w1': _L1_ffn_in['w1'], 'L1_ffn_b1': _L1_ffn_in['b1'], 'L1_ffn_w2': _L1_ffn_in['w2'], 'L1_ffn_b2': _L1_ffn_in['b2'], 'L1_c': _L1_c, 'L1_wmod': _L1_wmod}
    _x0 = _d['L0_attn_x']
    _d['L0_attn_x'] = jax.random.normal(jax.random.fold_in(jax.random.key(seed), 1), (8, 256, 128), dtype=_x0.dtype)
    del _x0
    return _d

def reference(L0_attn_x, L0_attn_w_qkv, L0_attn_w_o, L0_attn_log_p, L0_attn_log_a, L0_attn_w1, L0_attn_b1, L0_attn_w2, L0_attn_b2, L0_ffn_gate_w, L0_ffn_w1, L0_ffn_w2, L0_ffn_w3, L0_c, L0_wmod, L1_attn_W_q, L1_attn_W_k, L1_attn_W_v, L1_attn_W_o, L1_ffn_router_w, L1_ffn_router_b, L1_ffn_ln_g, L1_ffn_ln_b, L1_ffn_w1, L1_ffn_b1, L1_ffn_w2, L1_ffn_b2, L1_c, L1_wmod):

    def _L0_attn_ref(x, w_qkv, w_o, log_p, log_a, w1, b1, w2, b2):
        import jax, jax.numpy as jnp
        import numpy as np
        import math
        B, L, H, D, HID = (2, 128, 16, 64, 128)

        def _rope_tables(seq_len, dim):
            inv_freq = 1.0 / 10000.0 ** (jnp.arange(0, dim, 2, dtype=jnp.float32) / dim)
            t = jnp.arange(seq_len, dtype=jnp.float32)
            freqs = jnp.outer(t, inv_freq)
            emb = jnp.concatenate([freqs, freqs], -1)
            return (jnp.cos(emb), jnp.sin(emb))

        def _rotate_half(x):
            x1, x2 = jnp.split(x, 2, axis=-1)
            return jnp.concatenate([-x2, x1], axis=-1)

        def _apply_rope(x, cos, sin):
            return x * cos + _rotate_half(x) * sin

        def _forward(x, w_qkv, w_o, log_p, log_a, w1, b1, w2, b2):
            Bx, Lx, _ = x.shape
            qkv = jnp.dot(x, w_qkv).reshape(Bx, Lx, 3, H, D)
            qkv = jnp.transpose(qkv, (2, 0, 3, 1, 4))
            q, k, v = (qkv[0], qkv[1], qkv[2])
            cos, sin = _rope_tables(Lx, D)
            cos, sin = (cos[None, None], sin[None, None])
            q = _apply_rope(q, cos, sin)
            k = _apply_rope(k, cos, sin)
            scale = 1.0 / math.sqrt(D)
            scores = jnp.einsum('bhid,bhjd->bhij', q, k) * scale
            pos = jnp.arange(Lx, dtype=jnp.float32)
            dist = jnp.abs(pos[None, :] - pos[:, None])
            p = jax.nn.softplus(log_p)
            a = jax.nn.softplus(log_a)
            kerple = -p * jnp.log1p(a * dist[None])
            attn_t = jnp.transpose(scores, (0, 2, 3, 1))
            kerple_t = jnp.broadcast_to(jnp.transpose(kerple, (1, 2, 0))[None], attn_t.shape)
            combined = jnp.concatenate([attn_t, kerple_t], axis=-1)
            hdn = jax.nn.gelu(jnp.dot(combined, w1) + b1, approximate=False)
            refined = jnp.dot(hdn, w2) + b2
            refined = jnp.transpose(refined, (0, 3, 1, 2))
            scores = scores + kerple[None] + refined
            causal = jnp.tril(jnp.ones((Lx, Lx), dtype=bool))
            scores = jnp.where(causal[None, None], scores, -jnp.inf)
            weights = jax.nn.softmax(scores, axis=-1)
            out = jnp.einsum('bhij,bhjd->bhid', weights, v)
            out = jnp.transpose(out, (0, 2, 1, 3)).reshape(Bx, Lx, H * D)
            return jnp.dot(out, w_o)
        return _forward(x, w_qkv, w_o, log_p, log_a, w1, b1, w2, b2)

    def _L0_ffn_ref(x, gate_w, w1, w2, w3):
        import jax, jax.numpy as jnp
        import numpy as np
        TOP_K = 2

        def _route(x2d, gate_w, num_experts, top_k):
            scores = jax.nn.softmax((x2d @ gate_w.T).astype(jnp.float32), axis=1)
            top_scores, sel = jax.lax.top_k(scores, top_k)
            sel_flat = sel.reshape(-1)
            counts = jnp.bincount(sel_flat, length=num_experts)
            order = jnp.argsort(sel_flat, stable=True)
            top_scores_sorted = top_scores.reshape(-1)[order]
            token_idx = order // top_k
            return (top_scores_sorted, token_idx, counts)

        def _grouped_swiglu(xr, w1, w2, w3, eid):
            out = jnp.zeros((xr.shape[0], w2.shape[-1]), dtype=xr.dtype)
            for e in range(w1.shape[0]):
                xe = jnp.where((eid == e)[:, None], xr, 0.0)
                h = jax.nn.silu(xe @ w1[e]) * (xe @ w3[e])
                out = out + h @ w2[e]
            return out
        bs, slen, dim = x.shape
        E, top_k = (gate_w.shape[0], TOP_K)
        x2d = x.reshape(bs * slen, dim)
        top_scores, token_idx, counts = _route(x2d, gate_w, E, top_k)
        routed_in = (x2d[token_idx].astype(jnp.float32) * top_scores[:, None]).astype(x.dtype)
        Tr = bs * slen * top_k
        eid = jnp.repeat(jnp.arange(E), counts, total_repeat_length=Tr)
        routed_out = _grouped_swiglu(routed_in, w1, w2, w3, eid)
        out = jnp.zeros((bs * slen, dim), dtype=x.dtype).at[token_idx].add(routed_out)
        return out.reshape(bs, slen, dim)

    def _L1_attn_ref(X, W_q, W_k, W_v, W_o):
        import jax, jax.numpy as jnp
        import numpy as np
        D_MODEL = 128
        N_HEADS = 16
        N_GROUPS = 4
        D_K = D_MODEL // N_HEADS
        HEADS_PER_GROUP = N_HEADS // N_GROUPS

        def rope(x):
            s, d = (x.shape[1], x.shape[2])
            theta = 1.0 / 10000.0 ** (jnp.arange(d // 2, dtype=jnp.float32) / (d // 2))
            ang = jnp.arange(s, dtype=jnp.float32)[:, None] * theta[None, :]
            cos, sin = (jnp.cos(ang), jnp.sin(ang))
            xe, xo = (x[..., 0::2], x[..., 1::2])
            return jnp.concatenate([xe * cos - xo * sin, xe * sin + xo * cos], axis=-1)
        b, s, _ = X.shape
        Xr = rope(X)
        Q = (Xr @ W_q.T).reshape(b, s, N_HEADS, D_K).transpose(0, 2, 1, 3)
        K = (Xr @ W_k.T).reshape(b, s, N_GROUPS, D_K).transpose(0, 2, 1, 3)
        V = (Xr @ W_v.T).reshape(b, s, N_GROUPS, D_K).transpose(0, 2, 1, 3)
        Q = Q.reshape(b, N_GROUPS, HEADS_PER_GROUP, s, D_K)
        scores = jnp.einsum('bghsd,bgtd->bghst', Q, K) / jnp.sqrt(jnp.float32(D_K))
        mask = jnp.triu(jnp.ones((s, s), dtype=scores.dtype), k=1) * -1000000000.0
        attn = jax.nn.softmax(scores + mask, axis=-1)
        out = jnp.einsum('bghst,bgtd->bghsd', attn, V)
        out = out.reshape(b, N_HEADS, s, D_K).transpose(0, 2, 1, 3).reshape(b, s, D_MODEL)
        return out @ W_o.T

    def _L1_ffn_ref(hidden_states, router_w, router_b, ln_g, ln_b, w1, b1, w2, b2):
        import jax, jax.numpy as jnp
        import numpy as np
        L, E, H, F, K = (4, 4, 128, 512, 2)
        B, S = (4, 256)
        EPS = 1e-05

        def _moe_layer(x, rw, rb, g, b, w1, b1, w2, b2):
            logits = jnp.einsum('bsh,he->bse', x, rw) + rb
            probs = jax.nn.softmax(logits, axis=-1)
            vals, idx = jax.lax.top_k(probs, K)
            vals = vals / vals.sum(axis=-1, keepdims=True)
            mu = x.mean(axis=-1, keepdims=True)
            xc = x - mu
            xhat = xc * jax.lax.rsqrt((xc * xc).mean(axis=-1, keepdims=True) + EPS)
            xe = xhat[None] * g[:, None, None, :] + b[:, None, None, :]
            h = jax.nn.gelu(jnp.einsum('ebsh,ehf->ebsf', xe, w1) + b1[:, None, None, :], approximate=False)
            y = jnp.einsum('ebsf,efh->ebsh', h, w2) + b2[:, None, None, :]
            expert_out = x[None] + y
            comb = jnp.einsum('bsk,bske->bse', vals, jax.nn.one_hot(idx, E, dtype=x.dtype))
            return jnp.einsum('bse,ebsh->bsh', comb, expert_out)
        x = hidden_states
        for l in range(L):
            x = _moe_layer(x, router_w[l], router_b[l], ln_g[l], ln_b[l], w1[l], b1[l], w2[l], b2[l])
        return x
    x = L0_attn_x
    mod = (_silu(L0_c) @ L0_wmod).reshape(L0_c.shape[0], 6, 1, -1)
    sa, ca, ga, sb, cb, gb = (mod[:, 0], mod[:, 1], mod[:, 2], mod[:, 3], mod[:, 4], mod[:, 5])
    ga = (2 * (ga >= 0) - 1) * jnp.maximum(jnp.abs(ga), 0.25)
    gb = (2 * (gb >= 0) - 1) * jnp.maximum(jnp.abs(gb), 0.25)
    h = _layernorm(x, axis=-1) * (1 + ca) + sa
    x = x + ga * _L0_attn_ref(h, L0_attn_w_qkv, L0_attn_w_o, L0_attn_log_p, L0_attn_log_a, L0_attn_w1, L0_attn_b1, L0_attn_w2, L0_attn_b2)
    h = _layernorm(x, axis=-1) * (1 + cb) + sb
    x = x + gb * _L0_ffn_ref(h, L0_ffn_gate_w, L0_ffn_w1, L0_ffn_w2, L0_ffn_w3)
    mod = (_silu(L1_c) @ L1_wmod).reshape(L1_c.shape[0], 6, 1, -1)
    sa, ca, ga, sb, cb, gb = (mod[:, 0], mod[:, 1], mod[:, 2], mod[:, 3], mod[:, 4], mod[:, 5])
    ga = (2 * (ga >= 0) - 1) * jnp.maximum(jnp.abs(ga), 0.25)
    gb = (2 * (gb >= 0) - 1) * jnp.maximum(jnp.abs(gb), 0.25)
    h = _layernorm(x, axis=-1) * (1 + ca) + sa
    x = x + ga * _L1_attn_ref(h, L1_attn_W_q, L1_attn_W_k, L1_attn_W_v, L1_attn_W_o)
    h = _layernorm(x, axis=-1) * (1 + cb) + sb
    x = x + gb * _L1_ffn_ref(h, L1_ffn_router_w, L1_ffn_router_b, L1_ffn_ln_g, L1_ffn_ln_b, L1_ffn_w1, L1_ffn_b1, L1_ffn_w2, L1_ffn_b2)
    return x

_drawn_inputs = setup_inputs


def setup_inputs(seed=0):
    import zlib

    import numpy as np

    out = dict(_drawn_inputs(seed))
    spreads = {'L0_attn_b1': (0.0, 0.8),
     'L0_attn_b2': (0.0, 2.0),
     'L1_ffn_router_b': (0.0, 0.388),
     'L1_ffn_ln_g': (1.0, 0.6),
     'L1_ffn_ln_b': (0.0, 0.8),
     'L1_ffn_b1': (0.0, 0.8),
     'L1_ffn_b2': (0.0, 0.371)}
    factors = {'L0_attn_w_qkv': 8.0,
     'L0_attn_w_o': 8.0,
     'L0_attn_log_p': 8.0,
     'L0_attn_log_a': 29.237,
     'L0_attn_w1': 8.0,
     'L0_attn_w2': 8.0,
     'L0_ffn_gate_w': 8.0,
     'L0_ffn_w1': 8.0,
     'L0_ffn_w2': 8.0,
     'L0_ffn_w3': 8.0,
     'L0_c': 8.0,
     'L0_wmod': 8.0,
     'L1_attn_W_q': 8.0,
     'L1_attn_W_k': 8.0,
     'L1_attn_W_v': 8.0,
     'L1_attn_W_o': 8.0,
     'L1_ffn_w1': 2.876}
    for name, (base, spread) in spreads.items():
        noise = np.random.default_rng([zlib.crc32(name.encode()), seed]).standard_normal(out[name].shape)
        drawn = base * np.exp(spread * noise) if base else spread * noise
        out[name] = jnp.asarray(drawn.astype(out[name].dtype))
    for name, factor in factors.items():
        out[name] = (out[name] * factor).astype(out[name].dtype)
    return out
```

```python
from contextlib import ExitStack

import numpy as np

import concourse.bass as bass
from concourse import mybir

ALU = mybir.AluOpType
ACT = mybir.ActivationFunctionType
AX = mybir.AxisListType
F32 = mybir.dt.float32

P = 128
B, L = 8, 256
T = B * L
CH = 512
NCH = T // CH
TB = T // P
EPS = 1e-5

H0, D0 = 16, 64
PAIRS = H0 // 2
IG = 8
UNITS = L // IG
UPB = P // IG
SPAN = L - IG + L
NEG = -1.0e30

E0, F0 = 8, 352
FC0 = 3

H1, D1, G1 = 16, 8, 4
R1 = H1 // G1

LY, E1, F1 = 4, 4, 512
FC1 = F1 // P
NPAR = 3 * E1 + E1 * FC1 + E1 + TB * E1


def unit_columns(u):
    if u < UPB:
        return P * u, P
    return P * UPB + L * (u - UPB), L


UCOLS = P * UPB + L * UPB


class Kit:
    pass


def load_parts(nc, done, parts):
    for dst, src in parts:
        nc.dma_start(dst, src).then_inc(done, 16)


def since(eng, sem, value):
    if not isinstance(value, int) or value > 0:
        eng.wait_ge(sem, value)


def setup_stage(k):
    nc = k.nc
    with ExitStack() as ctx:
        def sb(name, shape):
            return ctx.enter_context(nc.sbuf_tensor(name, shape, F32))

        def sem(name):
            return ctx.enter_context(nc.semaphore(name))

        wmod = sb("wmod", [P, 2, 6, P])
        c = sb("c_cols", [P, 2, B])
        sc = sb("silu_c", [P, 2, B])
        mag = sb("gate_magnitude", [P, 2, 2, B])
        sgn = sb("gate_sign", [P, 2, 2, B])
        ps = ctx.enter_context(nc.psum_tensor("mod_ps", [P, 2, 6, B], F32))
        loaded, silu_ready, mod_ready, mod_copied, gate_parts = (
            sem("setup_loaded"), sem("silu_ready"), sem("mod_ready"), sem("mod_copied"), sem("gate_parts"))
        block = ctx.enter_context(nc.Block())

        @block.sync
        def _(sp):
            load_parts(sp, loaded, [(c[:], k.d["c"]), (wmod[:], k.d["wmod"]), (k.ident[:], k.d["ident"]),
                                    (k.mean_mat[:], k.d["mean_mat"]), (k.x[:], k.d["x"])])
            sp.wait_ge(loaded, 80)

        @block.scalar
        def _(act):
            act.wait_ge(loaded, 80)
            act.activation(sc[:], c[:], ACT.Silu).then_inc(silu_ready, 1)

        @block.tensor
        def _(pe):
            pe.wait_ge(silu_ready, 1)
            for l in range(2):
                for n in range(6):
                    mm = pe.matmul(ps[:, l, n, :], wmod[:, l, n, :], sc[:, l, :], start=True, stop=True)
            mm.then_inc(mod_ready, 1)

        @block.vector
        def _(dve):
            dve.memset(k.eps[:], EPS)
            dve.memset(k.zero[:], 0.0)
            dve.wait_ge(mod_ready, 1)
            for l in range(2):
                dve.tensor_copy(k.mod[:, l, :, :], ps[:, l, :, :]).then_inc(mod_copied, 1)
            dve.wait_ge(mod_copied, 2)
            for l in range(2):
                for j, n in enumerate((2, 5)):
                    dve.scalar_tensor_tensor(mag[:, l, j, :], k.mod[:, l, n, :], -1.0, k.mod[:, l, n, :],
                                             ALU.mult, ALU.max).then_inc(gate_parts, 1)
                    dve.tensor_scalar(sgn[:, l, j, :], k.mod[:, l, n, :], 0.0, 2.0, ALU.is_ge, ALU.mult)\
                       .then_inc(gate_parts, 1)
                for n in (1, 4):
                    dve.tensor_scalar(k.mod[:, l, n, :], k.mod[:, l, n, :], 1.0, None, ALU.add)
            dve.wait_ge(gate_parts, 8)
            dve.tensor_scalar(mag[:], mag[:], 0.25, None, ALU.max).then_inc(gate_parts, 1)
            dve.wait_ge(gate_parts, 9)
            for l in range(2):
                for j, n in enumerate((2, 5)):
                    dve.scalar_tensor_tensor(k.mod[:, l, n, :], sgn[:, l, j, :], -1.0, mag[:, l, j, :],
                                             ALU.add, ALU.mult)


def norm_pe(pe, k, s, src, first=0):
    for n in range(NCH):
        pe.matmul(k.mean_ps[n % 2][:], k.mean_mat[:], src[:, n * CH:(n + 1) * CH], start=True, stop=True)\
          .then_inc(s.mean, 1)
        if n >= 1:
            norm_pe_var(pe, k, s, n - 1)
        if n + 1 < NCH and n >= 1:
            pe.wait_ge(s.centered, s.base + n)
    norm_pe_var(pe, k, s, NCH - 1)


def norm_pe_var(pe, k, s, n):
    pe.wait_ge(s.squared, s.base + n + 1)
    if n >= 2:
        pe.wait_ge(s.rooted, s.base + n - 1)
    pe.matmul(k.var_ps[n % 2][:], k.mean_mat[:], k.squares[:, n % 2, :], start=True, stop=True).then_inc(s.var, 1)


def norm_act(act, k, s, dst):
    for n in range(NCH + 1):
        if n < NCH:
            act.wait_ge(s.centered, s.base + n + 1)
            if n >= 2:
                act.wait_ge(s.var, s.base + n - 1)
            act.activation(k.squares[:, n % 2, :], dst[:, n * CH:(n + 1) * CH], ACT.Square).then_inc(s.squared, 1)
        if n >= 1:
            act.wait_ge(s.var, s.base + n)
            act.activation(k.dev[:, n - 1, :], k.var_ps[(n - 1) % 2][:], ACT.Sqrt, bias=k.eps[:, 0:1])\
               .then_inc(s.rooted, 1)


def norm_dve(dve, k, s, src, dst):
    for n in range(NCH):
        cols = slice(n * CH, (n + 1) * CH)
        dve.wait_ge(s.mean, s.base + n + 1)
        dve.tensor_tensor(dst[:, cols], src[:, cols], k.mean_ps[n % 2][:], ALU.subtract).then_inc(s.centered, 1)
    for n in range(NCH):
        cols = slice(n * CH, (n + 1) * CH)
        dve.wait_ge(s.rooted, s.base + n + 1)
        dve.reciprocal(k.dev[:, n, :], k.dev[:, n, :]).then_inc(s.inverse, 1)
        dve.wait_ge(s.inverse, s.base + n + 1)
        dve.tensor_tensor(dst[:, cols], dst[:, cols], k.dev[:, n, :], ALU.mult).then_inc(s.normed, 1)


class NormSems:
    def __init__(self, nc, ctx, tag):
        self.base = 0
        self.mean, self.centered, self.squared, self.var, self.rooted, self.inverse, self.normed = (
            ctx.enter_context(nc.semaphore(f"{tag}_{n}"))
            for n in ("mean", "centered", "squared", "var", "rooted", "inverse", "normed"))


def norm_buffers(k, ctx, tag):
    nc = k.nc
    k.mean_ps = [ctx.enter_context(nc.psum_tensor(f"{tag}_mean_ps{i}", [P, CH], F32)) for i in range(2)]
    k.var_ps = [ctx.enter_context(nc.psum_tensor(f"{tag}_var_ps{i}", [P, CH], F32)) for i in range(2)]
    k.squares = ctx.enter_context(nc.sbuf_tensor(f"{tag}_squares", [P, 2, CH], F32))
    k.dev = ctx.enter_context(nc.sbuf_tensor(f"{tag}_deviation", [P, NCH, CH], F32))


def norm_stage(k, tag, layer=None, slot=None):
    nc = k.nc
    with ExitStack() as ctx:
        norm_buffers(k, ctx, tag)
        s = NormSems(nc, ctx, tag)
        block = ctx.enter_context(nc.Block())

        @block.tensor
        def _(pe):
            norm_pe(pe, k, s, k.x)

        @block.scalar
        def _(act):
            norm_act(act, k, s, k.xhat)

        @block.vector
        def _(dve):
            norm_dve(dve, k, s, k.x, k.xhat)
            if layer is not None:
                for b in range(B):
                    if b % 2 == 0:
                        dve.wait_ge(s.normed, b // 2 + 1)
                    dve.tensor_scalar(k.xhat[:, b * L:(b + 1) * L], k.xhat[:, b * L:(b + 1) * L],
                                      k.mod[:, layer, slot + 1, b:b + 1], k.mod[:, layer, slot, b:b + 1],
                                      ALU.mult, ALU.add)


def attention0_stage(k):
    nc = k.nc
    with ExitStack() as ctx:
        def sb(name, shape):
            return ctx.enter_context(nc.sbuf_tensor(name, shape, F32))

        def sem(name):
            return ctx.enter_context(nc.semaphore(name))

        w_qk = sb("w_qk", [P, 2 * PAIRS, 2, P])
        w_v = sb("w_v", [P, H0 * D0])
        w_o = sb("w_o", [P, PAIRS, P])
        rope = sb("rope0", [P, 2, L])
        w1a, w1b = sb("w1a", [P, P]), sb("w1b", [P, P])
        w2 = sb("w2", [P, IG // 2 * H0])
        cols = sb("head_cols", [P, 4])
        soft = sb("softplus", [P, 3, 2])
        h = sb("h_batch", [P, L])
        v = sb("v", [P, 2, H0 * D0])
        qk = sb("qk", [P, 2 * PAIRS, L])
        r1, r2 = sb("rope_cos_part", [P, 2, L]), sb("rope_sin_part", [P, 2, L])
        s0 = sb("scores_keys0", [P, L, H0])
        s1 = sb("scores_keys1", [P, P, H0])
        ta, tb = sb("mlp_in_a", [P, UCOLS]), sb("mlp_in_b", [P, UCOLS])
        hid = sb("hidden", [P, 2, 2 * L])
        probs = sb("logits_probs", [P, UCOLS])
        top = sb("row_max", [P, UNITS])
        wait_cell = sb("wait_cell", [P, UNITS])
        neg = sb("neg_row_max", [P, UNITS])
        tot = sb("row_sum", [P, UNITS])
        inv = sb("inv_row_sum", [P, UNITS])
        add_tab = sb("kerple_bias_mask", [P, SPAN])
        mix_tab = sb("kerple_shifted", [P, SPAN])
        o = qk[:, 0:PAIRS, :]
        p0 = sb("probs_keys0", [P, L, H0])
        p1 = sb("probs_keys1", [P, P, H0])
        dist = p0[:].rearrange("p i h -> p (i h)")[:, 0:3 * SPAN].rearrange("p (a t) -> p a t", a=3)

        def two_banks(name):
            return ctx.enter_context(nc.psum_tensor(name, [P, 2, CH], F32))

        proj_b, pair_b, hid_b = two_banks("proj_b"), [two_banks("pair_b0"), two_banks("pair_b1")], two_banks("hid_b")
        proj_ps = [proj_b[:, i, :] for i in range(2)]
        t_ps = [pair_b[0][:, i, :] for i in range(2)]
        logit_ps = [pair_b[1][:, i, :] for i in range(2)]
        hid_ps = [hid_b[:, i, :] for i in range(2)]
        out_ps = proj_ps[0]
        loaded = sem("a0_loaded")
        soft_step, lns, tabs, mix_laid = sem("soft_step"), sem("lns"), sem("tabs"), sem("mix_laid")
        tab_scaled = sem("tab_scaled")
        h_ready, proj_done, rope_parts, rope_done = sem("h_ready"), sem("proj_done"), sem("rope_parts"), sem("rope_done")
        s_done, s_even, s_odd = sem("s_done"), sem("s_even"), sem("s_odd")
        v_done, v_out = sem("v_done"), sem("v_out")
        t_done, ta_out, tb_out = sem("t_done"), sem("ta_out"), sem("tb_out")
        hid_done, gelu_done = sem("hid_done"), sem("gelu_done")
        logit_done, logit_out, neg_ready = sem("logit_done"), sem("logit_out"), sem("neg_ready")
        exp_done, inv_ready, probs_ready = sem("exp_done"), sem("inv_ready"), sem("probs_ready")
        pt_done, pt_even, pt_odd = sem("pt_done"), sem("pt_even"), sem("pt_odd")
        pv_done, o_even, o_odd = sem("pv_done"), sem("o_even"), sem("o_odd")
        wo_done, x_done = sem("wo_done"), sem("x_done")
        block = ctx.enter_context(nc.Block())

        NQ = 2 * PAIRS
        GROUPS = [(g, jb) for g in range(UNITS // 4) for jb in range(g // (UPB // 4) + 1)]
        NG = len(GROUPS)

        def batches(eng, first, whole, last):
            first()
            whole(0)
            with eng.Fori(1, B - 1) as b:
                whole(b)
            last()

        def weights_at(g, jb):
            i0 = 4 * IG * g
            if jb == 0:
                return p0[:, i0:i0 + 4 * IG, :].rearrange("p i h -> p (i h)")
            return p1[:, i0 - P:i0 - P + 4 * IG, :].rearrange("p i h -> p (i h)")

        @block.sync
        def _(sp):
            load_parts(sp, loaded, [(cols[:], k.d["head_cols"]), (dist, k.d["dist"]), (rope[:], k.d["rope0"]),
                                    (w_qk[:], k.d["w_qk"]), (w1a[:], k.d["w1a"]), (w1b[:], k.d["w1b"]),
                                    (w2[:], k.d["w2"]), (w_v[:], k.d["w_v"]), (w_o[:], k.d["w_o0"])])
            sp.wait_ge(tabs, 2)
            for u in range(UNITS):
                off, J = unit_columns(u)
                c0 = L - IG - IG * u
                sp.dma_start(ta[64:128, off:off + J], mix_tab[64:128, c0:c0 + J]).then_inc(mix_laid, 16)
                sp.dma_start(tb[0:64, off:off + J], mix_tab[0:64, c0:c0 + J]).then_inc(mix_laid, 16)

        @block.gpsimd
        def _(pool):
            def rope_add(b, first=False):
                for n in range(NQ):
                    pool.wait_ge(rope_parts, NQ * b + n + 1)
                    if not first:
                        pool.wait_ge(s_done, PAIRS * b + n // 2 - (PAIRS - 1))
                    pool.tensor_tensor(qk[:, n, :], r1[:, n % 2, :], r2[:, n % 2, :], ALU.add)\
                        .then_inc(rope_done, 1)

            def normalise(b):
                for u in range(UNITS):
                    off, J = unit_columns(u)
                    if u % 4 == 0:
                        pool.wait_ge(inv_ready, UNITS // 4 * b + u // 4 + 1)
                    pool.tensor_tensor(probs[:, off:off + J], probs[:, off:off + J],
                                       inv[:, u:u + 1].broadcast_to([P, J]), ALU.mult).then_inc(probs_ready, 1)

            def first():
                rope_add(0, first=True)

            def whole(b):
                rope_add(b + 1)
                normalise(b)

            batches(pool, first, whole, lambda: normalise(B - 1))

        @block.scalar
        def _(act):
            act.wait_ge(soft_step, 1)
            act.activation(soft[:, 1, :], soft[:, 0, :], ACT.Exp, scale=-1.0).then_inc(lns, 1)
            act.wait_ge(lns, 1)
            act.activation(soft[:, 2, :], soft[:, 1, :], ACT.Ln, bias=1.0).then_inc(lns, 1)
            act.wait_ge(soft_step, 3)
            act.activation(add_tab[:], dist[:, 0, :], ACT.Ln, bias=1.0, scale=soft[:, 0, 1:2]).then_inc(lns, 1)
            act.activation(mix_tab[:], dist[:, 1, :], ACT.Ln, bias=1.0, scale=soft[:, 0, 1:2]).then_inc(lns, 1)

            def scores_out(b, c):
                act.wait_ge(s_done, PAIRS * b + c + 1)
                act.activation(s0[:, :, 2 * c:2 * c + 2], pair_b[c % 2][:, :, 0:L].rearrange("p h i -> p i h"),
                               ACT.Copy, scale=D0 ** -0.5)
                act.activation(s1[:, :, 2 * c:2 * c + 2], pair_b[c % 2][:, :, L:L + P].rearrange("p h i -> p i h"),
                               ACT.Copy, scale=D0 ** -0.5).then_inc(s_even, 1)

            def exps(b, c):
                act.wait_ge(neg_ready, b + 1)
                for u in range(4 * c, 4 * c + 4):
                    off, J = unit_columns(u)
                    act.activation(probs[:, off:off + J], probs[:, off:off + J], ACT.Exp, bias=neg[:, u:u + 1],
                                   accum_out=tot[:, u:u + 1]).then_inc(exp_done, 1)

            def ta_copy(b, u):
                off, J = unit_columns(u)
                act.wait_ge(t_done, UNITS * b + u + 1)
                act.activation(ta[0:64, off:off + J], t_ps[u % 2][0:64, 0:J], ACT.Copy)\
                   .then_inc(ta_out, 1)

            def mlp(b):
                ta_copy(b, 0)
                for u in range(UNITS):
                    _, J = unit_columns(u)
                    if u + 1 < UNITS:
                        ta_copy(b, u + 1)
                    act.wait_ge(hid_done, UNITS * b + u + 1)
                    since(act, logit_done, UNITS * b + max(u - 1, 0))
                    act.activation(hid[:, u % 2, 0:2 * J], hid_ps[u % 2][:, 0:2 * J], ACT.Gelu, bias=cols[:, 3:4])\
                       .then_inc(gelu_done, 1)

            def heads_out(b):
                for n, (g, jb) in enumerate(GROUPS):
                    if n % 2 == 0:
                        continue
                    act.wait_ge(pt_done, NG * b + n + 1)
                    act.activation(weights_at(g, jb), hid_ps[n % 2], ACT.Copy).then_inc(pt_odd, 1)
                for c in range(1, PAIRS, 2):
                    act.wait_ge(pv_done, PAIRS * b + c + 1)
                    act.activation(o[:, c, :], proj_ps[c % 2][:, 0:L], ACT.Copy).then_inc(o_odd, 1)

            def first():
                for c in range(0, PAIRS, 2):
                    scores_out(0, c)

            def whole(b):
                mlp(b)
                for c in range(PAIRS):
                    if c % 2 == 0:
                        scores_out(b + 1, c)
                    exps(b, c)
                heads_out(b)

            def last():
                mlp(B - 1)
                for c in range(PAIRS):
                    exps(B - 1, c)
                heads_out(B - 1)

            batches(act, first, whole, last)

        @block.vector
        def _(dve):
            dve.wait_ge(loaded, 16 * 9)
            dve.scalar_tensor_tensor(soft[:, 0, :], cols[:, 0:2], -1.0, cols[:, 0:2], ALU.mult, ALU.max).then_inc(soft_step, 1)
            dve.wait_ge(lns, 2)
            dve.tensor_scalar(soft[:, 1, :], cols[:, 0:2], 0.0, None, ALU.max).then_inc(soft_step, 1)
            dve.wait_ge(soft_step, 2)
            dve.tensor_tensor(soft[:, 0, :], soft[:, 1, :], soft[:, 2, :], ALU.add).then_inc(soft_step, 1)
            dve.wait_ge(lns, 4)
            dve.wait_ge(soft_step, 3)
            dve.tensor_scalar(add_tab[:], add_tab[:], soft[:, 0, 0:1], -1.0, ALU.mult, ALU.mult).then_inc(tab_scaled, 1)
            dve.tensor_scalar(mix_tab[:], mix_tab[:], soft[:, 0, 0:1], -1.0, ALU.mult, ALU.mult).then_inc(tabs, 1)
            dve.wait_ge(tab_scaled, 1)
            dve.scalar_tensor_tensor(add_tab[:], add_tab[:], cols[:, 2:3], dist[:, 2, :], ALU.add, ALU.add)\
               .then_inc(tabs, 1)

            def scores(b, first=False):
                if not first:
                    since(dve, v_done, 4 * b)
                dve.tensor_scalar(h[:], k.xhat[:, bass.ds(b * L, L)], k.mod[:, 0, 1, bass.ds(b, 1)],
                                  k.mod[:, 0, 0, bass.ds(b, 1)], ALU.mult, ALU.add).then_inc(h_ready, 1)
                for n in range(NQ):
                    dve.wait_ge(proj_done, NQ * b + n + 1)
                    if not first or n >= 2:
                        dve.wait_ge(rope_done, NQ * b + n - 1)
                    ps = proj_ps[n % 2]
                    dve.tensor_tensor(r1[:, n % 2, :], ps[:, 0:L], rope[:, 0, :], ALU.mult)
                    dve.tensor_tensor(r2[:, n % 2, :], ps[:, L:2 * L], rope[:, 1, :], ALU.mult)\
                       .then_inc(rope_parts, 1)
                    if n % 4 == 3 and n >= 7:
                        scores_out(b, n // 2 - 2)
                scores_out(b, PAIRS - 1)

            def scores_out(b, c):
                dve.wait_ge(s_done, PAIRS * b + c + 1)
                dve.tensor_scalar(s0[:, :, 2 * c:2 * c + 2], pair_b[c % 2][:, :, 0:L].rearrange("p h i -> p i h"),
                                  D0 ** -0.5, None, ALU.mult)
                dve.tensor_scalar(s1[:, :, 2 * c:2 * c + 2], pair_b[c % 2][:, :, L:L + P].rearrange("p h i -> p i h"),
                                  D0 ** -0.5, None, ALU.mult).then_inc(s_odd, 1)

            def tb_copy(b, u):
                off, J = unit_columns(u)
                dve.wait_ge(t_done, UNITS * b + u + 1)
                dve.tensor_copy(tb[64:128, off:off + J], t_ps[u % 2][64:128, 0:J])\
                   .then_inc(tb_out, 1)

            def logits(b, u):
                off, J = unit_columns(u)
                c0 = L - IG - IG * u
                dve.wait_ge(logit_done, UNITS * b + u + 1)
                dve.memset(wait_cell[:, u:u + 1], 0.0)
                dve.tensor_tensor_reduce(probs[:, off:off + J], logit_ps[u % 2][:, 0:J], add_tab[:, c0:c0 + J],
                                         1.0, 3.0 * NEG, ALU.add, ALU.max, top[:, u:u + 1]).then_inc(logit_out, 1)

            def mlp(b):
                tb_copy(b, 0)
                for n in range(4):
                    dve.wait_ge(v_done, 4 * b + n + 1)
                    dve.tensor_copy(v[:, n // 2, CH * (n % 2):CH * (n % 2 + 1)], proj_ps[n % 2])\
                       .then_inc(v_out, 1)
                for u in range(UNITS):
                    if u + 1 < UNITS:
                        tb_copy(b, u + 1)
                    if u >= 1:
                        logits(b, u - 1)
                logits(b, UNITS - 1)
                dve.wait_ge(logit_out, UNITS * (b + 1))
                dve.tensor_scalar(neg[:], top[:], -1.0, None, ALU.mult).then_inc(neg_ready, 1)

            def sums(b):
                for g in range(UNITS // 4):
                    dve.wait_ge(exp_done, UNITS * b + 4 * g + 4)
                    dve.reciprocal(inv[:, 4 * g:4 * g + 4], tot[:, 4 * g:4 * g + 4]).then_inc(inv_ready, 1)

            def heads_out(b):
                for n, (g, jb) in enumerate(GROUPS):
                    if n % 2 == 1:
                        continue
                    dve.wait_ge(pt_done, NG * b + n + 1)
                    dve.tensor_copy(weights_at(g, jb), hid_ps[n % 2]).then_inc(pt_even, 1)
                for c in range(0, PAIRS, 2):
                    dve.wait_ge(pv_done, PAIRS * b + c + 1)
                    dve.tensor_copy(o[:, c, :], proj_ps[c % 2][:, 0:L]).then_inc(o_even, 1)
                dve.wait_ge(wo_done, b + 1)
                dve.scalar_tensor_tensor(k.x[:, bass.ds(b * L, L)], out_ps[:, 0:L], k.mod[:, 0, 2, bass.ds(b, 1)],
                                         k.x[:, bass.ds(b * L, L)], ALU.mult, ALU.add).then_inc(x_done, 1)

            def whole(b):
                mlp(b)
                scores(b + 1)
                sums(b)
                heads_out(b)

            def last():
                mlp(B - 1)
                sums(B - 1)
                heads_out(B - 1)

            batches(dve, lambda: scores(0, first=True), whole, last)

        @block.tensor
        def _(pe):
            def project(b, n, first):
                if not first or n >= 2:
                    pe.wait_ge(rope_parts, NQ * b + n - 1)
                for a in range(2):
                    mm = pe.matmul(proj_ps[n % 2][:, a * L:(a + 1) * L], w_qk[:, n, a, :], h[:],
                                   start=True, stop=True)
                mm.then_inc(proj_done, 1)

            def score(b, c, first):
                pe.wait_ge(rope_done, NQ * b + 2 * c + 2)
                if c >= 2:
                    pe.wait_ge((s_even, s_odd)[c % 2], PAIRS // 2 * b + c // 2)
                for hh in range(2):
                    r = slice(D0 * hh, D0 * hh + D0)
                    ps = pair_b[c % 2][:, hh, :]
                    pe.matmul(ps[:, 0:L], qk[r, 2 * c + 1, 0:P], qk[r, 2 * c, :], start=True, stop=True)
                    mm = pe.matmul(ps[:, L:L + P], qk[r, 2 * c + 1, P:L], qk[r, 2 * c, P:L], start=True, stop=True)
                mm.then_inc(s_done, 1)

            def scores(b, first=False):
                pe.wait_ge(h_ready, b + 1)
                if not first:
                    since(pe, v_out, 4 * b)
                    since(pe, logit_out, UNITS * b)
                    since(pe, x_done, b - 1)
                for n in range(4):
                    project(b, n, first)
                for c in range(PAIRS):
                    score(b, c, first)
                    for n in range(2 * c + 4, min(2 * c + 6, NQ)):
                        project(b, n, first)

            def transpose(b, u):
                _, J = unit_columns(u)
                if u >= 2:
                    pe.wait_ge(ta_out, UNITS * b + u - 1)
                    pe.wait_ge(tb_out, UNITS * b + u - 1)
                for jb in range(J // P):
                    mm = pe.transpose(t_ps[u % 2][:, P * jb:P * jb + P], score_block(u, jb), k.ident[:])
                mm.then_inc(t_done, 1)

            def score_block(u, jb):
                i0 = IG * u - (P if jb else 0)
                return (s1 if jb else s0)[:, i0:i0 + IG, :].rearrange("p i h -> p (i h)")

            def hidden(b, u):
                off, J = unit_columns(u)
                pe.wait_ge(ta_out, UNITS * b + u + 1)
                pe.wait_ge(tb_out, UNITS * b + u + 1)
                since(pe, gelu_done, UNITS * b + max(u - 1, 0))
                pe.matmul(hid_ps[u % 2][:, 0:J], w1a[:], ta[:, off:off + J], start=True, stop=True)
                pe.matmul(hid_ps[u % 2][:, J:2 * J], w1b[:], tb[:, off:off + J], start=True, stop=True)\
                  .then_inc(hid_done, 1)

            def logits(b, u):
                _, J = unit_columns(u)
                pe.wait_ge(gelu_done, UNITS * b + u + 1)
                since(pe, logit_out, UNITS * b + max(u - 1, 0))
                ps = logit_ps[u % 2]
                for jb in range(J // P):
                    pe.matmul(ps[:, P * jb:P * jb + P], score_block(u, jb), k.ident[:], start=(jb == 0), stop=False,
                              is_transpose=True, skip_group_check=True)
                for half in range(2):
                    mm = pe.matmul(ps[64 * half:64 * half + 64, 0:J], w2[:], hid[:, u % 2, half * J:half * J + J],
                                   start=False, stop=True, skip_group_check=True)
                mm.then_inc(logit_done, 1)

            def mlp(b):
                pe.wait_ge(s_even, PAIRS // 2 * (b + 1))
                pe.wait_ge(s_odd, PAIRS // 2 * (b + 1))
                transpose(b, 0)
                pe.wait_ge(rope_parts, NQ * (b + 1))
                since(pe, o_even, PAIRS // 2 * b)
                since(pe, o_odd, PAIRS // 2 * b)
                since(pe, x_done, b)
                for n in range(4):
                    if n >= 2:
                        since(pe, v_out, 4 * b + n - 1)
                    pe.matmul(proj_ps[n % 2], h[:, P * (n // 2):P * (n // 2) + P],
                              w_v[:, CH * (n % 2):CH * (n % 2 + 1)], start=True, stop=True).then_inc(v_done, 1)
                since(pe, pt_even, NG // 2 * b)
                since(pe, pt_odd, NG // 2 * b)
                for u in range(UNITS):
                    if u + 1 < UNITS:
                        transpose(b, u + 1)
                    hidden(b, u)
                    if u >= 1:
                        logits(b, u - 1)
                logits(b, UNITS - 1)

            def heads(b, nxt):
                for n, (g, jb) in enumerate(GROUPS):
                    pe.wait_ge(probs_ready, UNITS * b + 4 * g + 4)
                    if n >= 2:
                        pe.wait_ge((pt_even, pt_odd)[n % 2], NG // 2 * b + n // 2)
                    for j in range(4):
                        off, _ = unit_columns(4 * g + j)
                        mm = pe.transpose(hid_ps[n % 2][:, P * j:P * j + P], probs[:, off + P * jb:off + P * jb + P],
                                          k.ident[:])
                    mm.then_inc(pt_done, 1)
                pe.wait_ge(pt_even, NG // 2 * (b + 1))
                pe.wait_ge(pt_odd, NG // 2 * (b + 1))
                pe.wait_ge(rope_parts, NQ * nxt)
                pe.wait_ge(v_out, 4 * (b + 1))
                for c in range(PAIRS):
                    if c >= 2:
                        pe.wait_ge((o_even, o_odd)[c % 2], PAIRS // 2 * b + c // 2)
                    for hh in range(2):
                        hd = 2 * c + hh
                        dims = slice(D0 * hd, D0 * hd + D0)
                        pe.matmul(proj_ps[c % 2][D0 * hh:D0 * hh + D0, 0:L], v[:, 0, dims], p0[:, :, hd],
                                  start=True, stop=False, skip_group_check=True)
                        mm = pe.matmul(proj_ps[c % 2][D0 * hh:D0 * hh + D0, P:L], v[:, 1, dims], p1[:, :, hd],
                                       start=False, stop=True, skip_group_check=True)
                    mm.then_inc(pv_done, 1)
                pe.wait_ge(o_even, PAIRS // 2 * (b + 1))
                pe.wait_ge(o_odd, PAIRS // 2 * (b + 1))
                for c in range(PAIRS):
                    mm = pe.matmul(out_ps[:, 0:L], w_o[:, c, :], o[:, c, :], start=(c == 0), stop=(c == PAIRS - 1))
                mm.then_inc(wo_done, 1)

            def first():
                pe.wait_ge(loaded, 16 * 9)
                scores(0, first=True)
                pe.wait_ge(mix_laid, 16 * 2 * UNITS)

            def whole(b):
                mlp(b)
                scores(b + 1)
                heads(b, b + 2)

            def last():
                mlp(B - 1)
                heads(B - 1, B)

            batches(pe, first, whole, last)


class Chain:

    def __init__(self, eng, sem, done=0):
        self.eng, self.sem, self.done = eng, sem, done

    def __call__(self, instruction):
        self.done = self.done + 1
        instruction.then_inc(self.sem, 1)
        self.eng.wait_ge(self.sem, self.done)


class Router:
    STEPS = 20

    def __init__(self, k, ctx, tag, experts, renormalised):
        nc = k.nc

        def sb(name, shape):
            return ctx.enter_context(nc.sbuf_tensor(f"{tag}_{name}", shape, F32))

        def sem(name):
            return ctx.enter_context(nc.semaphore(f"{tag}_{name}"))

        self.E, self.renormalised = experts, renormalised
        wide, narrow = [P, TB, experts], [P, TB, 1]
        self.probs, self.work, self.first, self.second = (sb(n, wide) for n in ("probs", "work", "first", "second"))
        self.shifted, self.comb, self.order = sb("shifted", wide), sb("comb", wide), sb("order", wide)
        self.m, self.m1, self.m2, self.rank = (sb(n, narrow) for n in ("m", "m1", "m2", "rank"))
        self.sel = sb("sel", [experts, experts, P])
        self.comb_t = sb("comb_t", [experts, T])
        self.logits_done, self.link, self.shift_ready, self.exp_done, self.comb_ready = (
            sem("logits_done"), sem("link"), sem("shift_ready"), sem("exp_done"), sem("comb_ready"))
        self.turned, self.turned_out = sem("turned"), sem("turned_out")

    def route(self, dve, logits, bias, l):
        E = self.E

        def wide(a):
            return a[:].broadcast_to([P, TB, E])

        link = Chain(dve, self.link, self.STEPS * l)
        dve.wait_ge(self.logits_done, l + 1)
        if bias is None:
            link(dve.tensor_copy(self.work[:], logits))
        else:
            link(dve.tensor_tensor(self.work[:], logits, bias, ALU.add))
        link(dve.tensor_reduce(self.m[:], self.work[:], AX.X, ALU.max))
        dve.tensor_tensor(self.shifted[:], self.work[:], wide(self.m), ALU.subtract).then_inc(self.shift_ready, 1)
        dve.wait_ge(self.exp_done, l + 1)
        link(dve.tensor_reduce(self.m1[:], self.probs[:], AX.X, ALU.add))
        link(dve.reciprocal(self.m2[:], self.m1[:]))
        link(dve.tensor_tensor(self.probs[:], self.probs[:], wide(self.m2), ALU.mult))

        def highest(values, top, out):
            link(dve.tensor_reduce(top[:], values, AX.X, ALU.max))
            link(dve.tensor_tensor(out[:], values, wide(top), ALU.is_equal))
            link(dve.tensor_tensor(out[:], out[:], self.order[:], ALU.mult))
            link(dve.tensor_reduce(self.rank[:], out[:], AX.X, ALU.max))
            link(dve.tensor_tensor(out[:], out[:], wide(self.rank), ALU.is_equal))

        highest(self.probs[:], self.m1, self.first)
        link(dve.scalar_tensor_tensor(self.work[:], self.first[:], -2.0, self.probs[:], ALU.mult, ALU.add))
        highest(self.work[:], self.m2, self.second)
        if self.renormalised:
            link(dve.tensor_tensor(self.rank[:], self.m1[:], self.m2[:], ALU.add))
            link(dve.reciprocal(self.m[:], self.rank[:]))
            link(dve.tensor_tensor(self.probs[:], self.probs[:], wide(self.m), ALU.mult))
        link(dve.tensor_tensor(self.first[:], self.first[:], self.second[:], ALU.add))
        dve.tensor_tensor(self.comb[:], self.first[:], self.probs[:], ALU.mult).then_inc(self.comb_ready, 1)
        if self.renormalised:
            assert link.done - self.STEPS * l == self.STEPS if isinstance(l, int) else True

    def exps(self, act, l):
        act.wait_ge(self.shift_ready, l + 1)
        act.activation(self.probs[:], self.shifted[:], ACT.Exp).then_inc(self.exp_done, 1)

    def turn(self, pe, k, banks, l):
        pe.wait_ge(self.comb_ready, l + 1)
        for n in range(NCH):
            if n >= 2:
                pe.wait_ge(self.turned_out, NCH * l + n - 1)
            for j in range(4):
                mm = pe.matmul(banks[n % 2][0:self.E, P * j:P * j + P], self.comb[:, 4 * n + j, :], k.ident[:],
                               start=True, stop=True)
            mm.then_inc(self.turned, 1)

    def turn_out(self, dve, banks, l):
        for n in range(NCH):
            dve.wait_ge(self.turned, NCH * l + n + 1)
            dve.tensor_copy(self.comb_t[:, CH * n:CH * n + CH], banks[n % 2][0:self.E, :]).then_inc(self.turned_out, 1)


def experts0_stage(k):
    nc = k.nc
    with ExitStack() as ctx:
        def sb(name, shape):
            return ctx.enter_context(nc.sbuf_tensor(name, shape, F32))

        def sem(name):
            return ctx.enter_context(nc.semaphore(name))

        def bank(name):
            return ctx.enter_context(nc.psum_tensor(name, [P, CH], F32))

        r = Router(k, ctx, "r0", E0, renormalised=False)
        NF = E0 * FC0
        gate_w = sb("gate_w", [P, E0])
        w1, w3 = sb("e0_w1", [P, E0, FC0 * P]), sb("e0_w3", [P, E0, FC0 * P])
        w2 = sb("e0_w2", [P, E0, FC0, P])
        xe = sb("e0_x", [P, 2, CH])
        act_out = sb("e0_silu", [P, 2, CH])
        g = sb("e0_gated", [P, 2, CH])
        wide_ps = [bank(f"wide{i}") for i in range(2)]
        a1 = [bank(f"a1_{i}") for i in range(2)]
        a3 = [bank(f"a3_{i}") for i in range(2)]
        y_ps, lg = bank("y0"), bank("lg0")
        small, w_in = sem("e0_small"), [sem(f"e0_w_in{e}") for e in range(E0)]
        wide_done, xe_ready, a_done, silu_done, g_done, down_done, y_done, x_done = (
            sem(f"e0_{n}") for n in ("wide", "xe", "a", "silu", "g", "down", "y", "x"))
        block = ctx.enter_context(nc.Block())

        def chunks(eng, chunk):
            chunk(0)
            with eng.Fori(1, NCH) as n:
                chunk(n)

        @block.sync
        def _(sp):
            load_parts(sp, small, [(gate_w[:], k.d["gate_w"]), (r.order[:], k.d["order0"]), (r.sel[:], k.d["sel0"])])
            for e in range(E0):
                load_parts(sp, w_in[e], [(w1[:, e, :], k.d["e0_w1"][:, e, :]), (w3[:, e, :], k.d["e0_w3"][:, e, :]),
                                         (w2[:, e, :, :], k.d["e0_w2"][:, e, :, :])])

        @block.scalar
        def _(act):
            r.exps(act, 0)

            def chunk(n):
                for f in range(NF):
                    act.wait_ge(a_done, NF * n + f + 1)
                    since(act, g_done, NF * n + max(f - 1, 0))
                    act.activation(act_out[:, f % 2, :], a1[f % 2][:], ACT.Silu).then_inc(silu_done, 1)

            chunks(act, chunk)

        @block.vector
        def _(dve):
            dve.wait_ge(small, 48)
            r.route(dve, lg[:, 0:TB * E0].rearrange("p (t e) -> p t e", e=E0), None, 0)
            r.turn_out(dve, wide_ps, 0)

            def scaled(n, e):
                dve.wait_ge(wide_done, E0 * n + e + 1)
                since(dve, a_done, NF * n + FC0 * max(e - 1, 0))
                dve.tensor_tensor(xe[:, e % 2, :], k.xhat[:, bass.ds(n * CH, CH)], wide_ps[e % 2][:], ALU.mult)\
                   .then_inc(xe_ready, 1)

            def chunk(n):
                scaled(n, 0)
                for f in range(NF):
                    if f % FC0 == 1 and f // FC0 + 1 < E0:
                        scaled(n, f // FC0 + 1)
                    dve.wait_ge(silu_done, NF * n + f + 1)
                    since(dve, down_done, NF * n + max(f - 1, 0))
                    dve.tensor_tensor(g[:, f % 2, :], act_out[:, f % 2, :], a3[f % 2][:], ALU.mult)\
                       .then_inc(g_done, 1)
                dve.wait_ge(y_done, n + 1)
                for j in range(2):
                    cols = bass.ds(n * CH + j * L, L)
                    op = dve.scalar_tensor_tensor(k.x[:, cols], y_ps[:, j * L:j * L + L],
                                                  k.mod[:, 0, 5, bass.ds(2 * n + j, 1)], k.x[:, cols],
                                                  ALU.mult, ALU.add)
                op.then_inc(x_done, 1)

            chunks(dve, chunk)

        @block.tensor
        def _(pe):
            pe.wait_ge(small, 48)
            for t in range(TB):
                mm = pe.matmul(lg[:, t * E0:(t + 1) * E0], k.xhat[:, t * P:(t + 1) * P], gate_w[:],
                               start=True, stop=True)
            mm.then_inc(r.logits_done, 1)
            r.turn(pe, k, wide_ps, 0)
            pe.wait_ge(r.turned_out, NCH)

            def widen(n, e):
                pe.matmul(wide_ps[e % 2][:], r.sel[:, e, :], r.comb_t[:, bass.ds(n * CH, CH)],
                          start=True, stop=True).then_inc(wide_done, 1)

            def down(n, f):
                pe.wait_ge(g_done, NF * n + f + 1)
                if f == 0:
                    since(pe, x_done, n)
                mm = pe.matmul(y_ps[:], w2[:, f // FC0, f % FC0, :], g[:, f % 2, :],
                               start=(f == 0), stop=(f == NF - 1))
                mm.then_inc(down_done, 1)
                return mm

            def chunk(n):
                widen(n, 0)
                for f in range(NF):
                    e, fc = f // FC0, f % FC0
                    if fc == 0:
                        pe.wait_ge(xe_ready, E0 * n + e + 1)
                        if isinstance(n, int):
                            pe.wait_ge(w_in[e], 48)
                    since(pe, g_done, NF * n + max(f - 1, 0))
                    pe.matmul(a1[f % 2][:], w1[:, e, fc * P:fc * P + P], xe[:, e % 2, :], start=True, stop=True)
                    pe.matmul(a3[f % 2][:], w3[:, e, fc * P:fc * P + P], xe[:, e % 2, :], start=True, stop=True)\
                      .then_inc(a_done, 1)
                    if fc == 0 and e + 1 < E0:
                        widen(n, e + 1)
                    if f >= 1:
                        down(n, f - 1)
                down(n, NF - 1)
                pe.wait_ge(down_done, NF * n + NF)
                pe.sem_inc(y_done, 1)

            chunks(pe, chunk)


def attention1_stage(k):
    nc = k.nc
    with ExitStack() as ctx:
        def sb(name, shape):
            return ctx.enter_context(nc.sbuf_tensor(name, shape, F32))

        def sem(name):
            return ctx.enter_context(nc.semaphore(name))

        def bank(name):
            return ctx.enter_context(nc.psum_tensor(name, [P, CH], F32))

        ITEMS = [(ib, c, rp) for ib in range(2) for c in range(G1) for rp in range(R1 // 2)]
        NI = len(ITEMS)
        rope = sb("rope1", [P, 2, L])
        w_q, w_k, w_v, w_o = sb("w_q1", [P, R1, P]), sb("w_k1", [P, P]), sb("w_v1", [P, G1 * D1]), sb("w_o1", [P, P])
        mask = sb("mask1", [P, P + L])
        xr, part = sb("x_rotated", [P, T]), sb("rope_part", [P, T])
        v = sb("v1", [P, TB, G1 * D1])
        q, kk = sb("q1", [P, R1, L]), sb("k1", [P, L])
        masked = sb("masked", [P, 2, 2, L])
        low = sb("neg_max1", [P, 2 * H1])
        tot, inv = sb("sum1", [P, 2, H1, 1]), sb("inv1", [P, 2, H1, 1])
        wait_cell = sb("wait_cell1", [P, NI])
        probs, turned = sb("probs1", [P, 2, 2, L]), sb("probs1_t", [P, 2, 2, L])
        o, ot = sb("o1", [P, 2, H1, D1]), sb("o1_t", [P, L])
        s_ps = [bank(f"s1_{i}") for i in range(2)]
        pt_ps = [bank(f"pt1_{i}") for i in range(2)]
        o_ps = [bank(f"o1_{i}") for i in range(2)]
        q_ps = [bank(f"q1_{i}") for i in range(2)]
        loaded, rope_parts, xr_ready, v_done, v_out = (
            sem(f"a1_{n}") for n in ("loaded", "rope_parts", "xr", "v", "v_out"))
        qk_done, qk_ready, s_done, masked_done, exp_done, pt_done, pt_out, pv_done = (
            sem(f"a1_{n}") for n in ("qk", "qk_ready", "s", "masked", "exp", "pt", "pt_out", "pv"))
        inv_ready, o_out, ot_done, ot_out, wo_done, x_done = (
            sem(f"a1_{n}") for n in ("inv", "o_out", "ot", "ot_out", "wo", "x"))
        block = ctx.enter_context(nc.Block())

        def batches(eng, first, body):
            first()
            body(0, False)
            with eng.Fori(1, B - 1) as b:
                body(b, False)
            body(B - 1, True)

        @block.sync
        def _(sp):
            load_parts(sp, loaded, [(rope[:], k.d["rope1"]), (w_v[:], k.d["w_v1"]), (w_q[:], k.d["w_q1"]),
                                    (w_k[:], k.d["w_k1"]), (w_o[:], k.d["w_o1"]), (mask[:], k.d["mask1"])])

        @block.scalar
        def _(act):
            def qk_copy(b):
                act.wait_ge(qk_done, b + 1)
                for i in range(2):
                    act.activation(q[:, 2 * i:2 * i + 2, :], q_ps[i][:].rearrange("p (r i) -> p r i", r=2), ACT.Copy,
                                   scale=D1 ** -0.5)
                act.activation(kk[:], o_ps[0][:, 0:L], ACT.Copy).then_inc(qk_ready, 1)

            def body(b, last):
                for p, (ib, c, rp) in enumerate(ITEMS):
                    J = P * (ib + 1)
                    act.wait_ge(masked_done, NI * b + p + 1)
                    since(act, pt_done, NI * b + max(p - 1, 0))
                    for a in range(2):
                        hd = R1 * c + 2 * rp + a
                        op = act.activation(probs[:, p % 2, a, 0:J], masked[:, p % 2, a, 0:J], ACT.Exp, scale=-1.0,
                                            bias=low[:, H1 * ib + hd:H1 * ib + hd + 1],
                                            accum_out=tot[:, ib, hd, :])
                    op.then_inc(exp_done, 1)
                if not last:
                    qk_copy(b + 1)
                act.wait_ge(ot_done, b + 1)
                act.activation(ot[:], q_ps[0][:, 0:L], ACT.Copy).then_inc(ot_out, 1)

            batches(act, lambda: qk_copy(0), body)

        @block.vector
        def _(dve):
            def first():
                dve.wait_ge(loaded, 96)

                def wide(a, lo, hi):
                    return rope[lo:hi, a:a + 1, :].broadcast_to([hi - lo, B, L])

                def by_batch(a):
                    return a.rearrange("p (b i) -> p b i", b=B)

                dve.tensor_tensor(by_batch(xr[:]), by_batch(k.xhat[:]), wide(0, 0, P), ALU.mult).then_inc(rope_parts, 1)
                half = P // 2
                for lo, to in ((0, half), (half, 0)):
                    dve.tensor_tensor(by_batch(part[to:to + half, :]), by_batch(k.xhat[lo:lo + half, :]),
                                      wide(1, lo, lo + half), ALU.mult).then_inc(rope_parts, 1)
                dve.wait_ge(rope_parts, 3)
                dve.tensor_tensor(xr[:], xr[:], part[:], ALU.add).then_inc(xr_ready, 1)
                dve.wait_ge(v_done, 1)
                dve.tensor_copy(v[:], pt_ps[0][:].rearrange("p (t d) -> p t d", t=TB)).then_inc(v_out, 1)

            def weights_out(b, p):
                ib = ITEMS[p][0]
                J = P * (ib + 1)
                dve.wait_ge(pt_done, NI * b + p + 1)
                since(dve, pv_done, NI * b + max(p - 1, 0))
                dve.tensor_copy(turned[:, p % 2, :, 0:J], pt_ps[p % 2][:].rearrange("p (a j) -> p a j", a=2)[:, :, 0:J])\
                   .then_inc(pt_out, 1)

            def normalise(b, ib):
                dve.wait_ge(exp_done, NI * b + NI // 2 * (ib + 1))
                dve.reciprocal(inv[:, ib, :, :], tot[:, ib, :, :]).then_inc(inv_ready, 1)
                dve.wait_ge(pv_done, NI * b + NI // 2 * (ib + 1))
                dve.wait_ge(inv_ready, 2 * b + ib + 1)
                dve.tensor_tensor(o[:, ib, :, :], o_ps[ib][:, 0:P].rearrange("p (h d) -> p h d", h=H1),
                                  inv[:, ib, :, :].broadcast_to([P, H1, D1]), ALU.mult).then_inc(o_out, 1)

            def body(b, last):
                for p, (ib, c, rp) in enumerate(ITEMS):
                    J = P * (ib + 1)
                    dve.wait_ge(s_done, NI * b + p + 1)
                    if not isinstance(b, int) or NI * b + p >= 2:
                        dve.wait_ge(exp_done, NI * b + p - 1)
                    dve.memset(wait_cell[:, p:p + 1], 0.0)
                    for a in range(2):
                        hd = R1 * c + 2 * rp + a
                        op = dve.tensor_tensor_reduce(masked[:, p % 2, a, 0:J], s_ps[p % 2][:, L * a:L * a + J],
                                                      mask[:, P * (1 - ib):P * (1 - ib) + J], -1.0, -3.0 * NEG,
                                                      ALU.add, ALU.min, low[:, H1 * ib + hd:H1 * ib + hd + 1])
                    op.then_inc(masked_done, 1)
                    if p >= 2:
                        weights_out(b, p - 2)
                    if p == NI // 2 + 4:
                        normalise(b, 0)
                weights_out(b, NI - 2)
                weights_out(b, NI - 1)
                normalise(b, 1)
                dve.wait_ge(wo_done, b + 1)
                cols = bass.ds(b * L, L)
                dve.scalar_tensor_tensor(k.x[:, cols], q_ps[1][:, 0:L], k.mod[:, 1, 2, bass.ds(b, 1)], k.x[:, cols],
                                         ALU.mult, ALU.add).then_inc(x_done, 1)

            batches(dve, first, body)

        @block.tensor
        def _(pe):
            def project(b):
                cols = bass.ds(b * L, L)
                for r in range(R1):
                    pe.matmul(q_ps[r // 2][:, L * (r % 2):L * (r % 2) + L], w_q[:, r, :], xr[:, cols],
                              start=True, stop=True)
                pe.matmul(o_ps[0][:, 0:L], w_k[:], xr[:, cols], start=True, stop=True).then_inc(qk_done, 1)

            def first():
                pe.wait_ge(loaded, 96)
                pe.wait_ge(xr_ready, 1)
                project(0)
                for t in range(TB):
                    mm = pe.matmul(pt_ps[0][:, t * G1 * D1:(t + 1) * G1 * D1], xr[:, t * P:t * P + P], w_v[:],
                                   start=True, stop=True)
                mm.then_inc(v_done, 1)
                pe.wait_ge(v_out, 1)

            def scores(b, p):
                ib, c, rp = ITEMS[p]
                J = P * (ib + 1)
                if p >= 2:
                    pe.wait_ge(masked_done, NI * b + p - 1)
                rows = slice(32 * c, 32 * c + D1)
                for a in range(2):
                    mm = pe.matmul(s_ps[p % 2][:, L * a:L * a + J], q[rows, 2 * rp + a, P * ib:P * ib + P],
                                   kk[rows, 0:J], start=True, stop=True)
                mm.then_inc(s_done, 1)

            def turn(b, p):
                ib = ITEMS[p][0]
                pe.wait_ge(exp_done, NI * b + p + 1)
                since(pe, pt_out, NI * b + max(p - 1, 0))
                for a in range(2):
                    for jb in range(ib + 1):
                        mm = pe.transpose(pt_ps[p % 2][:, L * a + P * jb:L * a + P * jb + P],
                                          probs[:, p % 2, a, P * jb:P * jb + P], k.ident[:])
                mm.then_inc(pt_done, 1)

            def values(b, p):
                ib, c, rp = ITEMS[p]
                pe.wait_ge(pt_out, NI * b + p + 1)
                for a in range(2):
                    hd = R1 * c + 2 * rp + a
                    for jb in range(ib + 1):
                        mm = pe.matmul(o_ps[ib][:, D1 * hd:D1 * hd + D1], turned[:, p % 2, a, P * jb:P * jb + P],
                                       v[:, bass.ds(2 * b + jb, 1), D1 * c:D1 * c + D1].rearrange("p t d -> p (t d)"),
                                       start=(jb == 0), stop=(jb == ib), skip_group_check=True)
                mm.then_inc(pv_done, 1)

            def body(b, last):
                pe.wait_ge(qk_ready, b + 1)
                for p in range(NI):
                    scores(b, p)
                    if p >= 2:
                        turn(b, p - 2)
                    if p >= 3:
                        values(b, p - 3)
                turn(b, NI - 2)
                if not last:
                    since(pe, x_done, b)
                    pe.wait_ge(o_out, 2 * b + 1)
                    project(b + 1)
                values(b, NI - 3)
                turn(b, NI - 1)
                values(b, NI - 2)
                values(b, NI - 1)
                if not last:
                    pe.wait_ge(qk_ready, b + 2)
                for ib in range(2):
                    pe.wait_ge(o_out, 2 * b + ib + 1)
                    mm = pe.transpose(q_ps[0][:, P * ib:P * ib + P], o[:, ib, :, :].rearrange("p h d -> p (h d)"),
                                      k.ident[:])
                mm.then_inc(ot_done, 1)
                pe.wait_ge(ot_out, b + 1)
                pe.matmul(q_ps[1][:, 0:L], w_o[:], ot[:], start=True, stop=True).then_inc(wo_done, 1)

            batches(pe, first, body)


def experts1_stage(k):
    nc = k.nc
    with ExitStack() as ctx:
        def sb(name, shape):
            return ctx.enter_context(nc.sbuf_tensor(name, shape, F32))

        def sem(name):
            return ctx.enter_context(nc.semaphore(name))

        def bank(name):
            return ctx.enter_context(nc.psum_tensor(name, [P, CH], F32))

        ITEMS = [(e, n) for e in range(E1) for n in range(NCH)]
        NI = len(ITEMS)
        NF = NI * FC1
        r = Router(k, ctx, "r1", E1, renormalised=True)
        hs = k.xhat
        xn, acc = sb("x_normed", [P, T]), sb("acc", [P, T])
        pars, par = sb("pars", [P, LY, NPAR]), sb("layer_pars", [P, NPAR])
        g_e, b_e, b2_e, b1_e = par[:, 0:4], par[:, 4:8], par[:, 8:12], par[:, 12:28]
        router_w, router_b = par[:, 28:32], par[:, 32:96].rearrange("p (t e) -> p t e", e=E1)
        w1, w2 = sb("e1_w1", [P, E1, F1]), sb("e1_w2", [P, E1, FC1, P])
        xe, hid, t = sb("e1_x", [P, 2, CH]), sb("e1_hidden", [P, 2, CH]), sb("e1_sum", [P, 2, CH])
        tw = sb("e1_weighted", [P, 2, CH])
        k.squares = hid
        k.dev = sb("deviation1", [P, NCH, CH])
        h_ps, y_ps = [bank(f"h1_{i}") for i in range(2)], [bank(f"y1_{i}") for i in range(2)]
        wide_ps, lg = [bank(f"wide1_{i}") for i in range(2)], bank("lg1")
        k.mean_ps, k.var_ps = h_ps, y_ps
        ns = NormSems(nc, ctx, "n1")
        small, w_in = sem("e1_small"), [sem(f"e1_w_in{e}") for e in range(E1)]
        par_ready, expert_done, wide_done, xe_ready, h_done, gelu_done, down_done = (
            sem(f"e1_{n}") for n in ("par", "expert", "wide", "xe", "h", "gelu", "down"))
        t_done, tw_done, added = (sem(f"e1_{n}") for n in ("t", "tw", "added"))
        block = ctx.enter_context(nc.Block())

        def layers(eng, layer):
            layer(0)
            with eng.Fori(1, LY) as l:
                layer(l)

        @block.sync
        def _(sp):
            load_parts(sp, small, [(pars[:], k.d["pars"]), (r.order[:], k.d["order1"]), (r.sel[:], k.d["sel1"])])

            def layer(l):
                for e in range(E1):
                    since(sp, expert_done, E1 * l + e + 1 - E1)
                    sp.dma_start(w1[:, e, :], k.d["e1_w1"][:, bass.ds(l, 1), e, :].rearrange("p l f -> p (l f)"))\
                      .then_inc(w_in[e], 16)
                    sp.dma_start(w2[:, e, :, :].rearrange("p c n -> p (c n)"),
                                 k.d["e1_w2"][:, bass.ds(l, 1), e, :].rearrange("p l f -> p (l f)")).then_inc(w_in[e], 16)

            layers(sp, layer)

        @block.gpsimd
        def _(pool):
            def layer(l):
                for i, (e, n) in enumerate(ITEMS):
                    cols = slice(n * CH, (n + 1) * CH)
                    pool.wait_ge(tw_done, NI * l + i + 1)
                    since(pool, added, NI * l + max(i + 1 - NCH, 0))
                    if e == 0:
                        pool.tensor_tensor(acc[:, cols], tw[:, i % 2, :], k.zero[:].broadcast_to([P, CH]), ALU.add)\
                            .then_inc(added, 1)
                    else:
                        pool.tensor_tensor((hs if e == E1 - 1 else acc)[:, cols], acc[:, cols], tw[:, i % 2, :],
                                           ALU.add).then_inc(added, 1)

            layers(pool, layer)

        @block.scalar
        def _(act):
            def layer(l):
                ns.base = NCH * l
                since(act, down_done, NF * l)
                norm_act(act, k, ns, xn)
                r.exps(act, l)

                def scaled(i):
                    e, n = ITEMS[i]
                    act.wait_ge(ns.normed, NCH * l + n + 1)
                    since(act, h_done, NF * l + FC1 * max(i - 1, 0))
                    act.activation(xe[:, i % 2, :], xn[:, n * CH:(n + 1) * CH], ACT.Identity, scale=g_e[:, e:e + 1],
                                   bias=b_e[:, e:e + 1]).then_inc(xe_ready, 1)

                act.wait_ge(par_ready, l + 1)
                scaled(0)
                for f in range(NF):
                    i, fc = f // FC1, f % FC1
                    if fc == 1 and i + 1 < NI:
                        scaled(i + 1)
                    act.wait_ge(h_done, NF * l + f + 1)
                    since(act, down_done, NF * l + max(f - 1, 0))
                    c = FC1 * ITEMS[i][0] + fc
                    act.activation(hid[:, f % 2, :], h_ps[f % 2][:], ACT.Gelu, bias=b1_e[:, c:c + 1])\
                       .then_inc(gelu_done, 1)

            layers(act, layer)

        @block.vector
        def _(dve):
            def layer(l):
                ns.base = NCH * l
                if isinstance(l, int):
                    dve.wait_ge(small, 48)
                since(dve, added, NI * l)
                dve.tensor_copy(par[:], pars[:, bass.ds(l, 1), :].rearrange("p l n -> p (l n)")).then_inc(par_ready, 1)
                norm_dve(dve, k, ns, hs, xn)
                dve.wait_ge(par_ready, l + 1)
                r.route(dve, lg[:, 0:TB * E1].rearrange("p (t e) -> p t e", e=E1), router_b, l)
                r.turn_out(dve, wide_ps, l)
                for i, (e, n) in enumerate(ITEMS):
                    dve.wait_ge(down_done, NF * l + FC1 * (i + 1))
                    dve.scalar_tensor_tensor(t[:, i % 2, :], y_ps[i % 2][:], b2_e[:, e:e + 1],
                                             hs[:, n * CH:(n + 1) * CH], ALU.add, ALU.add).then_inc(t_done, 1)
                    dve.wait_ge(t_done, NI * l + i + 1)
                    dve.wait_ge(wide_done, NI * l + i + 1)
                    since(dve, added, NI * l + max(i - 1, 0))
                    dve.tensor_tensor(tw[:, i % 2, :], t[:, i % 2, :], wide_ps[i % 2][:], ALU.mult)\
                       .then_inc(tw_done, 1)

            layers(dve, layer)
            dve.wait_ge(added, NI * LY)
            for b in range(B):
                cols = slice(b * L, b * L + L)
                dve.scalar_tensor_tensor(k.x[:, cols], hs[:, cols], k.mod[:, 1, 5, b:b + 1], k.x[:, cols],
                                         ALU.mult, ALU.add)

        @block.tensor
        def _(pe):
            def layer(l):
                ns.base = NCH * l
                since(pe, added, NI * l)
                pe.wait_ge(par_ready, l + 1)
                for tb in range(TB):
                    mm = pe.matmul(lg[:, tb * E1:(tb + 1) * E1], hs[:, tb * P:(tb + 1) * P], router_w,
                                   start=True, stop=True)
                mm.then_inc(r.logits_done, 1)
                norm_pe(pe, k, ns, hs)
                r.turn(pe, k, wide_ps, l)
                pe.wait_ge(r.turned_out, NCH * (l + 1))

                def widen(i):
                    e, n = ITEMS[i]
                    since(pe, tw_done, NI * l + max(i - 1, 0))
                    pe.matmul(wide_ps[i % 2][:], r.sel[:, e, :], r.comb_t[:, n * CH:(n + 1) * CH],
                              start=True, stop=True).then_inc(wide_done, 1)

                def down(f):
                    i, fc = f // FC1, f % FC1
                    pe.wait_ge(gelu_done, NF * l + f + 1)
                    if fc == 0 and i >= 2:
                        pe.wait_ge(t_done, NI * l + i - 1)
                    mm = pe.matmul(y_ps[i % 2][:], w2[:, ITEMS[i][0], fc, :], hid[:, f % 2, :],
                                   start=(fc == 0), stop=(fc == FC1 - 1))
                    mm.then_inc(down_done, 1)

                widen(0)
                for f in range(NF):
                    i, fc = f // FC1, f % FC1
                    e, n = ITEMS[i]
                    if fc == 2 and i + 1 < NI:
                        widen(i + 1)
                    if fc == 0:
                        if n == 0:
                            pe.wait_ge(w_in[e], 32 * (l + 1))
                        pe.wait_ge(xe_ready, NI * l + i + 1)
                    since(pe, gelu_done, NF * l + max(f - 1, 0))
                    pe.matmul(h_ps[f % 2][:], w1[:, e, fc * P:fc * P + P], xe[:, i % 2, :], start=True, stop=True)\
                      .then_inc(h_done, 1)
                    if f >= 1:
                        down(f - 1)
                        if f % (NCH * FC1) == 0:
                            pe.wait_ge(down_done, NF * l + f)
                            pe.sem_inc(expert_done, 1)
                down(NF - 1)
                pe.wait_ge(down_done, NF * l + NF)
                pe.sem_inc(expert_done, 1)

            layers(pe, layer)


def build(nc, k):
    with ExitStack() as ctx:
        def sb(name, shape):
            return ctx.enter_context(nc.sbuf_tensor(name, shape, F32))

        k.x = sb("x", [P, T])
        k.xhat = sb("xhat", [P, T])
        k.ident = sb("ident", [P, P])
        k.mean_mat = sb("mean_mat", [P, P])
        k.mod = sb("mod", [P, 2, 6, B])
        k.eps, k.zero = sb("eps", [P, 1]), sb("zero", [P, 1])
        setup_stage(k)
        norm_stage(k, "n0a")
        attention0_stage(k)
        norm_stage(k, "n0b", 0, 3)
        experts0_stage(k)
        norm_stage(k, "n1a", 1, 0)
        attention1_stage(k)
        norm_stage(k, "n1b", 1, 3)
        experts1_stage(k)
        store_stage(k, k.x)


def store_stage(k, src):
    with k.nc.semaphore("stored") as stored, k.nc.Block() as block:
        @block.sync
        def _(sp):
            sp.dma_start(k.out, src[:]).then_inc(stored, 16)
            sp.wait_ge(stored, 16)



def constants():
    f = np.float32
    inv = (f(1.0) / np.power(f(10000.0), np.arange(0, D0, 2, dtype=f) / f(D0))).astype(f)
    ang = np.outer(np.arange(L, dtype=f), inv).astype(f)
    cos, sin = np.cos(ang).astype(f).T, np.sin(ang).astype(f).T
    rope0 = np.stack([np.tile(cos, (4, 1)), np.concatenate([-sin, sin, -sin, sin], 0)], 1)
    t = np.arange(SPAN)[None, :] - (L - IG)
    row = np.arange(P)[:, None] // H0
    signed = row - t
    swapped = (row + IG // 2) % IG - t
    dist = np.stack([np.abs(signed), np.abs(swapped), np.where(signed < 0, NEG, 0.0)], 1).astype(f)
    return {"rope0": rope0, **more_constants(), "dist": dist, "ident": np.eye(P, dtype=f), "mean_mat": np.full((P, P), 1.0 / P, f)}


def more_constants():
    f = np.float32
    half = P // 2
    theta = (f(1.0) / np.power(f(10000.0), np.arange(half, dtype=f) / f(half))).astype(f)
    ang = (np.arange(L, dtype=f)[:, None] * theta[None, :]).astype(f)
    cos, sin = np.cos(ang).astype(f).T, np.sin(ang).astype(f).T
    rope1 = np.stack([np.concatenate([cos, cos], 0), np.concatenate([sin, -sin], 0)], 1)
    future = np.arange(P + L)[None, :] - P > np.arange(P)[:, None]
    out = {"rope1": rope1, "mask1": np.where(future, -1.0e9, 0.0).astype(f)}
    for n, e in (("0", E0), ("1", E1)):
        out["order" + n] = np.ascontiguousarray(np.broadcast_to(np.arange(e, 0, -1).astype(f), (P, TB, e)))
        out["sel" + n] = np.ascontiguousarray(np.broadcast_to(np.eye(e, dtype=f)[:, :, None], (e, e, P)))
    return out


EVEN_FIRST = np.concatenate([np.arange(0, P, 2), np.arange(1, P, 2)])


def laid_out(i):
    a = {n: np.asarray(v) for n, v in i.items()}
    f = np.float32
    ch = EVEN_FIRST
    w = a["L0_attn_w_qkv"][ch].reshape(P, 3, H0, D0)
    rotated = np.concatenate([w[..., D0 // 2:], w[..., :D0 // 2]], -1)
    w_qk = np.stack([w[:, 0:2], rotated[:, 0:2]], 0)
    w_qk = w_qk.reshape(2, P, 2, PAIRS, P).transpose(1, 3, 2, 0, 4).reshape(P, 2 * PAIRS, 2, P)
    w1 = a["L0_attn_w1"]
    w1a, w1b, w2 = np.zeros((P, P), f), np.zeros((P, P), f), np.zeros((P, 64), f)
    for q in range(4):
        m = slice(32 * q, 32 * q + 32)
        lo, hi = slice(16 * q, 16 * q + 16), slice(64 + 16 * q, 80 + 16 * q)
        w1a[lo, m], w1a[hi, m] = w1[:H0], w1[H0:]
        w1b[lo, m], w1b[hi, m] = w1[H0:], w1[:H0]
        w2[m, lo] = a["L0_attn_w2"]
    cols = np.stack([np.tile(a["L0_attn_log_p"].reshape(-1), IG), np.tile(a["L0_attn_log_a"].reshape(-1), IG),
                     np.tile(a["L0_attn_b2"], IG), np.tile(a["L0_attn_b1"], 4)], 1)
    w_q = np.zeros((P, R1, P), f)
    w_k = np.zeros((P, P), f)
    for c in range(G1):
        w_k[:, 32 * c:32 * c + D1] = a["L1_attn_W_k"][D1 * c:D1 * c + D1].T
        for r in range(R1):
            hd = R1 * c + r
            w_q[:, r, 32 * c:32 * c + D1] = a["L1_attn_W_q"][D1 * hd:D1 * hd + D1].T
    wide = FC0 * P
    e0_w1, e0_w3, e0_w2 = np.zeros((P, E0, wide), f), np.zeros((P, E0, wide), f), np.zeros((E0, wide, P), f)
    e0_w1[:, :, :F0] = a["L0_ffn_w1"].transpose(1, 0, 2)[ch]
    e0_w3[:, :, :F0] = a["L0_ffn_w3"].transpose(1, 0, 2)[ch]
    e0_w2[:, :F0] = a["L0_ffn_w2"][:, :, ch]
    lg, lb, l2 = (a[n][:, :, ch].transpose(2, 0, 1) for n in ("L1_ffn_ln_g", "L1_ffn_ln_b", "L1_ffn_b2"))
    b1 = a["L1_ffn_b1"].reshape(LY, E1, FC1, P).transpose(3, 0, 1, 2).reshape(P, LY, E1 * FC1)
    rw = a["L1_ffn_router_w"][:, ch].transpose(1, 0, 2)
    rb = np.broadcast_to(np.tile(a["L1_ffn_router_b"], (1, TB))[None], (P, LY, TB * E1))
    d = {
        "x": a["L0_attn_x"].reshape(T, P).T[ch],
        "c": np.stack([a["L0_c"].T, a["L1_c"].T], 1),
        "wmod": np.stack([a["L0_wmod"].reshape(P, 6, P)[:, :, ch], a["L1_wmod"].reshape(P, 6, P)[:, :, ch]], 1),
        "w_qk": w_qk, "w_v": w[:, 2].reshape(P, H0 * D0),
        "w_o0": a["L0_attn_w_o"].reshape(PAIRS, P, P).transpose(1, 0, 2)[:, :, ch],
        "w1a": w1a, "w1b": w1b, "w2": w2, "head_cols": cols,
        "gate_w": a["L0_ffn_gate_w"].T[ch], "e0_w1": e0_w1, "e0_w3": e0_w3,
        "e0_w2": e0_w2.reshape(E0, FC0, P, P).transpose(2, 0, 1, 3),
        "w_q1": w_q, "w_k1": w_k, "w_v1": a["L1_attn_W_v"].T, "w_o1": a["L1_attn_W_o"].T[:, ch],
        "pars": np.concatenate([lg, lb, l2, b1, rw, rb], 2),
        "e1_w1": a["L1_ffn_w1"].transpose(2, 0, 1, 3)[ch],
        "e1_w2": a["L1_ffn_w2"][:, :, :, ch].reshape(LY, E1, FC1, P, P).transpose(3, 0, 1, 2, 4)
                 .reshape(P, LY, E1, FC1 * P),
    }
    d.update(constants())
    return {n: np.ascontiguousarray(v) for n, v in d.items()}


def kernel(**inputs):
    import concourse.bacc as bacc
    from concourse.bass_utils import run_bass_kernel_spmd

    nc = bacc.Bacc("TRN2", target_bir_lowering=False, num_devices=1)
    k = Kit()
    k.nc, k.d = nc, {}
    arrays = {}
    for name, a in laid_out(inputs).items():
        arrays[f"in_{name}"] = a
        k.d[name] = nc.dram_tensor(f"in_{name}", a.shape, mybir.dt.from_np(a.dtype), kind="ExternalInput").ap()
    k.out = nc.dram_tensor("out_x", (P, T), F32, kind="ExternalOutput").ap()
    build(nc, k)
    r = run_bass_kernel_spmd(nc, [arrays], core_ids=[0])
    return np.ascontiguousarray(r.results[0]["out_x"][np.argsort(EVEN_FIRST)].T).reshape(B, L, P)
```

```python
from contextlib import ExitStack

import numpy as np

import concourse.bass as bass
from concourse import mybir

ALU = mybir.AluOpType
ACT = mybir.ActivationFunctionType
AX = mybir.AxisListType
F32 = mybir.dt.float32
F32R = mybir.dt.float32r

P = 128
B, L = 8, 256
T = B * L
CH = 512
NCH = T // CH
TB = T // P
BPC = CH // P
EPS = 1e-5

H0, D0 = 16, 64
PAIRS = H0 // 2
IG = 8
UNITS = L // IG
UPB = P // IG
SPAN = L - IG + L
NEG = -1.0e30

E0, F0 = 8, 352
FC0 = 3

H1, D1, G1 = 16, 8, 4
R1 = H1 // G1

LY, E1, F1 = 4, 4, 512
FC1 = F1 // P
ROUTER = 3 * E1 + E1 * FC1
NPAR = ROUTER + E1 + TB * E1
NADD = (E1 - 2) * NCH


def unit_columns(u):
    if u < UPB:
        return P * u, P
    return P * UPB + L * (u - UPB), L


UCOLS = P * UPB + L * UPB


class Kit:
    pass


def load_parts(nc, done, parts):
    for dst, src in parts:
        nc.dma_start(dst, src).then_inc(done, 16)


def since(eng, sem, value):
    if not isinstance(value, int) or value > 0:
        eng.wait_ge(sem, value)


def setup_stage(k):
    nc = k.nc
    with ExitStack() as ctx:
        def sb(name, shape):
            return ctx.enter_context(nc.sbuf_tensor(name, shape, F32))

        def sem(name):
            return ctx.enter_context(nc.semaphore(name))

        wmod = sb("wmod", [P, 2, 6, P])
        c = sb("c_cols", [P, 2, B])
        sc = sb("silu_c", [P, 2, B])
        mag = sb("gate_magnitude", [P, 2, 2, B])
        sgn = sb("gate_sign", [P, 2, 2, B])
        ps = ctx.enter_context(nc.psum_tensor("mod_ps", [P, 2, 6, B], F32))
        loaded, silu_ready, mod_ready, mod_copied, gate_parts = (
            sem("setup_loaded"), sem("silu_ready"), sem("mod_ready"), sem("mod_copied"), sem("gate_parts"))
        block = ctx.enter_context(nc.Block())

        @block.sync
        def _(sp):
            load_parts(sp, loaded, [(c[:], k.d["c"]), (wmod[:], k.d["wmod"]), (k.ident[:], k.d["ident"]),
                                    (k.mean_mat[:], k.d["mean_mat"]), (k.x[:], k.d["x"])])
            sp.wait_ge(loaded, 80)

        @block.scalar
        def _(act):
            act.wait_ge(loaded, 80)
            act.activation(sc[:], c[:], ACT.Silu).then_inc(silu_ready, 1)

        @block.tensor
        def _(pe):
            pe.wait_ge(silu_ready, 1)
            for l in range(2):
                for n in range(6):
                    mm = pe.matmul(ps[:, l, n, :], wmod[:, l, n, :], sc[:, l, :], start=True, stop=True)
            mm.then_inc(mod_ready, 1)

        @block.vector
        def _(dve):
            dve.wait_ge(loaded, 80)
            dve.tensor_copy(k.ident_r[:], k.ident[:])
            dve.memset(k.neg_half[:], -0.5)
            dve.wait_ge(mod_ready, 1)
            for l in range(2):
                dve.tensor_copy(k.mod[:, l, :, :], ps[:, l, :, :]).then_inc(mod_copied, 1)
            dve.wait_ge(mod_copied, 2)
            for l in range(2):
                for j, n in enumerate((2, 5)):
                    dve.scalar_tensor_tensor(mag[:, l, j, :], k.mod[:, l, n, :], -1.0, k.mod[:, l, n, :],
                                             ALU.mult, ALU.max).then_inc(gate_parts, 1)
                    dve.tensor_scalar(sgn[:, l, j, :], k.mod[:, l, n, :], 0.0, 2.0, ALU.is_ge, ALU.mult)\
                       .then_inc(gate_parts, 1)
                for n in (1, 4):
                    dve.tensor_scalar(k.mod[:, l, n, :], k.mod[:, l, n, :], 1.0, None, ALU.add)
            dve.wait_ge(gate_parts, 8)
            dve.tensor_scalar(mag[:], mag[:], 0.25, None, ALU.max).then_inc(gate_parts, 1)
            dve.wait_ge(gate_parts, 9)
            for l in range(2):
                for j, n in enumerate((2, 5)):
                    dve.scalar_tensor_tensor(k.mod[:, l, n, :], sgn[:, l, j, :], -1.0, mag[:, l, j, :],
                                             ALU.add, ALU.mult)


class Norm:

    SEMAPHORES = ("mean", "centered", "squared", "var", "var_out", "rooted", "high_ready", "split", "wide", "normed")

    def __init__(self, k, ctx, tag, mean_ps, wide_ps, var_ps):
        nc = k.nc

        def sb(name, shape, dtype=F32):
            return ctx.enter_context(nc.sbuf_tensor(f"{tag}_{name}", shape, dtype))

        self.k, self.mean_ps, self.wide_ps, self.var_ps = k, mean_ps, wide_ps, var_ps
        self.squares = sb("squares", [P, 2, CH])
        self.plus_eps, self.rstd = sb("var_plus_eps", [P, NCH, BPC]), sb("rstd", [P, NCH, BPC])
        self.high, self.rest = sb("rstd_high", [P, NCH, BPC], F32R), sb("rstd_rest", [P, NCH, BPC], F32R)
        (self.mean, self.centered, self.squared, self.var, self.var_out, self.rooted, self.high_ready, self.split,
         self.wide, self.normed) = k.norm_semaphores
        self.base = k.chunks_normed
        k.chunks_normed = k.chunks_normed + NCH

    def pe_mean(self, pe, src, n, at):
        at = self.base + at
        since(pe, self.centered, at + 1 - len(self.mean_ps))
        pe.matmul(self.mean_ps[n % len(self.mean_ps)][:], self.k.mean_mat[:], src[:, n * CH:(n + 1) * CH],
                  start=True, stop=True).then_inc(self.mean, 1)

    def pe_var(self, pe, n, at):
        at = self.base + at
        pe.wait_ge(self.squared, at + 1)
        since(pe, self.var_out, at)
        for j in range(BPC):
            mm = pe.matmul(self.var_ps[:, n * BPC + j:n * BPC + j + 1], self.squares[:, n % 2, P * j:P * j + P],
                           self.k.mean_mat[:, 0:1], start=True, stop=True)
        mm.then_inc(self.var, 1)

    def pe_wide(self, pe, n, at):
        at = self.base + at
        pe.wait_ge(self.split, at + 1)
        since(pe, self.normed, at + 1 - len(self.wide_ps))
        widen(pe, self.k, self.wide_ps[n % len(self.wide_ps)], self.high[:, n, :], self.rest[:, n, :])\
            .then_inc(self.wide, 1)

    def act_square(self, act, dst, n, at):
        at = self.base + at
        act.wait_ge(self.centered, at + 1)
        since(act, self.var, at - 1)
        act.activation(self.squares[:, n % 2, :], dst[:, n * CH:(n + 1) * CH], ACT.Square).then_inc(self.squared, 1)

    def dve_center(self, dve, src, dst, n, at):
        at = self.base + at
        cols = slice(n * CH, (n + 1) * CH)
        dve.wait_ge(self.mean, at + 1)
        dve.tensor_tensor(dst[:, cols], src[:, cols], self.mean_ps[n % len(self.mean_ps)][:], ALU.subtract)\
           .then_inc(self.centered, 1)

    def dve_add_eps(self, dve, n, at):
        at = self.base + at
        dve.wait_ge(self.var, at + 1)
        dve.tensor_scalar(self.plus_eps[:, n, :], self.var_ps[:, n * BPC:(n + 1) * BPC], EPS, None, ALU.add)\
           .then_inc(self.var_out, 1)

    def pool_root(self, pool, n, at):
        at = self.base + at
        pool.wait_ge(self.var_out, at + 1)
        pool.tensor_tensor(self.rstd[:, n, :], self.plus_eps[:, n, :], self.k.neg_half[:].broadcast_to([P, BPC]),
                           ALU.pow).then_inc(self.rooted, 1)

    def dve_split(self, dve, n, at):
        at = self.base + at
        dve.wait_ge(self.rooted, at + 1)
        dve.tensor_copy(self.high[:, n, :], self.rstd[:, n, :]).then_inc(self.high_ready, 1)
        dve.wait_ge(self.high_ready, at + 1)
        dve.tensor_tensor(self.rest[:, n, :], self.rstd[:, n, :], self.high[:, n, :].bitcast(F32), ALU.subtract)\
           .then_inc(self.split, 1)

    def dve_scale(self, dve, dst, n, at):
        at = self.base + at
        cols = slice(n * CH, (n + 1) * CH)
        dve.wait_ge(self.wide, at + 1)
        dve.tensor_tensor(dst[:, cols], dst[:, cols], self.wide_ps[n % len(self.wide_ps)][:], ALU.mult)\
           .then_inc(self.normed, 1)


def widen(pe, k, bank, high, rest):
    for j in range(BPC):
        for part, first in ((high, True), (rest, False)):
            mm = pe.matmul(bank[:, P * j:P * j + P], part[:, j:j + 1].broadcast_to([P, P]), k.ident_r[:],
                           start=first, stop=not first, skip_group_check=True)
    return mm


def norm_stage(k, tag, layer=None, slot=None):
    nc = k.nc
    with ExitStack() as ctx:
        def banks(name):
            return [ctx.enter_context(nc.psum_tensor(f"{tag}_{name}{i}", [P, CH], F32)) for i in range(2)]

        var_ps = ctx.enter_context(nc.psum_tensor(f"{tag}_var", [P, CH], F32))
        norm = Norm(k, ctx, tag, banks("mean_ps"), banks("wide_ps"), var_ps)
        block = ctx.enter_context(nc.Block())

        def modulate(dve, n):
            dve.wait_ge(norm.normed, norm.base + n + 1)
            for b in range(2 * n, 2 * n + 2):
                dve.tensor_scalar(k.xhat[:, b * L:(b + 1) * L], k.xhat[:, b * L:(b + 1) * L],
                                  k.mod[:, layer, slot + 1, b:b + 1], k.mod[:, layer, slot, b:b + 1],
                                  ALU.mult, ALU.add)

        @block.tensor
        def _(pe):
            for n in range(NCH + 2):
                if n < NCH:
                    norm.pe_mean(pe, k.x, n, n)
                if 1 <= n <= NCH:
                    norm.pe_var(pe, n - 1, n - 1)
                if n >= 2:
                    norm.pe_wide(pe, n - 2, n - 2)

        @block.scalar
        def _(act):
            for n in range(NCH):
                norm.act_square(act, k.xhat, n, n)

        @block.gpsimd
        def _(pool):
            for n in range(NCH):
                norm.pool_root(pool, n, n)

        @block.vector
        def _(dve):
            for n in range(NCH + 2):
                if n < NCH:
                    norm.dve_center(dve, k.x, k.xhat, n, n)
                if n >= 2:
                    norm.dve_split(dve, n - 2, n - 2)
                if 1 <= n <= NCH:
                    norm.dve_add_eps(dve, n - 1, n - 1)
                if n >= 2:
                    norm.dve_scale(dve, k.xhat, n - 2, n - 2)
                    if layer is not None and n >= 3:
                        modulate(dve, n - 3)
            if layer is not None:
                modulate(dve, NCH - 1)


def attention0_stage(k):
    nc = k.nc
    with ExitStack() as ctx:
        def sb(name, shape):
            return ctx.enter_context(nc.sbuf_tensor(name, shape, F32))

        def sem(name):
            return ctx.enter_context(nc.semaphore(name))

        w_qk = sb("w_qk", [P, 2 * PAIRS, 2, P])
        w_v = sb("w_v", [P, H0 * D0])
        w_o = sb("w_o", [P, PAIRS, P])
        rope = sb("rope0", [P, 2, L])
        w1a, w1b = sb("w1a", [P, P]), sb("w1b", [P, P])
        w2 = sb("w2", [P, IG // 2 * H0])
        cols = sb("head_cols", [P, 4])
        soft = sb("softplus", [P, 3, 2])
        h = sb("h_batch", [P, L])
        v = sb("v", [P, 2, H0 * D0])
        qk = sb("qk", [P, 2 * PAIRS, L])
        r1, r2 = sb("rope_cos_part", [P, 2, L]), sb("rope_sin_part", [P, 2, L])
        s0 = sb("scores_keys0", [P, L, H0])
        s1 = sb("scores_keys1", [P, P, H0])
        ta, tb = sb("mlp_in_a", [P, UCOLS]), sb("mlp_in_b", [P, UCOLS])
        hid = sb("hidden", [P, 2, 2 * L])
        probs = sb("logits_probs", [P, UCOLS])
        top = sb("row_max", [P, UNITS])
        wait_cell = sb("wait_cell", [P, UNITS])
        neg = sb("neg_row_max", [P, UNITS])
        tot = sb("row_sum", [P, UNITS])
        inv = sb("inv_row_sum", [P, UNITS])
        add_tab = sb("kerple_bias_mask", [P, SPAN])
        mix_tab = sb("kerple_shifted", [P, SPAN])
        o = qk[:, 0:PAIRS, :]
        p0 = sb("probs_keys0", [P, L, H0])
        p1 = sb("probs_keys1", [P, P, H0])
        dist = p0[:].rearrange("p i h -> p (i h)")[:, 0:3 * SPAN].rearrange("p (a t) -> p a t", a=3)

        def two_banks(name):
            return ctx.enter_context(nc.psum_tensor(name, [P, 2, CH], F32))

        proj_b, pair_b, hid_b = two_banks("proj_b"), [two_banks("pair_b0"), two_banks("pair_b1")], two_banks("hid_b")
        proj_ps = [proj_b[:, i, :] for i in range(2)]
        t_ps = [pair_b[0][:, i, :] for i in range(2)]
        logit_ps = [pair_b[1][:, i, :] for i in range(2)]
        hid_ps = [hid_b[:, i, :] for i in range(2)]
        out_ps = proj_ps[0]
        loaded = sem("a0_loaded")
        soft_step, lns, tabs, mix_laid = sem("soft_step"), sem("lns"), sem("tabs"), sem("mix_laid")
        tab_scaled = sem("tab_scaled")
        h_ready, proj_done, rope_parts, rope_done = sem("h_ready"), sem("proj_done"), sem("rope_parts"), sem("rope_done")
        s_done, s_even, s_odd = sem("s_done"), sem("s_even"), sem("s_odd")
        v_done, v_out = sem("v_done"), sem("v_out")
        t_done, ta_out, tb_out = sem("t_done"), sem("ta_out"), sem("tb_out")
        hid_done, gelu_done = sem("hid_done"), sem("gelu_done")
        logit_done, logit_out, neg_ready = sem("logit_done"), sem("logit_out"), sem("neg_ready")
        exp_done, inv_ready, probs_ready = sem("exp_done"), sem("inv_ready"), sem("probs_ready")
        pt_done, pt_even, pt_odd = sem("pt_done"), sem("pt_even"), sem("pt_odd")
        pv_done, o_even, o_odd = sem("pv_done"), sem("o_even"), sem("o_odd")
        wo_done, x_done = sem("wo_done"), sem("x_done")
        block = ctx.enter_context(nc.Block())

        NQ = 2 * PAIRS
        GROUPS = [(g, jb) for g in range(UNITS // 4) for jb in range(g // (UPB // 4) + 1)]
        NG = len(GROUPS)

        def batches(eng, first, whole, last):
            first()
            whole(0)
            with eng.Fori(1, B - 1) as b:
                whole(b)
            last()

        def weights_at(g, jb):
            i0 = 4 * IG * g
            if jb == 0:
                return p0[:, i0:i0 + 4 * IG, :].rearrange("p i h -> p (i h)")
            return p1[:, i0 - P:i0 - P + 4 * IG, :].rearrange("p i h -> p (i h)")

        @block.sync
        def _(sp):
            load_parts(sp, loaded, [(cols[:], k.d["head_cols"]), (dist, k.d["dist"]), (rope[:], k.d["rope0"]),
                                    (w_qk[:], k.d["w_qk"]), (w1a[:], k.d["w1a"]), (w1b[:], k.d["w1b"]),
                                    (w2[:], k.d["w2"]), (w_v[:], k.d["w_v"]), (w_o[:], k.d["w_o0"])])
            sp.wait_ge(tabs, 2)
            for u in range(UNITS):
                off, J = unit_columns(u)
                c0 = L - IG - IG * u
                sp.dma_start(ta[64:128, off:off + J], mix_tab[64:128, c0:c0 + J]).then_inc(mix_laid, 16)
                sp.dma_start(tb[0:64, off:off + J], mix_tab[0:64, c0:c0 + J]).then_inc(mix_laid, 16)

        @block.gpsimd
        def _(pool):
            def rope_add(b, first=False):
                for n in range(NQ):
                    pool.wait_ge(rope_parts, NQ * b + n + 1)
                    if not first:
                        pool.wait_ge(s_done, PAIRS * b + n // 2 - (PAIRS - 1))
                    pool.tensor_tensor(qk[:, n, :], r1[:, n % 2, :], r2[:, n % 2, :], ALU.add)\
                        .then_inc(rope_done, 1)

            def normalise(b):
                for u in range(UNITS):
                    off, J = unit_columns(u)
                    if u % 4 == 0:
                        pool.wait_ge(inv_ready, UNITS // 4 * b + u // 4 + 1)
                    pool.tensor_tensor(probs[:, off:off + J], probs[:, off:off + J],
                                       inv[:, u:u + 1].broadcast_to([P, J]), ALU.mult).then_inc(probs_ready, 1)

            def first():
                rope_add(0, first=True)

            def whole(b):
                rope_add(b + 1)
                normalise(b)

            batches(pool, first, whole, lambda: normalise(B - 1))

        @block.scalar
        def _(act):
            act.wait_ge(soft_step, 1)
            act.activation(soft[:, 1, :], soft[:, 0, :], ACT.Exp, scale=-1.0).then_inc(lns, 1)
            act.wait_ge(lns, 1)
            act.activation(soft[:, 2, :], soft[:, 1, :], ACT.Ln, bias=1.0).then_inc(lns, 1)
            act.wait_ge(soft_step, 3)
            act.activation(add_tab[:], dist[:, 0, :], ACT.Ln, bias=1.0, scale=soft[:, 0, 1:2]).then_inc(lns, 1)
            act.activation(mix_tab[:], dist[:, 1, :], ACT.Ln, bias=1.0, scale=soft[:, 0, 1:2]).then_inc(lns, 1)

            def scores_out(b, c):
                act.wait_ge(s_done, PAIRS * b + c + 1)
                act.activation(s0[:, :, 2 * c:2 * c + 2], pair_b[c % 2][:, :, 0:L].rearrange("p h i -> p i h"),
                               ACT.Copy, scale=D0 ** -0.5)
                act.activation(s1[:, :, 2 * c:2 * c + 2], pair_b[c % 2][:, :, L:L + P].rearrange("p h i -> p i h"),
                               ACT.Copy, scale=D0 ** -0.5).then_inc(s_even, 1)

            def exps(b, c):
                act.wait_ge(neg_ready, b + 1)
                for u in range(4 * c, 4 * c + 4):
                    off, J = unit_columns(u)
                    act.activation(probs[:, off:off + J], probs[:, off:off + J], ACT.Exp, bias=neg[:, u:u + 1],
                                   accum_out=tot[:, u:u + 1]).then_inc(exp_done, 1)

            def ta_copy(b, u):
                off, J = unit_columns(u)
                act.wait_ge(t_done, UNITS * b + u + 1)
                act.activation(ta[0:64, off:off + J], t_ps[u % 2][0:64, 0:J], ACT.Copy)\
                   .then_inc(ta_out, 1)

            def mlp(b):
                ta_copy(b, 0)
                for u in range(UNITS):
                    _, J = unit_columns(u)
                    if u + 1 < UNITS:
                        ta_copy(b, u + 1)
                    act.wait_ge(hid_done, UNITS * b + u + 1)
                    since(act, logit_done, UNITS * b + max(u - 1, 0))
                    act.activation(hid[:, u % 2, 0:2 * J], hid_ps[u % 2][:, 0:2 * J], ACT.Gelu, bias=cols[:, 3:4])\
                       .then_inc(gelu_done, 1)

            def heads_out(b):
                for n, (g, jb) in enumerate(GROUPS):
                    if n % 2 == 0:
                        continue
                    act.wait_ge(pt_done, NG * b + n + 1)
                    act.activation(weights_at(g, jb), hid_ps[n % 2], ACT.Copy).then_inc(pt_odd, 1)
                for c in range(1, PAIRS, 2):
                    act.wait_ge(pv_done, PAIRS * b + c + 1)
                    act.activation(o[:, c, :], proj_ps[c % 2][:, 0:L], ACT.Copy).then_inc(o_odd, 1)

            def first():
                for c in range(0, PAIRS, 2):
                    scores_out(0, c)

            def whole(b):
                mlp(b)
                for c in range(PAIRS):
                    if c % 2 == 0:
                        scores_out(b + 1, c)
                    exps(b, c)
                heads_out(b)

            def last():
                mlp(B - 1)
                for c in range(PAIRS):
                    exps(B - 1, c)
                heads_out(B - 1)

            batches(act, first, whole, last)

        @block.vector
        def _(dve):
            dve.wait_ge(loaded, 16 * 9)
            dve.scalar_tensor_tensor(soft[:, 0, :], cols[:, 0:2], -1.0, cols[:, 0:2], ALU.mult, ALU.max).then_inc(soft_step, 1)
            dve.wait_ge(lns, 2)
            dve.tensor_scalar(soft[:, 1, :], cols[:, 0:2], 0.0, None, ALU.max).then_inc(soft_step, 1)
            dve.wait_ge(soft_step, 2)
            dve.tensor_tensor(soft[:, 0, :], soft[:, 1, :], soft[:, 2, :], ALU.add).then_inc(soft_step, 1)
            dve.wait_ge(lns, 4)
            dve.wait_ge(soft_step, 3)
            dve.tensor_scalar(add_tab[:], add_tab[:], soft[:, 0, 0:1], -1.0, ALU.mult, ALU.mult).then_inc(tab_scaled, 1)
            dve.tensor_scalar(mix_tab[:], mix_tab[:], soft[:, 0, 0:1], -1.0, ALU.mult, ALU.mult).then_inc(tabs, 1)
            dve.wait_ge(tab_scaled, 1)
            dve.scalar_tensor_tensor(add_tab[:], add_tab[:], cols[:, 2:3], dist[:, 2, :], ALU.add, ALU.add)\
               .then_inc(tabs, 1)

            def scores(b, first=False):
                if not first:
                    since(dve, v_done, 4 * b)
                dve.tensor_scalar(h[:], k.xhat[:, bass.ds(b * L, L)], k.mod[:, 0, 1, bass.ds(b, 1)],
                                  k.mod[:, 0, 0, bass.ds(b, 1)], ALU.mult, ALU.add).then_inc(h_ready, 1)
                for n in range(NQ):
                    dve.wait_ge(proj_done, NQ * b + n + 1)
                    if not first or n >= 2:
                        dve.wait_ge(rope_done, NQ * b + n - 1)
                    ps = proj_ps[n % 2]
                    dve.tensor_tensor(r1[:, n % 2, :], ps[:, 0:L], rope[:, 0, :], ALU.mult)
                    dve.tensor_tensor(r2[:, n % 2, :], ps[:, L:2 * L], rope[:, 1, :], ALU.mult)\
                       .then_inc(rope_parts, 1)
                    if n % 4 == 3 and n >= 7:
                        scores_out(b, n // 2 - 2)
                scores_out(b, PAIRS - 1)

            def scores_out(b, c):
                dve.wait_ge(s_done, PAIRS * b + c + 1)
                dve.tensor_scalar(s0[:, :, 2 * c:2 * c + 2], pair_b[c % 2][:, :, 0:L].rearrange("p h i -> p i h"),
                                  D0 ** -0.5, None, ALU.mult)
                dve.tensor_scalar(s1[:, :, 2 * c:2 * c + 2], pair_b[c % 2][:, :, L:L + P].rearrange("p h i -> p i h"),
                                  D0 ** -0.5, None, ALU.mult).then_inc(s_odd, 1)

            def tb_copy(b, u):
                off, J = unit_columns(u)
                dve.wait_ge(t_done, UNITS * b + u + 1)
                dve.tensor_copy(tb[64:128, off:off + J], t_ps[u % 2][64:128, 0:J])\
                   .then_inc(tb_out, 1)

            def logits(b, u):
                off, J = unit_columns(u)
                c0 = L - IG - IG * u
                dve.wait_ge(logit_done, UNITS * b + u + 1)
                dve.memset(wait_cell[:, u:u + 1], 0.0)
                dve.tensor_tensor_reduce(probs[:, off:off + J], logit_ps[u % 2][:, 0:J], add_tab[:, c0:c0 + J],
                                         1.0, 3.0 * NEG, ALU.add, ALU.max, top[:, u:u + 1]).then_inc(logit_out, 1)

            def mlp(b):
                tb_copy(b, 0)
                for n in range(4):
                    dve.wait_ge(v_done, 4 * b + n + 1)
                    dve.tensor_copy(v[:, n // 2, CH * (n % 2):CH * (n % 2 + 1)], proj_ps[n % 2])\
                       .then_inc(v_out, 1)
                for u in range(UNITS):
                    if u + 1 < UNITS:
                        tb_copy(b, u + 1)
                    if u >= 1:
                        logits(b, u - 1)
                logits(b, UNITS - 1)
                dve.wait_ge(logit_out, UNITS * (b + 1))
                dve.tensor_scalar(neg[:], top[:], -1.0, None, ALU.mult).then_inc(neg_ready, 1)

            def sums(b):
                for g in range(UNITS // 4):
                    dve.wait_ge(exp_done, UNITS * b + 4 * g + 4)
                    dve.reciprocal(inv[:, 4 * g:4 * g + 4], tot[:, 4 * g:4 * g + 4]).then_inc(inv_ready, 1)

            def heads_out(b):
                for n, (g, jb) in enumerate(GROUPS):
                    if n % 2 == 1:
                        continue
                    dve.wait_ge(pt_done, NG * b + n + 1)
                    dve.tensor_copy(weights_at(g, jb), hid_ps[n % 2]).then_inc(pt_even, 1)
                for c in range(0, PAIRS, 2):
                    dve.wait_ge(pv_done, PAIRS * b + c + 1)
                    dve.tensor_copy(o[:, c, :], proj_ps[c % 2][:, 0:L]).then_inc(o_even, 1)
                dve.wait_ge(wo_done, b + 1)
                dve.scalar_tensor_tensor(k.x[:, bass.ds(b * L, L)], out_ps[:, 0:L], k.mod[:, 0, 2, bass.ds(b, 1)],
                                         k.x[:, bass.ds(b * L, L)], ALU.mult, ALU.add).then_inc(x_done, 1)

            def whole(b):
                mlp(b)
                scores(b + 1)
                sums(b)
                heads_out(b)

            def last():
                mlp(B - 1)
                sums(B - 1)
                heads_out(B - 1)

            batches(dve, lambda: scores(0, first=True), whole, last)

        @block.tensor
        def _(pe):
            def project(b, n, first):
                if not first or n >= 2:
                    pe.wait_ge(rope_parts, NQ * b + n - 1)
                for a in range(2):
                    mm = pe.matmul(proj_ps[n % 2][:, a * L:(a + 1) * L], w_qk[:, n, a, :], h[:],
                                   start=True, stop=True)
                mm.then_inc(proj_done, 1)

            def score(b, c, first):
                pe.wait_ge(rope_done, NQ * b + 2 * c + 2)
                if c >= 2:
                    pe.wait_ge((s_even, s_odd)[c % 2], PAIRS // 2 * b + c // 2)
                for hh in range(2):
                    r = slice(D0 * hh, D0 * hh + D0)
                    ps = pair_b[c % 2][:, hh, :]
                    pe.matmul(ps[:, 0:L], qk[r, 2 * c + 1, 0:P], qk[r, 2 * c, :], start=True, stop=True)
                    mm = pe.matmul(ps[:, L:L + P], qk[r, 2 * c + 1, P:L], qk[r, 2 * c, P:L], start=True, stop=True)
                mm.then_inc(s_done, 1)

            def scores(b, first=False):
                pe.wait_ge(h_ready, b + 1)
                if not first:
                    since(pe, v_out, 4 * b)
                    since(pe, logit_out, UNITS * b)
                    since(pe, x_done, b - 1)
                for n in range(4):
                    project(b, n, first)
                for c in range(PAIRS):
                    score(b, c, first)
                    for n in range(2 * c + 4, min(2 * c + 6, NQ)):
                        project(b, n, first)

            def transpose(b, u):
                _, J = unit_columns(u)
                if u >= 2:
                    pe.wait_ge(ta_out, UNITS * b + u - 1)
                    pe.wait_ge(tb_out, UNITS * b + u - 1)
                for jb in range(J // P):
                    mm = pe.transpose(t_ps[u % 2][:, P * jb:P * jb + P], score_block(u, jb), k.ident[:])
                mm.then_inc(t_done, 1)

            def score_block(u, jb):
                i0 = IG * u - (P if jb else 0)
                return (s1 if jb else s0)[:, i0:i0 + IG, :].rearrange("p i h -> p (i h)")

            def hidden(b, u):
                off, J = unit_columns(u)
                pe.wait_ge(ta_out, UNITS * b + u + 1)
                pe.wait_ge(tb_out, UNITS * b + u + 1)
                since(pe, gelu_done, UNITS * b + max(u - 1, 0))
                pe.matmul(hid_ps[u % 2][:, 0:J], w1a[:], ta[:, off:off + J], start=True, stop=True)
                pe.matmul(hid_ps[u % 2][:, J:2 * J], w1b[:], tb[:, off:off + J], start=True, stop=True)\
                  .then_inc(hid_done, 1)

            def logits(b, u):
                _, J = unit_columns(u)
                pe.wait_ge(gelu_done, UNITS * b + u + 1)
                since(pe, logit_out, UNITS * b + max(u - 1, 0))
                ps = logit_ps[u % 2]
                for jb in range(J // P):
                    pe.matmul(ps[:, P * jb:P * jb + P], score_block(u, jb), k.ident[:], start=(jb == 0), stop=False,
                              is_transpose=True, skip_group_check=True)
                for half in range(2):
                    mm = pe.matmul(ps[64 * half:64 * half + 64, 0:J], w2[:], hid[:, u % 2, half * J:half * J + J],
                                   start=False, stop=True, skip_group_check=True)
                mm.then_inc(logit_done, 1)

            def mlp(b):
                pe.wait_ge(s_even, PAIRS // 2 * (b + 1))
                pe.wait_ge(s_odd, PAIRS // 2 * (b + 1))
                transpose(b, 0)
                pe.wait_ge(rope_parts, NQ * (b + 1))
                since(pe, o_even, PAIRS // 2 * b)
                since(pe, o_odd, PAIRS // 2 * b)
                since(pe, x_done, b)
                for n in range(4):
                    if n >= 2:
                        since(pe, v_out, 4 * b + n - 1)
                    pe.matmul(proj_ps[n % 2], h[:, P * (n // 2):P * (n // 2) + P],
                              w_v[:, CH * (n % 2):CH * (n % 2 + 1)], start=True, stop=True).then_inc(v_done, 1)
                since(pe, pt_even, NG // 2 * b)
                since(pe, pt_odd, NG // 2 * b)
                for u in range(UNITS):
                    if u + 1 < UNITS:
                        transpose(b, u + 1)
                    hidden(b, u)
                    if u >= 1:
                        logits(b, u - 1)
                logits(b, UNITS - 1)

            def heads(b, nxt):
                for n, (g, jb) in enumerate(GROUPS):
                    pe.wait_ge(probs_ready, UNITS * b + 4 * g + 4)
                    if n >= 2:
                        pe.wait_ge((pt_even, pt_odd)[n % 2], NG // 2 * b + n // 2)
                    for j in range(4):
                        off, _ = unit_columns(4 * g + j)
                        mm = pe.transpose(hid_ps[n % 2][:, P * j:P * j + P], probs[:, off + P * jb:off + P * jb + P],
                                          k.ident[:])
                    mm.then_inc(pt_done, 1)
                pe.wait_ge(pt_even, NG // 2 * (b + 1))
                pe.wait_ge(pt_odd, NG // 2 * (b + 1))
                pe.wait_ge(rope_parts, NQ * nxt)
                pe.wait_ge(v_out, 4 * (b + 1))
                for c in range(PAIRS):
                    if c >= 2:
                        pe.wait_ge((o_even, o_odd)[c % 2], PAIRS // 2 * b + c // 2)
                    for hh in range(2):
                        hd = 2 * c + hh
                        dims = slice(D0 * hd, D0 * hd + D0)
                        pe.matmul(proj_ps[c % 2][D0 * hh:D0 * hh + D0, 0:L], v[:, 0, dims], p0[:, :, hd],
                                  start=True, stop=False, skip_group_check=True)
                        mm = pe.matmul(proj_ps[c % 2][D0 * hh:D0 * hh + D0, P:L], v[:, 1, dims], p1[:, :, hd],
                                       start=False, stop=True, skip_group_check=True)
                    mm.then_inc(pv_done, 1)
                pe.wait_ge(o_even, PAIRS // 2 * (b + 1))
                pe.wait_ge(o_odd, PAIRS // 2 * (b + 1))
                for c in range(PAIRS):
                    mm = pe.matmul(out_ps[:, 0:L], w_o[:, c, :], o[:, c, :], start=(c == 0), stop=(c == PAIRS - 1))
                mm.then_inc(wo_done, 1)

            def first():
                pe.wait_ge(loaded, 16 * 9)
                scores(0, first=True)
                pe.wait_ge(mix_laid, 16 * 2 * UNITS)

            def whole(b):
                mlp(b)
                scores(b + 1)
                heads(b, b + 2)

            def last():
                mlp(B - 1)
                heads(B - 1, B)

            batches(pe, first, whole, last)


class Chain:

    def __init__(self, eng, sem, done=0):
        self.eng, self.sem, self.done = eng, sem, done

    def __call__(self, instruction):
        self.done = self.done + 1
        instruction.then_inc(self.sem, 1)
        self.eng.wait_ge(self.sem, self.done)


class Router:
    PARTS = 5
    STARTS = (0, 2, 5, 10, 16)
    STEPS = 21

    def __init__(self, k, ctx, tag, experts, renormalised):
        nc = k.nc

        def sb(name, shape, dtype=F32):
            return ctx.enter_context(nc.sbuf_tensor(f"{tag}_{name}", shape, dtype))

        def sem(name):
            return ctx.enter_context(nc.semaphore(f"{tag}_{name}"))

        self.E, self.renormalised = experts, renormalised
        wide, narrow = [P, TB, experts], [P, TB, 1]
        self.probs, self.work, self.first, self.second = (sb(n, wide) for n in ("probs", "work", "first", "second"))
        self.shifted, self.comb, self.order = sb("shifted", wide), sb("comb", wide), sb("order", wide)
        self.high, self.rest = sb("comb_high", wide, F32R), sb("comb_rest", wide, F32R)
        self.m, self.m1, self.m2, self.rank = (sb(n, narrow) for n in ("m", "m1", "m2", "rank"))
        self.logits_done, self.link, self.shift_ready, self.exp_done, self.comb_ready = (
            sem("logits_done"), sem("link"), sem("shift_ready"), sem("exp_done"), sem("comb_ready"))

    def route(self, dve, part, logits, bias, l):
        def wide(a):
            return a[:].broadcast_to([P, TB, self.E])

        link = Chain(dve, self.link, self.STEPS * l + self.STARTS[part])
        if part == 0:
            dve.wait_ge(self.logits_done, l + 1)
            if bias is None:
                link(dve.tensor_copy(self.work[:], logits))
            else:
                link(dve.tensor_tensor(self.work[:], logits, bias, ALU.add))
            link(dve.tensor_reduce(self.m[:], self.work[:], AX.X, ALU.max))
            dve.tensor_tensor(self.shifted[:], self.work[:], wide(self.m), ALU.subtract).then_inc(self.shift_ready, 1)
        elif part == 1:
            dve.wait_ge(self.exp_done, l + 1)
            link(dve.tensor_reduce(self.m1[:], self.probs[:], AX.X, ALU.add))
            link(dve.reciprocal(self.m2[:], self.m1[:]))
            link(dve.tensor_tensor(self.probs[:], self.probs[:], wide(self.m2), ALU.mult))
        elif part == 2:
            self.highest(dve, link, self.probs[:], self.m1, self.first)
        elif part == 3:
            link(dve.scalar_tensor_tensor(self.work[:], self.first[:], -2.0, self.probs[:], ALU.mult, ALU.add))
            self.highest(dve, link, self.work[:], self.m2, self.second)
        else:
            link(dve.tensor_tensor(self.first[:], self.first[:], self.second[:], ALU.add))
            if self.renormalised:
                link(dve.tensor_tensor(self.rank[:], self.m1[:], self.m2[:], ALU.add))
                link(dve.reciprocal(self.m[:], self.rank[:]))
                link(dve.tensor_tensor(self.probs[:], self.probs[:], wide(self.m), ALU.mult))
            dve.tensor_tensor(self.high[:], self.first[:], self.probs[:], ALU.mult)
            link(dve.tensor_tensor(self.comb[:], self.first[:], self.probs[:], ALU.mult))
            dve.tensor_tensor(self.rest[:], self.comb[:], self.high[:].bitcast(F32), ALU.subtract)\
               .then_inc(self.comb_ready, 1)

    def highest(self, dve, link, values, top, out):
        link(dve.tensor_reduce(top[:], values, AX.X, ALU.max))
        link(dve.tensor_tensor(out[:], values, top[:].broadcast_to([P, TB, self.E]), ALU.is_equal))
        link(dve.tensor_tensor(out[:], out[:], self.order[:], ALU.mult))
        link(dve.tensor_reduce(self.rank[:], out[:], AX.X, ALU.max))
        link(dve.tensor_tensor(out[:], out[:], self.rank[:].broadcast_to([P, TB, self.E]), ALU.is_equal))

    def exps(self, act, l):
        act.wait_ge(self.shift_ready, l + 1)
        act.activation(self.probs[:], self.shifted[:], ACT.Exp).then_inc(self.exp_done, 1)


def products(pe, out, weights, values, start, stop):
    for n, (a, b) in enumerate(((0, 0), (0, 1), (1, 0))):
        mm = pe.matmul(out, weights[a], values[b], start=start and n == 0, stop=stop and n == 2)
    return mm


def experts0_stage(k):
    nc = k.nc
    with ExitStack() as ctx:
        def sb(name, shape, dtype=F32):
            return ctx.enter_context(nc.sbuf_tensor(name, shape, dtype))

        def sem(name):
            return ctx.enter_context(nc.semaphore(name))

        def bank(name):
            return ctx.enter_context(nc.psum_tensor(name, [P, CH], F32))

        r = Router(k, ctx, "r0", E0, renormalised=False)
        NF = E0 * FC0
        FW = FC0 * P
        WE = 3 * FW
        SLOTS = 4
        DOWN = 2
        gate_w = sb("gate_w", [P, E0])
        raw = sb("e0_w_raw", [P, 2, WE])
        w_high, w_rest = sb("e0_w_high", [P, E0, WE], F32R), sb("e0_w_rest", [P, E0, WE], F32R)
        comb_high, comb_rest = sb("e0_comb_high", [P, E0, BPC], F32R), sb("e0_comb_rest", [P, E0, BPC], F32R)
        xe = sb("e0_x", [P, 2, CH])
        xe_high, xe_rest = sb("e0_x_high", [P, 2, CH], F32R), sb("e0_x_rest", [P, 2, CH], F32R)
        silu = sb("e0_silu", [P, 2, CH])
        g = sb("e0_gated", [P, 2, CH])
        g_high, g_rest = sb("e0_gated_high", [P, SLOTS, CH], F32R), sb("e0_gated_rest", [P, SLOTS, CH], F32R)
        wide_ps = [bank(f"wide{i}") for i in range(2)]
        a1 = [bank(f"a1_{i}") for i in range(2)]
        a3 = [bank(f"a3_{i}") for i in range(2)]
        y_ps, lg = bank("y0"), bank("lg0")
        small, w_in = sem("e0_small"), sem("e0_w_in")
        high_done, rest_done, comb_laid, wide_done, xe_ready, xe_high_ready, xe_rest_ready = (
            sem(f"e0_{n}") for n in ("w_high", "w_rest", "comb_laid", "wide", "xe", "xe_high", "xe_rest"))
        up_done, silu_done, g_done, g_high_done, g_ready, down_done, x_done = (
            sem(f"e0_{n}") for n in ("up", "silu", "g", "g_high", "g_rest", "down", "x"))
        block = ctx.enter_context(nc.Block())

        def chunks(eng, first, chunk, end):
            first()
            chunk(0)
            with eng.Fori(1, NCH - 1) as n:
                chunk(n)
            chunk(NCH - 1)
            end()

        def last(n):
            return isinstance(n, int) and n == NCH - 1

        def starts(n):
            return isinstance(n, int) and n == 0

        def ahead(step, n, e):
            if e + 1 < E0:
                step(n, e + 1)
            elif not last(n):
                step(n + 1, 0)

        def behind(step, n, f, lag):
            if f >= lag:
                step(n, f - lag)
            elif not starts(n):
                step(n - 1, f - lag + NF)

        @block.sync
        def _(sp):
            load_parts(sp, small, [(gate_w[:], k.d["gate_w"]), (r.order[:], k.d["order0"])])
            for e in range(E0):
                if e >= 2:
                    sp.wait_ge(rest_done, e - 1)
                    sp.wait_ge(w_in, 48 * (e - 1))
                load_parts(sp, w_in, [(raw[:, e % 2, 0:FW], k.d["e0_w1"][:, e, :]),
                                      (raw[:, e % 2, FW:2 * FW], k.d["e0_w3"][:, e, :]),
                                      (raw[:, e % 2, 2 * FW:WE].rearrange("p (c n) -> p c n", c=FC0),
                                       k.d["e0_w2"][:, e, :, :])])
                sp.wait_ge(w_in, 48 * (e + 1))

        @block.gpsimd
        def _(pool):
            def split_rest(e):
                pool.wait_ge(high_done, e + 1)
                pool.tensor_tensor(w_rest[:, e, :], raw[:, e % 2, :], w_high[:, e, :].bitcast(F32), ALU.subtract)\
                    .then_inc(rest_done, 1)

            def x_rest(n, e):
                pool.wait_ge(xe_high_ready, E0 * n + e + 1)
                pool.tensor_tensor(xe_rest[:, e % 2, :], xe[:, e % 2, :], xe_high[:, e % 2, :].bitcast(F32),
                                   ALU.subtract).then_inc(xe_rest_ready, 1)

            def first():
                split_rest(0)
                x_rest(0, 0)

            def chunk(n):
                for e in range(E0):
                    if starts(n) and e + 1 < E0:
                        split_rest(e + 1)
                    ahead(x_rest, n, e)

            chunks(pool, first, chunk, lambda: None)

        @block.scalar
        def _(act):
            def x_high(n, e):
                act.wait_ge(xe_ready, E0 * n + e + 1)
                since(act, up_done, NF * n + FC0 * (e - 1))
                act.activation(xe_high[:, e % 2, :], xe[:, e % 2, :], ACT.Copy).then_inc(xe_high_ready, 1)

            def gated_high(n, f):
                act.wait_ge(g_done, NF * n + f + 1)
                since(act, down_done, NF * n + f + 1 - SLOTS)
                act.activation(g_high[:, f % SLOTS, :], g[:, f % 2, :], ACT.Copy).then_inc(g_high_done, 1)

            def first():
                r.exps(act, 0)
                x_high(0, 0)

            def chunk(n):
                for f in range(NF):
                    if f % FC0 == 0:
                        ahead(x_high, n, f // FC0)
                    act.wait_ge(up_done, NF * n + f + 1)
                    since(act, g_done, NF * n + f - 1)
                    act.activation(silu[:, f % 2, :], a1[f % 2][:], ACT.Silu).then_inc(silu_done, 1)
                    gated_high(n, f)

            chunks(act, first, chunk, lambda: None)

        @block.vector
        def _(dve):
            def split_high(e):
                dve.wait_ge(w_in, 48 * (e + 1))
                dve.tensor_copy(w_high[:, e, :], raw[:, e % 2, :]).then_inc(high_done, 1)

            def lay_comb(n):
                since(dve, wide_done, E0 * n)
                for dst, src in ((comb_high, r.high), (comb_rest, r.rest)):
                    op = dve.tensor_copy(dst[:], src[:, bass.ds(BPC * n, BPC), :].rearrange("p t e -> p e t"))
                op.then_inc(comb_laid, 1)

            def scale_x(n, e):
                dve.wait_ge(wide_done, E0 * n + e + 1)
                since(dve, xe_rest_ready, E0 * n + e - 1)
                dve.tensor_tensor(xe[:, e % 2, :], k.xhat[:, bass.ds(n * CH, CH)], wide_ps[e % 2][:], ALU.mult)\
                   .then_inc(xe_ready, 1)

            def gated_rest(n, f):
                dve.wait_ge(g_high_done, NF * n + f + 1)
                dve.tensor_tensor(g_rest[:, f % SLOTS, :], g[:, f % 2, :], g_high[:, f % SLOTS, :].bitcast(F32),
                                  ALU.subtract).then_inc(g_ready, 1)

            def add_x(n):
                dve.wait_ge(down_done, NF * (n + 1))
                for j in range(2):
                    cols = bass.ds(n * CH + j * L, L)
                    op = dve.scalar_tensor_tensor(k.x[:, cols], y_ps[:, j * L:j * L + L],
                                                  k.mod[:, 0, 5, bass.ds(2 * n + j, 1)], k.x[:, cols],
                                                  ALU.mult, ALU.add)
                op.then_inc(x_done, 1)

            def first():
                split_high(0)
                dve.wait_ge(small, 32)
                for part in range(r.PARTS):
                    r.route(dve, part, lg[:, 0:TB * E0].rearrange("p (t e) -> p t e", e=E0), None, 0)
                dve.wait_ge(r.comb_ready, 1)
                lay_comb(0)
                scale_x(0, 0)

            def chunk(n):
                for f in range(NF):
                    e, fc = f // FC0, f % FC0
                    if fc == 0 and starts(n) and e + 1 < E0:
                        split_high(e + 1)
                    if fc == 0:
                        ahead(scale_x, n, e)
                    behind(gated_rest, n, f, 1)
                    dve.wait_ge(silu_done, NF * n + f + 1)
                    dve.tensor_tensor(g[:, f % 2, :], silu[:, f % 2, :], a3[f % 2][:], ALU.mult).then_inc(g_done, 1)
                    if f == NF - FC0 - 1 and not last(n):
                        lay_comb(n + 1)
                    if f == DOWN and not starts(n):
                        add_x(n - 1)

            def end():
                gated_rest(NCH - 1, NF - 1)
                add_x(NCH - 1)

            chunks(dve, first, chunk, end)

        @block.tensor
        def _(pe):
            def wide(n, e):
                if e == 0:
                    pe.wait_ge(comb_laid, n + 1)
                since(pe, xe_ready, E0 * n + e - 1)
                widen(pe, k, wide_ps[e % 2], comb_high[:, e, :], comb_rest[:, e, :]).then_inc(wide_done, 1)

            def first():
                pe.wait_ge(small, 32)
                for t in range(TB):
                    mm = pe.matmul(lg[:, t * E0:(t + 1) * E0], k.xhat[:, t * P:(t + 1) * P], gate_w[:],
                                   start=True, stop=True)
                mm.then_inc(r.logits_done, 1)
                wide(0, 0)

            def up(n, f):
                e, fc = f // FC0, f % FC0
                if fc == 0:
                    pe.wait_ge(xe_rest_ready, E0 * n + e + 1)
                    if starts(n):
                        pe.wait_ge(rest_done, e + 1)
                since(pe, g_done, NF * n + f - 1)
                values = (xe_high[:, e % 2, :], xe_rest[:, e % 2, :])
                for out, c0 in ((a1, 0), (a3, FW)):
                    cols = slice(c0 + fc * P, c0 + fc * P + P)
                    mm = products(pe, out[f % 2][:], (w_high[:, e, cols], w_rest[:, e, cols]), values, True, True)
                mm.then_inc(up_done, 1)

            def down(n, f):
                e, fc = f // FC0, f % FC0
                pe.wait_ge(g_ready, NF * n + f + 1)
                if f == 0:
                    since(pe, x_done, n)
                cols = slice(2 * FW + fc * P, 2 * FW + fc * P + P)
                products(pe, y_ps[:], (w_high[:, e, cols], w_rest[:, e, cols]),
                         (g_high[:, f % SLOTS, :], g_rest[:, f % SLOTS, :]), f == 0, f == NF - 1)\
                    .then_inc(down_done, 1)

            def chunk(n):
                for f in range(NF):
                    if f % FC0 == 0:
                        ahead(wide, n, f // FC0)
                    up(n, f)
                    behind(down, n, f, DOWN)

            def end():
                for f in range(NF - DOWN, NF):
                    down(NCH - 1, f)

            chunks(pe, first, chunk, end)


def attention1_stage(k):
    nc = k.nc
    with ExitStack() as ctx:
        def sb(name, shape, dtype=F32):
            return ctx.enter_context(nc.sbuf_tensor(name, shape, dtype))

        def sem(name):
            return ctx.enter_context(nc.semaphore(name))

        def bank(name):
            return ctx.enter_context(nc.psum_tensor(name, [P, CH], F32))

        HEADS = [(r, c) for r in range(R1) for c in range(G1)]
        NH = len(HEADS)
        W = P + L
        BLOCKS = (slice(0, P), slice(P, W))
        SLOTS = 4
        TURN, VALUES = 2, 3
        rope = sb("rope1", [P, 2, L])
        w_q, w_k, w_v, w_o = sb("w_q1", [P, R1, P]), sb("w_k1", [P, P]), sb("w_v1", [P, G1 * D1]), sb("w_o1", [P, R1, P])
        mask = sb("mask1", [P, W])
        xr, part = sb("x_rotated", [P, T]), sb("rope_part", [P, T])
        v, v_b = sb("v1", [P, TB, G1 * D1]), sb("v1_batch", [P, 2, G1, 32])
        rest = sb("rest1", [P, 2])
        q_round, k_round = sb("q1_rounded", [P, R1, L], F32R), sb("k1_rounded", [P, L], F32R)
        q, kk = sb("q1", [P, R1, L], F32R), sb("k1", [P, L], F32R)
        masked = sb("masked", [P, 2, W])
        low, tot, inv = sb("neg_max1", [P, NH, 2]), sb("sum1", [P, NH, 2]), sb("inv1", [P, NH, 2])
        wait_cell = sb("wait_cell1", [P, NH])
        probs, turned = sb("probs1", [P, SLOTS, W]), sb("probs1_t", [P, 2, W])
        o = sb("o1", [P, R1, L])
        s_ps = [bank(f"s1_{i}") for i in range(2)]
        pt_ps = [bank(f"pt1_{i}") for i in range(2)]
        o_ps = [bank(f"o1_{i}") for i in range(2)]
        q_ps = [bank(f"q1_{i}") for i in range(2)]
        loaded, rope_parts, xr_ready, v_done, v_out, v_zeroed, v_ready = (
            sem(f"a1_{n}") for n in ("loaded", "rope_parts", "xr", "v", "v_out", "v_zeroed", "v_ready"))
        q_done, q_rounded, q_low_out, q_high_out, k_done, k_rounded, k_out = (
            sem(f"a1_{n}") for n in ("q", "q_rounded", "q_low_out", "q_high_out", "k", "k_rounded", "k_out"))
        s_done, masked_done, exp_done, inv_ready, normed, pt_done, pt_out, pv_done = (
            sem(f"a1_{n}") for n in ("s", "masked", "exp", "inv", "normed", "pt", "pt_out", "pv"))
        o_low_out, o_high_out, wo_done, x_done = (sem(f"a1_{n}") for n in ("o_low_out", "o_high_out", "wo", "x"))
        block = ctx.enter_context(nc.Block())

        def pair(a, i):
            return a[:, 2 * i:2 * i + 2, :].rearrange("p r i -> p (r i)")

        def batches(eng, first, body, end):
            first()
            body(0)
            with eng.Fori(1, B - 1) as b:
                body(b)
            body(B - 1)
            end()

        def behind(step, b, p, lag):
            if p >= lag:
                step(b, p - lag)
            elif not isinstance(b, int) or b > 0:
                step(b - 1, p - lag + NH)

        def last(b):
            return isinstance(b, int) and b == B - 1

        def starts(b):
            return isinstance(b, int) and b == 0

        @block.sync
        def _(sp):
            load_parts(sp, loaded, [(rope[:], k.d["rope1"]), (w_v[:], k.d["w_v1"]), (w_q[:], k.d["w_q1"]),
                                    (w_k[:], k.d["w_k1"]), (w_o[:], k.d["w_o1"]), (mask[:], k.d["mask1"]),
                                    (rest[:], k.d["rest1"])])

        @block.scalar
        def _(act):
            def round_q(b):
                act.wait_ge(q_done, b + 1)
                since(act, q_high_out, b)
                for i in range(2):
                    op = act.activation(pair(q_round, i), q_ps[i][:], ACT.Copy)
                op.then_inc(q_rounded, 1)

            def round_k(b):
                act.wait_ge(k_done, b + 1)
                since(act, k_out, b)
                act.activation(k_round[:], q_ps[0][:, 0:L], ACT.Copy).then_inc(k_rounded, 1)

            def exps(b, p):
                act.wait_ge(masked_done, NH * b + p + 1)
                since(act, pt_done, NH * b + p + 1 - SLOTS)
                for i, cols in enumerate(BLOCKS):
                    op = act.activation(probs[:, p % SLOTS, cols], masked[:, p % 2, cols], ACT.Exp, scale=-1.0,
                                        bias=low[:, p, i:i + 1], accum_out=tot[:, p, i:i + 1])
                op.then_inc(exp_done, 1)

            def turned_copy(b, p):
                act.wait_ge(pt_done, NH * b + p + 1)
                since(act, pv_done, NH * b + p - 1)
                act.activation(turned[:, p % 2, :], pt_ps[p % 2][:, 0:W], ACT.Copy).then_inc(pt_out, 1)

            def o_low(b):
                act.wait_ge(pv_done, NH * b + NH // 2)
                since(act, wo_done, b)
                act.activation(o[:, 0:2, :].rearrange("p r i -> p (r i)"), o_ps[0][:], ACT.Copy).then_inc(o_low_out, 1)

            def o_high(b):
                act.wait_ge(pv_done, NH * (b + 1))
                act.activation(o[:, 2:4, :].rearrange("p r i -> p (r i)"), o_ps[1][:], ACT.Copy).then_inc(o_high_out, 1)

            def first():
                round_q(0)
                round_k(0)

            def body(b):
                for p in range(NH):
                    exps(b, p)
                    behind(turned_copy, b, p, TURN)
                    if p == 4 and not starts(b):
                        o_high(b - 1)
                    if p == 12:
                        o_low(b)
                    if p == 11 and not last(b):
                        round_q(b + 1)
                    if p == 14 and not last(b):
                        round_k(b + 1)

            def end():
                for p in range(NH - TURN, NH):
                    turned_copy(B - 1, p)
                o_high(B - 1)

            batches(act, first, body, end)

        @block.gpsimd
        def _(pool):
            pool.memset(v_b[:], 0.0).then_inc(v_zeroed, 1)

        @block.vector
        def _(dve):
            def v_copy(b):
                since(dve, pv_done, NH * b)
                dve.tensor_copy(v_b[:, :, :, 0:D1], v[:, bass.ds(2 * b, 2), :].rearrange("p t (c d) -> p t c d", c=G1))\
                   .then_inc(v_ready, 1)

            def first():
                dve.wait_ge(loaded, 16 * 7)

                def wide(a, lo, hi):
                    return rope[lo:hi, a:a + 1, :].broadcast_to([hi - lo, B, L])

                def by_batch(a):
                    return a.rearrange("p (b i) -> p b i", b=B)

                dve.tensor_tensor(by_batch(xr[:]), by_batch(k.xhat[:]), wide(0, 0, P), ALU.mult).then_inc(rope_parts, 1)
                half = P // 2
                for lo, to in ((0, half), (half, 0)):
                    dve.tensor_tensor(by_batch(part[to:to + half, :]), by_batch(k.xhat[lo:lo + half, :]),
                                      wide(1, lo, lo + half), ALU.mult).then_inc(rope_parts, 1)
                dve.wait_ge(rope_parts, 3)
                dve.tensor_tensor(xr[:], xr[:], part[:], ALU.add).then_inc(xr_ready, 1)
                split_q(0, 0)
                split_k(0)
                split_q(0, 1)
                dve.wait_ge(v_done, 1)
                dve.tensor_copy(v[:], pt_ps[0][:].rearrange("p (t d) -> p t d", t=TB)).then_inc(v_out, 1)
                dve.wait_ge(v_zeroed, 1)
                dve.wait_ge(v_out, 1)

            def split_q(b, i):
                dve.wait_ge(q_rounded, b + 1)
                since(dve, s_done, (NH * (b - 1) + NH // 2) if i == 0 else NH * b)
                dve.scalar_tensor_tensor(pair(q, i), pair(q_round, i).bitcast(F32), rest[:, 0:1], q_ps[i][:],
                                         ALU.mult, ALU.add).then_inc((q_low_out, q_high_out)[i], 1)

            def split_k(b):
                dve.wait_ge(k_rounded, b + 1)
                since(dve, s_done, NH * b)
                dve.scalar_tensor_tensor(kk[:], k_round[:].bitcast(F32), rest[:, 1:2], q_ps[0][:, 0:L],
                                         ALU.mult, ALU.add).then_inc(k_out, 1)

            def maxima(b, p):
                dve.wait_ge(s_done, NH * b + p + 1)
                since(dve, exp_done, NH * b + p - 1)
                dve.memset(wait_cell[:, p:p + 1], 0.0)
                for i, cols in enumerate(BLOCKS):
                    op = dve.tensor_tensor_reduce(masked[:, p % 2, cols], s_ps[p % 2][:, cols],
                                                  mask[:, P:W - P] if i == 0 else mask[:, 0:L],
                                                  -D1 ** -0.5, -3.0 * NEG,
                                                  ALU.add, ALU.min, low[:, p, i:i + 1])
                op.then_inc(masked_done, 1)

            def normalise(b, p):
                dve.wait_ge(exp_done, NH * b + p + 1)
                dve.reciprocal(inv[:, p, :], tot[:, p, :]).then_inc(inv_ready, 1)
                dve.wait_ge(inv_ready, NH * b + p + 1)
                for i, cols in enumerate(BLOCKS):
                    op = dve.tensor_scalar(probs[:, p % SLOTS, cols], probs[:, p % SLOTS, cols], inv[:, p, i:i + 1],
                                           None, ALU.mult)
                op.then_inc(normed, 1)

            def add_x(b):
                dve.wait_ge(wo_done, b + 1)
                cols = bass.ds(b * L, L)
                dve.scalar_tensor_tensor(k.x[:, cols], q_ps[1][:, 0:L], k.mod[:, 1, 2, bass.ds(b, 1)], k.x[:, cols],
                                         ALU.mult, ALU.add).then_inc(x_done, 1)

            def body(b):
                for p in range(NH):
                    maxima(b, p)
                    behind(normalise, b, p, 1)
                    if p == VALUES:
                        v_copy(b)
                    if p == 8 and not starts(b):
                        add_x(b - 1)
                    if p == 12 and not last(b):
                        split_q(b + 1, 0)
                if not last(b):
                    split_k(b + 1)
                    split_q(b + 1, 1)

            def end():
                normalise(B - 1, NH - 1)
                add_x(B - 1)

            batches(dve, first, body, end)

        @block.tensor
        def _(pe):
            def project_q(b):
                cols = bass.ds(b * L, L)
                for r in range(R1):
                    mm = pe.matmul(q_ps[r // 2][:, L * (r % 2):L * (r % 2) + L], w_q[:, r, :], xr[:, cols],
                                   start=True, stop=True)
                mm.then_inc(q_done, 1)

            def project_k(b):
                pe.wait_ge(q_low_out, b + 1)
                pe.matmul(q_ps[0][:, 0:L], w_k[:], xr[:, bass.ds(b * L, L)], start=True, stop=True).then_inc(k_done, 1)

            def first():
                pe.wait_ge(loaded, 16 * 7)
                pe.wait_ge(xr_ready, 1)
                project_q(0)
                for t in range(TB):
                    mm = pe.matmul(pt_ps[0][:, t * G1 * D1:(t + 1) * G1 * D1], xr[:, t * P:t * P + P], w_v[:],
                                   start=True, stop=True)
                mm.then_inc(v_done, 1)
                project_k(0)
                pe.wait_ge(v_out, 1)

            def scores(b, p):
                r, c = HEADS[p]
                if p == 0:
                    pe.wait_ge(k_out, b + 1)
                if p == NH // 2:
                    pe.wait_ge(q_high_out, b + 1)
                since(pe, masked_done, NH * b + p - 1)
                rows = slice(32 * c, 32 * c + 3 * D1)
                for i, cols in enumerate(BLOCKS):
                    mm = pe.matmul(s_ps[p % 2][:, cols], q[rows, r, P * i:P * i + P], kk[rows, 0:P * (i + 1)],
                                   start=True, stop=True)
                mm.then_inc(s_done, 1)

            def turn(b, p):
                pe.wait_ge(normed, NH * b + p + 1)
                since(pe, pt_out, NH * b + p - 1)
                for i in range(W // P):
                    mm = pe.transpose(pt_ps[p % 2][:, P * i:P * i + P], probs[:, p % SLOTS, P * i:P * i + P], k.ident[:])
                mm.then_inc(pt_done, 1)

            def values(b, p):
                r, c = HEADS[p]
                if p == 0:
                    pe.wait_ge(v_ready, b + 1)
                    since(pe, o_low_out, b)
                if p == NH // 2:
                    since(pe, o_high_out, b)
                pe.wait_ge(pt_out, NH * b + p + 1)
                out = o_ps[r // 2][32 * c:32 * c + 32, L * (r % 2):L * (r % 2) + L]
                pe.matmul(out, v_b[:, 0, c, :], turned[:, p % 2, 0:L], start=True, stop=False, skip_group_check=True,
                          tile_position=(0, 32 * c))
                pe.matmul(out[:, P:L], v_b[:, 1, c, :], turned[:, p % 2, L:W], start=False, stop=True,
                          skip_group_check=True, tile_position=(0, 32 * c)).then_inc(pv_done, 1)

            def project_out(b):
                pe.wait_ge(o_low_out, b + 1)
                pe.wait_ge(o_high_out, b + 1)
                for r in range(R1):
                    mm = pe.matmul(q_ps[1][:, 0:L], w_o[:, r, :], o[:, r, :], start=(r == 0), stop=(r == R1 - 1))
                mm.then_inc(wo_done, 1)

            def body(b):
                for p in range(NH):
                    scores(b, p)
                    behind(turn, b, p, TURN)
                    behind(values, b, p, VALUES)
                    if p == 6 and not starts(b):
                        pe.wait_ge(q_high_out, b + 1)
                        project_out(b - 1)
                    if p == 10 and not last(b):
                        since(pe, x_done, b)
                        pe.wait_ge(q_high_out, b + 1)
                        pe.wait_ge(k_out, b + 1)
                        project_q(b + 1)
                    if p == 13 and not last(b):
                        project_k(b + 1)

            def end():
                turn(B - 1, NH - 2)
                values(B - 1, NH - 3)
                turn(B - 1, NH - 1)
                values(B - 1, NH - 2)
                values(B - 1, NH - 1)
                project_out(B - 1)

            batches(pe, first, body, end)


def experts1_stage(k):
    nc = k.nc
    with ExitStack() as ctx:
        def sb(name, shape, dtype=F32):
            return ctx.enter_context(nc.sbuf_tensor(name, shape, dtype))

        def sem(name):
            return ctx.enter_context(nc.semaphore(name))

        def bank(name):
            return ctx.enter_context(nc.psum_tensor(name, [P, CH], F32))

        ITEMS = [(e, n) for e in range(E1) for n in range(NCH)]
        NI = len(ITEMS)
        NF = NI * FC1
        SLOTS = 4
        ROUTE = FC1 + 2
        BY_DVE = FC1 - 1
        DOWN = 3
        WE = F1 + FC1 * P
        r = Router(k, ctx, "r1", E1, renormalised=True)
        hs = k.xhat
        xn, acc = sb("x_normed", [P, T]), sb("acc", [P, T])
        pars = sb("pars", [P, LY, NPAR])
        b1 = sb("e1_b1", [P, E1 * FC1])
        raw = sb("e1_w_raw", [P, 2, WE])
        w_high, w_rest = sb("e1_w_high", [P, E1, WE], F32R), sb("e1_w_rest", [P, E1, WE], F32R)
        xe = sb("e1_x", [P, 2, CH])
        xe_high, xe_rest = sb("e1_x_high", [P, 2, CH], F32R), sb("e1_x_rest", [P, 2, CH], F32R)
        hid = sb("e1_hidden", [P, SLOTS, CH])
        hid_high, hid_rest = sb("e1_hidden_high", [P, SLOTS, CH], F32R), sb("e1_hidden_rest", [P, SLOTS, CH], F32R)
        t, tw = sb("e1_sum", [P, 2, CH]), sb("e1_weighted", [P, 2, CH])
        HB = 4
        h_ps, y_ps = [bank(f"h1_{i}") for i in range(HB)], [bank(f"y1_{i}") for i in range(2)]
        mean_ps, wide_ps = bank("mean1"), bank("e1_wide")
        logits_ps = wide_ps[:, 0:TB * E1].rearrange("p (t e) -> p t e", e=E1)
        norm = Norm(k, ctx, "n1", [mean_ps], [wide_ps], mean_ps[:, 0:TB])
        small, w_in = sem("e1_small"), [sem(f"e1_w_in{e}") for e in range(E1)]
        high_done, rest_done, xe_ready, xe_high_ready, xe_rest_ready, h_done, gelu_done, hid_ready, down_done = (
            sem(f"e1_{n}") for n in ("w_high", "w_rest", "xe", "xe_high", "xe_rest", "h", "gelu", "hid", "down"))
        comb_done, t_done, tw_done, added, final, hid_high_done = (
            sem(f"e1_{n}") for n in ("comb", "t", "tw", "added", "final", "hid_high"))
        block = ctx.enter_context(nc.Block())

        def par(l, i):
            return pars[:, bass.ds(l, 1), i:i + 1].rearrange("p l n -> p (l n)")

        def layers(eng, first, layer):
            first()
            layer(0)
            with eng.Fori(1, LY - 1) as l:
                layer(l)
            layer(LY - 1)

        def last(l):
            return isinstance(l, int) and l == LY - 1

        def starts(l):
            return isinstance(l, int) and l == 0

        def ahead(step, l, i):
            if i + 1 < NI:
                step(l, i + 1)
            elif not last(l):
                step(l + 1, 0)

        def norm_steps(l, i, delay):
            n = i - delay - (NI - NCH + 2)
            if n >= 0:
                if not last(l):
                    return l + 1, n
            elif n + NI < NCH and not (starts(l) and n + NI < 2):
                return l, n + NI
            return None

        def splits(i):
            return ((i // NCH + E1 - 1) % E1, i >= NCH) if i % NCH == 1 else None

        def split_of(l, i):
            which = splits(i)
            if which and not (which[1] and last(l)):
                return (l + 1 if which[1] else l), which[0]
            return None

        @block.sync
        def _(sp):
            load_parts(sp, small, [(pars[:], k.d["pars"]), (r.order[:], k.d["order1"])])

            def layer(l):
                for e in range(E1):
                    since(sp, rest_done, E1 * l + e - 1)
                    sp.dma_start(raw[:, e % 2, 0:F1], k.d["e1_w1"][:, bass.ds(l, 1), e, :].rearrange("p l f -> p (l f)"))\
                      .then_inc(w_in[e], 16)
                    sp.dma_start(raw[:, e % 2, F1:WE], k.d["e1_w2"][:, bass.ds(l, 1), e, :].rearrange("p l f -> p (l f)"))\
                      .then_inc(w_in[e], 16)

            layers(sp, lambda: None, layer)

        @block.gpsimd
        def _(pool):
            def split_rest(l, e):
                pool.wait_ge(high_done, E1 * l + e + 1)
                pool.tensor_tensor(w_rest[:, e, :], raw[:, e % 2, :], w_high[:, e, :].bitcast(F32), ALU.subtract)\
                    .then_inc(rest_done, 1)

            def x_rest(l, i):
                pool.wait_ge(xe_high_ready, NI * l + i + 1)
                pool.tensor_tensor(xe_rest[:, i % 2, :], xe[:, i % 2, :], xe_high[:, i % 2, :].bitcast(F32),
                                   ALU.subtract).then_inc(xe_rest_ready, 1)

            def add(l, i):
                e, n = ITEMS[i]
                cols = slice(n * CH, (n + 1) * CH)
                pool.wait_ge(tw_done, NI * l + i + 1)
                since(pool, added, NADD * l + i + 1 - 2 * NCH)
                pool.tensor_tensor(acc[:, cols], acc[:, cols], tw[:, i % 2, :], ALU.add).then_inc(added, 1)

            def first():
                norm.pool_root(pool, 0, 0)
                norm.pool_root(pool, 1, 1)
                for e in range(E1 - 1):
                    split_rest(0, e)
                    if e == 0:
                        x_rest(0, 0)

            def layer(l):
                for i in range(NI):
                    ahead(x_rest, l, i)
                    at = norm_steps(l, i, 0)
                    if at:
                        norm.pool_root(pool, at[1], NCH * at[0] + at[1])
                    if 1 <= ITEMS[i - 1][0] < E1 - 1 and i >= 1:
                        add(l, i - 1)
                    at = split_of(l, i)
                    if at:
                        split_rest(*at)

            layers(pool, first, layer)

        @block.scalar
        def _(act):
            def x_high(l, i):
                act.wait_ge(xe_ready, NI * l + i + 1)
                since(act, h_done, NF * l + FC1 * (i - 1))
                act.activation(xe_high[:, i % 2, :], xe[:, i % 2, :], ACT.Copy).then_inc(xe_high_ready, 1)

            def gelu(l, f):
                i, fc = f // FC1, f % FC1
                act.wait_ge(h_done, NF * l + f + 1)
                since(act, down_done, NF * l + f + 1 - SLOTS)
                c = FC1 * ITEMS[i][0] + fc
                op = act.activation(hid[:, f % SLOTS, :], h_ps[f % HB][:], ACT.Gelu, bias=b1[:, c:c + 1])
                if fc != BY_DVE:
                    op = act.activation(hid_high[:, f % SLOTS, :], h_ps[f % HB][:], ACT.Gelu, bias=b1[:, c:c + 1])
                op.then_inc(gelu_done, 1)

            def first():
                norm.act_square(act, xn, 0, 0)
                norm.act_square(act, xn, 1, 1)
                act.wait_ge(small, 32)
                x_high(0, 0)

            def layer(l):
                for f in range(NF):
                    i, fc = f // FC1, f % FC1
                    gelu(l, f)
                    at = norm_steps(l, i, 0)
                    if fc == 1 and at:
                        norm.act_square(act, xn, at[1], NCH * at[0] + at[1])
                    if f == ROUTE + 1:
                        r.exps(act, l)
                    if fc == 1:
                        ahead(x_high, l, i)

            layers(act, first, layer)

        @block.vector
        def _(dve):
            def split_high(l, e):
                dve.wait_ge(w_in[e], 32 * (l + 1))
                since(dve, down_done, NF * (l - 1) + NCH * FC1 * (e + 1))
                c = FC1 * e
                dve.tensor_copy(b1[:, c:c + FC1], pars[:, bass.ds(l, 1), 3 * E1 + c:3 * E1 + c + FC1]
                                .rearrange("p l n -> p (l n)"))
                dve.tensor_copy(w_high[:, e, :], raw[:, e % 2, :]).then_inc(high_done, 1)

            def scale_x(l, i):
                e, n = ITEMS[i]
                dve.wait_ge(norm.normed, norm.base + NCH * l + n + 1)
                since(dve, xe_rest_ready, NI * l + i - 1)
                dve.tensor_scalar(xe[:, i % 2, :], xn[:, n * CH:(n + 1) * CH], par(l, e), par(l, E1 + e),
                                  ALU.mult, ALU.add).then_inc(xe_ready, 1)

            def hid_split(l, f):
                dve.wait_ge(gelu_done, NF * l + f + 1)
                if f % FC1 == BY_DVE:
                    dve.tensor_copy(hid_high[:, f % SLOTS, :], hid[:, f % SLOTS, :]).then_inc(hid_high_done, 1)
                    dve.wait_ge(hid_high_done, NI * l + f // FC1 + 1)
                dve.tensor_tensor(hid_rest[:, f % SLOTS, :], hid[:, f % SLOTS, :],
                                  hid_high[:, f % SLOTS, :].bitcast(F32), ALU.subtract).then_inc(hid_ready, 1)

            def expert_out(l, i):
                e, n = ITEMS[i]
                dve.wait_ge(down_done, NF * l + FC1 * (i + 1))
                dve.scalar_tensor_tensor(t[:, i % 2, :], y_ps[i % 2][:], par(l, 2 * E1 + e),
                                         hs[:, n * CH:(n + 1) * CH], ALU.add, ALU.add).then_inc(t_done, 1)

            def weighted(l, i):
                e, n = ITEMS[i]
                dve.wait_ge(t_done, NI * l + i + 1)
                dve.wait_ge(comb_done, NI * l + i + 1)
                if e > 0:
                    since(dve, added, NADD * l + min(i - NCH - 1, NADD))
                out = acc[:, n * CH:(n + 1) * CH] if e == 0 else tw[:, i % 2, :]
                dve.tensor_tensor(out, t[:, i % 2, :], wide_ps[:], ALU.mult).then_inc(tw_done, 1)
                if e == E1 - 1:
                    dve.wait_ge(tw_done, NI * l + i + 1)
                    dve.tensor_tensor(hs[:, n * CH:(n + 1) * CH], acc[:, n * CH:(n + 1) * CH], tw[:, i % 2, :],
                                      ALU.add).then_inc(final, 1)

            def first():
                dve.wait_ge(small, 32)
                norm.dve_center(dve, hs, xn, 0, 0)
                norm.dve_add_eps(dve, 0, 0)
                norm.dve_center(dve, hs, xn, 1, 1)
                split_high(0, 0)
                norm.dve_split(dve, 0, 0)
                norm.dve_scale(dve, xn, 0, 0)
                scale_x(0, 0)
                norm.dve_add_eps(dve, 1, 1)
                split_high(0, 1)
                split_high(0, 2)

            def layer(l):
                for f in range(NF):
                    i, fc = f // FC1, f % FC1
                    hid_split(l, f)
                    at, end = norm_steps(l, i, 0), norm_steps(l, i, 1)
                    if fc == 1 and at:
                        norm.dve_center(dve, hs, xn, at[1], NCH * at[0] + at[1])
                    if fc == 3 and at:
                        norm.dve_add_eps(dve, at[1], NCH * at[0] + at[1])
                    if end is None and starts(l) and i == 0:
                        end = (l, 1)
                    if fc == 0 and end:
                        norm.dve_split(dve, end[1], NCH * end[0] + end[1])
                    if fc == 1 and end:
                        norm.dve_scale(dve, xn, end[1], NCH * end[0] + end[1])
                    if ROUTE <= f < ROUTE + r.PARTS:
                        r.route(dve, f - ROUTE, logits_ps,
                                pars[:, bass.ds(l, 1), NPAR - TB * E1:NPAR].rearrange("p l (t e) -> p (l t) e", e=E1), l)
                    if (i, fc) in ((2, 3), (3, 0)):
                        weighted(l, i - 2)
                    if fc == 1:
                        ahead(scale_x, l, i)
                    if fc == 2:
                        if i >= 1:
                            expert_out(l, i - 1)
                            if i >= 3:
                                weighted(l, i - 1)
                        elif not starts(l):
                            expert_out(l - 1, NI - 1)
                            weighted(l - 1, NI - 1)
                    at = split_of(l, i)
                    if fc == 3 and at:
                        split_high(*at)

            layers(dve, first, layer)
            expert_out(LY - 1, NI - 1)
            weighted(LY - 1, NI - 1)
            dve.wait_ge(final, NCH * LY)
            for b in range(B):
                cols = slice(b * L, b * L + L)
                dve.scalar_tensor_tensor(k.x[:, cols], hs[:, cols], k.mod[:, 1, 5, b:b + 1], k.x[:, cols],
                                         ALU.mult, ALU.add)

        @block.tensor
        def _(pe):
            def up(l, f):
                i, fc = f // FC1, f % FC1
                e, n = ITEMS[i]
                if fc == 0:
                    if n == 0:
                        pe.wait_ge(rest_done, E1 * l + e + 1)
                    pe.wait_ge(xe_rest_ready, NI * l + i + 1)
                since(pe, gelu_done, NF * l + f + 1 - HB)
                cols = slice(fc * P, fc * P + P)
                products(pe, h_ps[f % HB][:], (w_high[:, e, cols], w_rest[:, e, cols]),
                         (xe_high[:, i % 2, :], xe_rest[:, i % 2, :]), True, True).then_inc(h_done, 1)

            def down(l, f):
                i, fc = f // FC1, f % FC1
                e = ITEMS[i][0]
                pe.wait_ge(hid_ready, NF * l + f + 1)
                if fc == 0:
                    since(pe, t_done, NI * l + i - 1)
                cols = slice(F1 + fc * P, F1 + fc * P + P)
                products(pe, y_ps[i % 2][:], (w_high[:, e, cols], w_rest[:, e, cols]),
                         (hid_high[:, f % SLOTS, :], hid_rest[:, f % SLOTS, :]), fc == 0, fc == FC1 - 1)\
                    .then_inc(down_done, 1)

            def comb(l, i, scaled):
                pe.wait_ge(norm.normed, norm.base + scaled)
                e, n = ITEMS[i]
                pe.wait_ge(r.comb_ready, l + 1)
                since(pe, tw_done, NI * l + i)
                blocks = slice(BPC * n, BPC * n + BPC)
                widen(pe, k, wide_ps, r.high[:, blocks, e], r.rest[:, blocks, e]).then_inc(comb_done, 1)

            def logits(l):
                since(pe, final, NCH * l)
                pe.wait_ge(norm.normed, norm.base + NCH * l + NCH - 1)
                for tb in range(TB):
                    mm = pe.matmul(logits_ps[:, tb, :], hs[:, tb * P:(tb + 1) * P],
                                   pars[:, bass.ds(l, 1), ROUTER:ROUTER + E1].rearrange("p l e -> p (l e)"),
                                   start=True, stop=True)
                mm.then_inc(r.logits_done, 1)

            def mean(l, n):
                since(pe, final, NCH * l - (NCH - 1 - n))
                since(pe, norm.var_out, norm.base + NCH * l + n)
                norm.pe_mean(pe, hs, n, NCH * l + n)

            def first():
                mean(0, 0)
                norm.pe_var(pe, 0, 0)
                mean(0, 1)
                norm.pe_wide(pe, 0, 0)
                norm.pe_var(pe, 1, 1)
                pe.wait_ge(small, 32)

            def layer(l):
                for f in range(NF):
                    i, fc = f // FC1, f % FC1
                    up(l, f)
                    at, end = norm_steps(l, i, 0), norm_steps(l, i, 1)
                    if end is None and starts(l) and i == 0:
                        end = (l, 1)
                    if fc == 1 and at:
                        mean(*at)
                    if (i, fc) == (1, 2):
                        logits(l)
                    if fc == 3 and at:
                        norm.pe_var(pe, at[1], NCH * at[0] + at[1])
                    if fc == 1 and end:
                        if i == 2:
                            pe.wait_ge(r.link, r.STEPS * l + 1)
                        since(pe, tw_done, NI * l + {NI - 1: NI - 2, 0: -1, 1: 0, 2: 0}[i])
                        norm.pe_wide(pe, end[1], NCH * end[0] + end[1])
                    if (i, fc) in ((2, 3), (3, 0)):
                        comb(l, i - 2, NCH * (l + 1))
                    if fc == 2 and i >= 3:
                        comb(l, i - 1, NCH * (l + 1) + (i == NI - 1 and not last(l)))
                    if fc == 2 and i == 0 and not starts(l):
                        comb(l - 1, NI - 1, NCH * l + 2)
                    if f >= DOWN:
                        down(l, f - DOWN)
                    elif not starts(l):
                        down(l - 1, f - DOWN + NF)

            layers(pe, first, layer)
            for f in range(NF - DOWN, NF):
                down(LY - 1, f)
            comb(LY - 1, NI - 1, NCH * LY)


def build(nc, k):
    with ExitStack() as ctx:
        def sb(name, shape):
            return ctx.enter_context(nc.sbuf_tensor(name, shape, F32))

        k.x = sb("x", [P, T])
        k.xhat = sb("xhat", [P, T])
        k.ident = sb("ident", [P, P])
        k.mean_mat = sb("mean_mat", [P, P])
        k.mod = sb("mod", [P, 2, 6, B])
        k.ident_r = ctx.enter_context(nc.sbuf_tensor("ident_rounded", [P, P], F32R))
        k.neg_half = sb("neg_half", [P, 1])
        k.norm_semaphores = [ctx.enter_context(nc.semaphore(f"norm_{n}")) for n in Norm.SEMAPHORES]
        k.chunks_normed = 0
        setup_stage(k)
        norm_stage(k, "n0a")
        attention0_stage(k)
        norm_stage(k, "n0b", 0, 3)
        experts0_stage(k)
        norm_stage(k, "n1a", 1, 0)
        attention1_stage(k)
        norm_stage(k, "n1b", 1, 3)
        experts1_stage(k)
        store_stage(k, k.x)


def store_stage(k, src):
    with k.nc.semaphore("stored") as stored, k.nc.Block() as block:
        @block.sync
        def _(sp):
            sp.dma_start(k.out, src[:]).then_inc(stored, 16)
            sp.wait_ge(stored, 16)



def constants():
    f = np.float32
    inv = (f(1.0) / np.power(f(10000.0), np.arange(0, D0, 2, dtype=f) / f(D0))).astype(f)
    ang = np.outer(np.arange(L, dtype=f), inv).astype(f)
    cos, sin = np.cos(ang).astype(f).T, np.sin(ang).astype(f).T
    rope0 = np.stack([np.tile(cos, (4, 1)), np.concatenate([-sin, sin, -sin, sin], 0)], 1)
    t = np.arange(SPAN)[None, :] - (L - IG)
    row = np.arange(P)[:, None] // H0
    signed = row - t
    swapped = (row + IG // 2) % IG - t
    dist = np.stack([np.abs(signed), np.abs(swapped), np.where(signed < 0, NEG, 0.0)], 1).astype(f)
    return {"rope0": rope0, **more_constants(), "dist": dist, "ident": np.eye(P, dtype=f), "mean_mat": np.full((P, P), 1.0 / P, f)}


def more_constants():
    f = np.float32
    half = P // 2
    theta = (f(1.0) / np.power(f(10000.0), np.arange(half, dtype=f) / f(half))).astype(f)
    ang = (np.arange(L, dtype=f)[:, None] * theta[None, :]).astype(f)
    cos, sin = np.cos(ang).astype(f).T, np.sin(ang).astype(f).T
    rope1 = np.stack([np.concatenate([cos, cos], 0), np.concatenate([sin, -sin], 0)], 1)
    future = np.arange(P + L)[None, :] - P > np.arange(P)[:, None]
    part = np.arange(P) % 32 // D1
    out = {"rope1": rope1, "mask1": np.where(future, -1.0e9, 0.0).astype(f),
           "rest1": np.stack([-1.0 * (part == 1), -1.0 * (part == 2)], 1).astype(f)}
    for n, e in (("0", E0), ("1", E1)):
        out["order" + n] = np.ascontiguousarray(np.broadcast_to(np.arange(e, 0, -1).astype(f), (P, TB, e)))
    return out


EVEN_FIRST = np.concatenate([np.arange(0, P, 2), np.arange(1, P, 2)])


def laid_out(i):
    a = {n: np.asarray(v) for n, v in i.items()}
    f = np.float32
    ch = EVEN_FIRST
    w = a["L0_attn_w_qkv"][ch].reshape(P, 3, H0, D0)
    rotated = np.concatenate([w[..., D0 // 2:], w[..., :D0 // 2]], -1)
    w_qk = np.stack([w[:, 0:2], rotated[:, 0:2]], 0)
    w_qk = w_qk.reshape(2, P, 2, PAIRS, P).transpose(1, 3, 2, 0, 4).reshape(P, 2 * PAIRS, 2, P)
    w1 = a["L0_attn_w1"]
    w1a, w1b, w2 = np.zeros((P, P), f), np.zeros((P, P), f), np.zeros((P, 64), f)
    for q in range(4):
        m = slice(32 * q, 32 * q + 32)
        lo, hi = slice(16 * q, 16 * q + 16), slice(64 + 16 * q, 80 + 16 * q)
        w1a[lo, m], w1a[hi, m] = w1[:H0], w1[H0:]
        w1b[lo, m], w1b[hi, m] = w1[H0:], w1[:H0]
        w2[m, lo] = a["L0_attn_w2"]
    cols = np.stack([np.tile(a["L0_attn_log_p"].reshape(-1), IG), np.tile(a["L0_attn_log_a"].reshape(-1), IG),
                     np.tile(a["L0_attn_b2"], IG), np.tile(a["L0_attn_b1"], 4)], 1)
    w_q = np.zeros((P, R1, P), f)
    w_k = np.zeros((P, P), f)
    w_o = np.zeros((P, R1, P), f)
    for c in range(G1):
        w_k[:, 32 * c:32 * c + 3 * D1] = np.tile(a["L1_attn_W_k"][D1 * c:D1 * c + D1].T, (1, 3))
        for r in range(R1):
            hd = R1 * c + r
            w_q[:, r, 32 * c:32 * c + 3 * D1] = np.tile(a["L1_attn_W_q"][D1 * hd:D1 * hd + D1].T, (1, 3))
            w_o[32 * c:32 * c + D1, r, :] = a["L1_attn_W_o"][ch, D1 * hd:D1 * hd + D1].T
    wide = FC0 * P
    e0_w1, e0_w3, e0_w2 = np.zeros((P, E0, wide), f), np.zeros((P, E0, wide), f), np.zeros((E0, wide, P), f)
    e0_w1[:, :, :F0] = a["L0_ffn_w1"].transpose(1, 0, 2)[ch]
    e0_w3[:, :, :F0] = a["L0_ffn_w3"].transpose(1, 0, 2)[ch]
    e0_w2[:, :F0] = a["L0_ffn_w2"][:, :, ch]
    lg, lb, l2 = (a[n][:, :, ch].transpose(2, 0, 1) for n in ("L1_ffn_ln_g", "L1_ffn_ln_b", "L1_ffn_b2"))
    b1 = a["L1_ffn_b1"].reshape(LY, E1, FC1, P).transpose(3, 0, 1, 2).reshape(P, LY, E1 * FC1)
    rw = a["L1_ffn_router_w"][:, ch].transpose(1, 0, 2)
    rb = np.broadcast_to(np.tile(a["L1_ffn_router_b"], (1, TB))[None], (P, LY, TB * E1))
    d = {
        "x": a["L0_attn_x"].reshape(T, P).T[ch],
        "c": np.stack([a["L0_c"].T, a["L1_c"].T], 1),
        "wmod": np.stack([a["L0_wmod"].reshape(P, 6, P)[:, :, ch], a["L1_wmod"].reshape(P, 6, P)[:, :, ch]], 1),
        "w_qk": w_qk, "w_v": w[:, 2].reshape(P, H0 * D0),
        "w_o0": a["L0_attn_w_o"].reshape(PAIRS, P, P).transpose(1, 0, 2)[:, :, ch],
        "w1a": w1a, "w1b": w1b, "w2": w2, "head_cols": cols,
        "gate_w": a["L0_ffn_gate_w"].T[ch], "e0_w1": e0_w1, "e0_w3": e0_w3,
        "e0_w2": e0_w2.reshape(E0, FC0, P, P).transpose(2, 0, 1, 3),
        "w_q1": w_q, "w_k1": w_k, "w_v1": a["L1_attn_W_v"].T, "w_o1": w_o,
        "pars": np.concatenate([lg, lb, l2, b1, rw, rb], 2),
        "e1_w1": a["L1_ffn_w1"].transpose(2, 0, 1, 3)[ch],
        "e1_w2": a["L1_ffn_w2"][:, :, :, ch].reshape(LY, E1, FC1, P, P).transpose(3, 0, 1, 2, 4)
                 .reshape(P, LY, E1, FC1 * P),
    }
    d.update(constants())
    return {n: np.ascontiguousarray(v) for n, v in d.items()}


def kernel(**inputs):
    import concourse.bacc as bacc
    from concourse.bass_utils import run_bass_kernel_spmd

    nc = bacc.Bacc("TRN2", target_bir_lowering=False, num_devices=1)
    k = Kit()
    k.nc, k.d = nc, {}
    arrays = {}
    for name, a in laid_out(inputs).items():
        arrays[f"in_{name}"] = a
        k.d[name] = nc.dram_tensor(f"in_{name}", a.shape, mybir.dt.from_np(a.dtype), kind="ExternalInput").ap()
    k.out = nc.dram_tensor("out_x", (P, T), F32, kind="ExternalOutput").ap()
    build(nc, k)
    r = run_bass_kernel_spmd(nc, [arrays], core_ids=[0])
    return np.ascontiguousarray(r.results[0]["out_x"][np.argsort(EVEN_FIRST)].T).reshape(B, L, P)
```

```python
from contextlib import ExitStack

import numpy as np

import concourse.bass as bass
from concourse import mybir

ALU = mybir.AluOpType
ACT = mybir.ActivationFunctionType
AX = mybir.AxisListType
F32 = mybir.dt.float32
F32R = mybir.dt.float32r

P = 128
B, L = 8, 256
T = B * L
CH = 512
NCH = T // CH
TB = T // P
BPC = CH // P
EPS = 1e-5

H0, D0 = 16, 64
PAIRS = H0 // 2
IG = 8
UNITS = L // IG
UPB = P // IG
SPAN = L - IG + L
NEG = -1.0e30

E0, F0 = 8, 352
FC0 = 3

H1, D1, G1 = 16, 8, 4
R1 = H1 // G1

LY, E1, F1 = 4, 4, 512
FC1 = F1 // P
ROUTER = 3 * E1 + E1 * FC1
NPAR = ROUTER + E1 + TB * E1
NADD = (E1 - 2) * NCH


def unit_columns(u):
    if u < UPB:
        return P * (UPB - 1 - u), P
    return P * UPB + L * (UNITS - 1 - u), L


UCOLS = P * UPB + L * UPB


class Kit:
    pass


def load_parts(nc, done, parts):
    for dst, src in parts:
        nc.dma_start(dst, src).then_inc(done, 16)


def since(eng, sem, value):
    if not isinstance(value, int) or value > 0:
        eng.wait_ge(sem, value)


def setup_stage(k, later_loads, later_loaded):
    nc = k.nc
    with ExitStack() as ctx:
        def sb(name, shape):
            return ctx.enter_context(nc.sbuf_tensor(name, shape, F32))

        def sem(name):
            return ctx.enter_context(nc.semaphore(name))

        wmod = sb("wmod", [P, 2, 6, P])
        c = sb("c_cols", [P, 2, B])
        sc = sb("silu_c", [P, 2, B])
        mag = sb("gate_magnitude", [P, 2, 2, B])
        sgn = sb("gate_sign", [P, 2, 2, B])
        ps = ctx.enter_context(nc.psum_tensor("mod_ps", [P, 2, 6, B], F32))
        loaded, silu_ready, mod_ready, mod_copied, gate_parts = (
            sem("setup_loaded"), sem("silu_ready"), sem("mod_ready"), sem("mod_copied"), sem("gate_parts"))
        block = ctx.enter_context(nc.Block())

        @block.sync
        def _(sp):
            load_parts(sp, loaded, [(c[:], k.d["c"]), (wmod[:], k.d["wmod"]), (k.ident[:], k.d["ident"]),
                                    (k.mean_mat[:], k.d["mean_mat"]), (k.x[:], k.d["x"])])
            load_parts(sp, later_loaded, later_loads)

        @block.scalar
        def _(act):
            act.wait_ge(loaded, 80)
            act.activation(sc[:], c[:], ACT.Silu).then_inc(silu_ready, 1)

        @block.tensor
        def _(pe):
            pe.wait_ge(silu_ready, 1)
            for l in range(2):
                for n in range(6):
                    mm = pe.matmul(ps[:, l, n, :], wmod[:, l, n, :], sc[:, l, :], start=True, stop=True)
            mm.then_inc(mod_ready, 1)

        @block.vector
        def _(dve):
            dve.memset(k.neg_half[:], -0.5)
            dve.wait_ge(loaded, 80)
            dve.wait_ge(mod_ready, 1)
            for l in range(2):
                dve.tensor_copy(k.mod[:, l, :, :], ps[:, l, :, :]).then_inc(mod_copied, 1)
            dve.wait_ge(mod_copied, 2)
            for l in range(2):
                for j, n in enumerate((2, 5)):
                    dve.scalar_tensor_tensor(mag[:, l, j, :], k.mod[:, l, n, :], -1.0, k.mod[:, l, n, :],
                                             ALU.mult, ALU.max).then_inc(gate_parts, 1)
                    dve.tensor_scalar(sgn[:, l, j, :], k.mod[:, l, n, :], 0.0, 2.0, ALU.is_ge, ALU.mult)\
                       .then_inc(gate_parts, 1)
                for n in (1, 4):
                    dve.tensor_scalar(k.mod[:, l, n, :], k.mod[:, l, n, :], 1.0, None, ALU.add)
            dve.wait_ge(gate_parts, 8)
            dve.tensor_scalar(mag[:], mag[:], 0.25, None, ALU.max).then_inc(gate_parts, 1)
            dve.wait_ge(gate_parts, 9)
            for l in range(2):
                for j, n in enumerate((2, 5)):
                    dve.scalar_tensor_tensor(k.mod[:, l, n, :], sgn[:, l, j, :], -1.0, mag[:, l, j, :],
                                             ALU.add, ALU.mult)


class Norm:

    SEMAPHORES = ("mean", "centered", "squared", "var", "var_out", "rooted", "wide", "normed")

    def __init__(self, k, ctx, tag, mean_ps, wide_ps, var_ps):
        nc = k.nc

        def sb(name, shape, dtype=F32):
            return ctx.enter_context(nc.sbuf_tensor(f"{tag}_{name}", shape, dtype))

        self.k, self.mean_ps, self.wide_ps, self.var_ps = k, mean_ps, wide_ps, var_ps
        self.squares = sb("squares", [P, 2, CH])
        self.plus_eps, self.rstd = sb("var_plus_eps", [P, NCH, BPC]), sb("rstd", [P, NCH, BPC])
        (self.mean, self.centered, self.squared, self.var, self.var_out, self.rooted, self.wide,
         self.normed) = k.norm_semaphores
        self.base = k.chunks_normed
        k.chunks_normed = k.chunks_normed + NCH

    def pe_mean(self, pe, src, n, at):
        at = self.base + at
        since(pe, self.centered, at + 1 - len(self.mean_ps))
        pe.matmul(self.mean_ps[n % len(self.mean_ps)][:], self.k.mean_mat[:], src[:, n * CH:(n + 1) * CH],
                  start=True, stop=True).then_inc(self.mean, 1)

    def pe_var(self, pe, n, at):
        at = self.base + at
        pe.wait_ge(self.squared, at + 1)
        since(pe, self.var_out, at)
        for j in range(BPC):
            mm = pe.matmul(self.var_ps[:, n * BPC + j:n * BPC + j + 1], self.squares[:, n % 2, P * j:P * j + P],
                           self.k.mean_mat[:, 0:1], start=True, stop=True)
        mm.then_inc(self.var, 1)

    def pe_wide(self, pe, n, at):
        at = self.base + at
        pe.wait_ge(self.rooted, at + 1)
        since(pe, self.normed, at + 1 - len(self.wide_ps))
        widen(pe, self.k, self.wide_ps[n % len(self.wide_ps)], self.rstd[:, n, :])\
            .then_inc(self.wide, 1)

    def act_square(self, act, dst, n, at):
        at = self.base + at
        act.wait_ge(self.centered, at + 1)
        since(act, self.var, at - 1)
        act.activation(self.squares[:, n % 2, :], dst[:, n * CH:(n + 1) * CH], ACT.Square).then_inc(self.squared, 1)

    def dve_center(self, dve, src, dst, n, at):
        at = self.base + at
        cols = slice(n * CH, (n + 1) * CH)
        dve.wait_ge(self.mean, at + 1)
        dve.tensor_tensor(dst[:, cols], src[:, cols], self.mean_ps[n % len(self.mean_ps)][:], ALU.subtract)\
           .then_inc(self.centered, 1)

    def dve_add_eps(self, dve, n, at):
        at = self.base + at
        dve.wait_ge(self.var, at + 1)
        dve.tensor_scalar(self.plus_eps[:, n, :], self.var_ps[:, n * BPC:(n + 1) * BPC], EPS, None, ALU.add)\
           .then_inc(self.var_out, 1)

    def pool_root(self, pool, n, at):
        at = self.base + at
        pool.wait_ge(self.var_out, at + 1)
        pool.tensor_tensor(self.rstd[:, n, :], self.plus_eps[:, n, :], self.k.neg_half[:].broadcast_to([P, BPC]),
                           ALU.pow).then_inc(self.rooted, 1)

    def dve_scale(self, dve, dst, n, at):
        at = self.base + at
        cols = slice(n * CH, (n + 1) * CH)
        dve.wait_ge(self.wide, at + 1)
        dve.tensor_tensor(dst[:, cols], dst[:, cols], self.wide_ps[n % len(self.wide_ps)][:], ALU.mult)\
           .then_inc(self.normed, 1)


def widen(pe, k, bank, values):
    for j in range(BPC):
        mm = pe.transpose(bank[:, P * j:P * j + P], values[:, j:j + 1].broadcast_to([P, P]), k.ident[:])
    return mm


def norm_stage(k, tag, layer=None, slot=None):
    nc = k.nc
    with ExitStack() as ctx:
        def banks(name):
            return [ctx.enter_context(nc.psum_tensor(f"{tag}_{name}{i}", [P, CH], F32)) for i in range(2)]

        var_ps = ctx.enter_context(nc.psum_tensor(f"{tag}_var", [P, CH], F32))
        norm = Norm(k, ctx, tag, banks("mean_ps"), banks("wide_ps"), var_ps)
        block = ctx.enter_context(nc.Block())

        def modulate(dve, n):
            dve.wait_ge(norm.normed, norm.base + n + 1)
            for b in range(2 * n, 2 * n + 2):
                dve.tensor_scalar(k.xhat[:, b * L:(b + 1) * L], k.xhat[:, b * L:(b + 1) * L],
                                  k.mod[:, layer, slot + 1, b:b + 1], k.mod[:, layer, slot, b:b + 1],
                                  ALU.mult, ALU.add)

        @block.tensor
        def _(pe):
            for n in range(NCH + 2):
                if n < NCH:
                    norm.pe_mean(pe, k.x, n, n)
                if 1 <= n <= NCH:
                    norm.pe_var(pe, n - 1, n - 1)
                if n >= 2:
                    norm.pe_wide(pe, n - 2, n - 2)

        @block.scalar
        def _(act):
            for n in range(NCH):
                norm.act_square(act, k.xhat, n, n)

        @block.gpsimd
        def _(pool):
            for n in range(NCH):
                norm.pool_root(pool, n, n)

        @block.vector
        def _(dve):
            for n in range(NCH + 2):
                if n < NCH:
                    norm.dve_center(dve, k.x, k.xhat, n, n)
                if 1 <= n <= NCH:
                    norm.dve_add_eps(dve, n - 1, n - 1)
                if n >= 2:
                    norm.dve_scale(dve, k.xhat, n - 2, n - 2)
                    if layer is not None and n >= 3:
                        modulate(dve, n - 3)
            if layer is not None:
                modulate(dve, NCH - 1)


def attention0_inputs(k, ctx):
    def sb(name, shape):
        return ctx.enter_context(k.nc.sbuf_tensor(name, shape, F32))

    w_qk = sb("w_qk", [P, 2 * PAIRS, 2, P])
    w_v = sb("w_v", [P, H0 * D0])
    w_o = sb("w_o", [P, PAIRS, P])
    rope = sb("rope0", [P, 2, L])
    w1a, w1b = sb("w1a", [P, P]), sb("w1b", [P, P])
    w2 = sb("w2", [P, IG // 2 * H0])
    cols = sb("head_cols", [P, 4])
    loaded = ctx.enter_context(k.nc.semaphore("a0_loaded"))
    k.attention0_inputs = w_qk, w_v, w_o, rope, w1a, w1b, w2, cols, loaded
    return [(cols[:], k.d["head_cols"]), (rope[:], k.d["rope0"]), (w_qk[:], k.d["w_qk"]), (w1a[:], k.d["w1a"]),
            (w1b[:], k.d["w1b"]), (w2[:], k.d["w2"]), (w_v[:], k.d["w_v"]), (w_o[:], k.d["w_o0"])]


def attention0_stage(k):
    nc = k.nc
    with ExitStack() as ctx:
        def sb(name, shape):
            return ctx.enter_context(nc.sbuf_tensor(name, shape, F32))

        def sem(name):
            return ctx.enter_context(nc.semaphore(name))

        w_qk, w_v, w_o, rope, w1a, w1b, w2, cols, loaded = k.attention0_inputs
        soft = sb("softplus", [P, 3, 2])
        h = sb("h_batch", [P, L])
        v = sb("v", [P, 2, H0 * D0])
        qk = sb("qk", [P, 2 * PAIRS, L])
        r1, r2 = sb("rope_cos_part", [P, 2, L]), sb("rope_sin_part", [P, 2, L])
        s0 = sb("scores_keys0", [P, L, H0])
        s1 = sb("scores_keys1", [P, P, H0])
        ta, tb = sb("mlp_in_a", [P, UCOLS]), sb("mlp_in_b", [P, UCOLS])
        hid = sb("hidden", [P, 2, 2 * L])
        probs = sb("logits_probs", [P, UCOLS])
        top = sb("row_max", [P, UNITS])
        wait_cell = sb("wait_cell", [P, UNITS])
        neg = sb("neg_row_max", [P, UNITS])
        tot = sb("row_sum", [P, UNITS])
        inv = sb("inv_row_sum", [P, UNITS])
        add_tab = sb("kerple_bias_mask", [P, SPAN])
        mix_tab = sb("kerple_shifted", [P, SPAN])
        o = qk[:, 0:PAIRS, :]
        p0 = sb("probs_keys0", [P, L, H0])
        p1 = sb("probs_keys1", [P, P, H0])
        dist = p0[:].rearrange("p i h -> p (i h)")[:, 0:3 * SPAN].rearrange("p (a t) -> p a t", a=3)

        def two_banks(name):
            return ctx.enter_context(nc.psum_tensor(name, [P, 2, CH], F32))

        proj_b, pair_b, hid_b = two_banks("proj_b"), [two_banks("pair_b0"), two_banks("pair_b1")], two_banks("hid_b")
        proj_ps = [proj_b[:, i, :] for i in range(2)]
        t_ps = [pair_b[0][:, i, :] for i in range(2)]
        logit_ps = [pair_b[1][:, i, :] for i in range(2)]
        hid_ps = [hid_b[:, i, :] for i in range(2)]
        out_ps = proj_ps[0]
        dist_loaded = sem("dist_loaded")
        soft_step, lns, tabs, mix_laid = sem("soft_step"), sem("lns"), sem("tabs"), sem("mix_laid")
        tab_scaled = sem("tab_scaled")
        h_ready, proj_done, rope_parts, rope_done = sem("h_ready"), sem("proj_done"), sem("rope_parts"), sem("rope_done")
        s_done, s_even, s_odd = sem("s_done"), sem("s_even"), sem("s_odd")
        v_done, v_out = sem("v_done"), sem("v_out")
        t_done, ta_out, tb_out = sem("t_done"), sem("ta_out"), sem("tb_out")
        hid_done, gelu_done = sem("hid_done"), sem("gelu_done")
        logit_done, logit_out, neg_ready = sem("logit_done"), sem("logit_out"), sem("neg_ready")
        exp_done, inv_ready, probs_ready = sem("exp_done"), sem("inv_ready"), sem("probs_ready")
        pt_done, pt_even, pt_odd = sem("pt_done"), sem("pt_even"), sem("pt_odd")
        pv_done, o_even, o_odd = sem("pv_done"), sem("o_even"), sem("o_odd")
        wo_done, x_done = sem("wo_done"), sem("x_done")
        block = ctx.enter_context(nc.Block())

        NQ = 2 * PAIRS
        GROUPS = [(g, jb) for g in range(UNITS // 4) for jb in range(g // (UPB // 4) + 1)]
        NG = len(GROUPS)

        def batches(eng, first, whole, last):
            first()
            whole(0)
            with eng.Fori(1, B - 1) as b:
                whole(b)
            last()

        def weights_at(g, jb):
            i0 = 4 * IG * g
            if jb == 0:
                return p0[:, i0:i0 + 4 * IG, :].rearrange("p i h -> p (i h)")
            return p1[:, i0 - P:i0 - P + 4 * IG, :].rearrange("p i h -> p (i h)")

        @block.sync
        def _(sp):
            load_parts(sp, dist_loaded, [(dist, k.d["dist"])])
            sp.wait_ge(tabs, 2)
            for u, J in ((UPB - 1, P), (UNITS - 1, L)):
                off, _ = unit_columns(u)
                c0 = L - IG - IG * u
                for rows, dst in ((slice(64, 128), ta), (slice(0, 64), tb)):
                    window = mix_tab[rows, c0:c0 + J]
                    windows = bass.AP(tensor=window.tensor, offset=window.offset, ap=[window.ap[0], [IG, UPB], [1, J]])
                    sp.dma_start(dst[rows, off:off + UPB * J].rearrange("p (u j) -> p u j", u=UPB), windows)\
                      .then_inc(mix_laid, 16)

        @block.gpsimd
        def _(pool):
            def rope_add(b, first=False):
                for n in range(NQ):
                    pool.wait_ge(rope_parts, NQ * b + n + 1)
                    if not first:
                        pool.wait_ge(s_done, PAIRS * b + n // 2 - (PAIRS - 1))
                    pool.tensor_tensor(qk[:, n, :], r1[:, n % 2, :], r2[:, n % 2, :], ALU.add)\
                        .then_inc(rope_done, 1)

            def first():
                rope_add(0, first=True)

            batches(pool, first, lambda b: rope_add(b + 1), lambda: None)

        @block.scalar
        def _(act):
            act.wait_ge(soft_step, 1)
            act.activation(soft[:, 1, :], soft[:, 0, :], ACT.Exp, scale=-1.0).then_inc(lns, 1)
            act.wait_ge(lns, 1)
            act.activation(soft[:, 2, :], soft[:, 1, :], ACT.Ln, bias=1.0).then_inc(lns, 1)
            act.wait_ge(soft_step, 3)
            act.wait_ge(dist_loaded, 16)
            act.activation(add_tab[:], dist[:, 0, :], ACT.Ln, bias=1.0, scale=soft[:, 0, 1:2]).then_inc(lns, 1)
            act.activation(mix_tab[:], dist[:, 1, :], ACT.Ln, bias=1.0, scale=soft[:, 0, 1:2]).then_inc(lns, 1)

            def scores_out(b, c):
                act.wait_ge(s_done, PAIRS * b + c + 1)
                act.activation(s0[:, :, 2 * c:2 * c + 2], pair_b[c % 2][:, :, 0:L].rearrange("p h i -> p i h"),
                               ACT.Copy, scale=D0 ** -0.5)
                act.activation(s1[:, :, 2 * c:2 * c + 2], pair_b[c % 2][:, :, L:L + P].rearrange("p h i -> p i h"),
                               ACT.Copy, scale=D0 ** -0.5).then_inc(s_even, 1)

            def exps(b, c):
                act.wait_ge(neg_ready, b + 1)
                for u in range(4 * c, 4 * c + 4):
                    off, J = unit_columns(u)
                    act.activation(probs[:, off:off + J], probs[:, off:off + J], ACT.Exp, bias=neg[:, u:u + 1],
                                   accum_out=tot[:, u:u + 1]).then_inc(exp_done, 1)

            def ta_copy(b, u):
                off, J = unit_columns(u)
                act.wait_ge(t_done, UNITS * b + u + 1)
                act.activation(ta[0:64, off:off + J], t_ps[u % 2][0:64, 0:J], ACT.Copy)\
                   .then_inc(ta_out, 1)

            def mlp(b):
                ta_copy(b, 0)
                for u in range(UNITS):
                    _, J = unit_columns(u)
                    if u + 1 < UNITS:
                        ta_copy(b, u + 1)
                    act.wait_ge(hid_done, UNITS * b + u + 1)
                    since(act, logit_done, UNITS * b + max(u - 1, 0))
                    act.activation(hid[:, u % 2, 0:2 * J], hid_ps[u % 2][:, 0:2 * J], ACT.Gelu, bias=cols[:, 3:4])\
                       .then_inc(gelu_done, 1)

            def heads_out(b):
                for n, (g, jb) in enumerate(GROUPS):
                    if n % 2 == 0:
                        continue
                    act.wait_ge(pt_done, NG * b + n + 1)
                    act.activation(weights_at(g, jb), hid_ps[n % 2], ACT.Copy).then_inc(pt_odd, 1)
                for c in range(1, PAIRS, 2):
                    act.wait_ge(pv_done, PAIRS * b + c + 1)
                    act.activation(o[:, c, :], proj_ps[c % 2][:, 0:L], ACT.Copy).then_inc(o_odd, 1)

            def first():
                for c in range(0, PAIRS, 2):
                    scores_out(0, c)

            def whole(b):
                mlp(b)
                exps(b, 0)
                exps(b, 1)
                for c in range(0, PAIRS, 2):
                    scores_out(b + 1, c)
                    for g in range(c + 2, min(c + 4, PAIRS)):
                        exps(b, g)
                heads_out(b)

            def last():
                mlp(B - 1)
                for c in range(PAIRS):
                    exps(B - 1, c)
                heads_out(B - 1)

            batches(act, first, whole, last)

        @block.vector
        def _(dve):
            dve.wait_ge(loaded, 16 * 8)
            dve.scalar_tensor_tensor(soft[:, 0, :], cols[:, 0:2], -1.0, cols[:, 0:2], ALU.mult, ALU.max).then_inc(soft_step, 1)
            dve.wait_ge(lns, 2)
            dve.tensor_scalar(soft[:, 1, :], cols[:, 0:2], 0.0, None, ALU.max).then_inc(soft_step, 1)
            dve.wait_ge(soft_step, 2)
            dve.tensor_tensor(soft[:, 0, :], soft[:, 1, :], soft[:, 2, :], ALU.add).then_inc(soft_step, 1)
            dve.wait_ge(lns, 4)
            dve.wait_ge(soft_step, 3)
            dve.tensor_scalar(add_tab[:], add_tab[:], soft[:, 0, 0:1], -1.0, ALU.mult, ALU.mult).then_inc(tab_scaled, 1)
            dve.tensor_scalar(mix_tab[:], mix_tab[:], soft[:, 0, 0:1], -1.0, ALU.mult, ALU.mult).then_inc(tabs, 1)
            dve.wait_ge(tab_scaled, 1)
            dve.wait_ge(dist_loaded, 16)
            dve.scalar_tensor_tensor(add_tab[:], add_tab[:], cols[:, 2:3], dist[:, 2, :], ALU.add, ALU.add)\
               .then_inc(tabs, 1)

            def scores(b, first=False, weights_of=None):
                if not first:
                    since(dve, v_done, 4 * b)
                dve.tensor_scalar(h[:], k.xhat[:, bass.ds(b * L, L)], k.mod[:, 0, 1, bass.ds(b, 1)],
                                  k.mod[:, 0, 0, bass.ds(b, 1)], ALU.mult, ALU.add).then_inc(h_ready, 1)
                for n in range(NQ):
                    dve.wait_ge(proj_done, NQ * b + n + 1)
                    if not first or n >= 2:
                        dve.wait_ge(rope_done, NQ * b + n - 1)
                    ps = proj_ps[n % 2]
                    dve.tensor_tensor(r1[:, n % 2, :], ps[:, 0:L], rope[:, 0, :], ALU.mult)
                    dve.tensor_tensor(r2[:, n % 2, :], ps[:, L:2 * L], rope[:, 1, :], ALU.mult)\
                       .then_inc(rope_parts, 1)
                    if n % 4 == 3 and n >= 7:
                        scores_out(b, n // 2 - 2)
                    if weights_of is not None and n % 2 == 1 and n >= 3:
                        weights(weights_of, n // 2 - 1)
                if weights_of is not None:
                    weights(weights_of, UNITS // 4 - 1)
                scores_out(b, PAIRS - 1)

            def scores_out(b, c):
                dve.wait_ge(s_done, PAIRS * b + c + 1)
                dve.tensor_scalar(s0[:, :, 2 * c:2 * c + 2], pair_b[c % 2][:, :, 0:L].rearrange("p h i -> p i h"),
                                  D0 ** -0.5, None, ALU.mult)
                dve.tensor_scalar(s1[:, :, 2 * c:2 * c + 2], pair_b[c % 2][:, :, L:L + P].rearrange("p h i -> p i h"),
                                  D0 ** -0.5, None, ALU.mult).then_inc(s_odd, 1)

            def tb_copy(b, u):
                off, J = unit_columns(u)
                dve.wait_ge(t_done, UNITS * b + u + 1)
                dve.tensor_copy(tb[64:128, off:off + J], t_ps[u % 2][64:128, 0:J])\
                   .then_inc(tb_out, 1)

            def logits(b, u):
                off, J = unit_columns(u)
                c0 = L - IG - IG * u
                dve.wait_ge(logit_done, UNITS * b + u + 1)
                dve.memset(wait_cell[:, u:u + 1], 0.0)
                dve.tensor_tensor_reduce(probs[:, off:off + J], logit_ps[u % 2][:, 0:J], add_tab[:, c0:c0 + J],
                                         1.0, 3.0 * NEG, ALU.add, ALU.max, top[:, u:u + 1]).then_inc(logit_out, 1)

            def mlp(b):
                tb_copy(b, 0)
                for n in range(4):
                    dve.wait_ge(v_done, 4 * b + n + 1)
                    dve.tensor_copy(v[:, n // 2, CH * (n % 2):CH * (n % 2 + 1)], proj_ps[n % 2])\
                       .then_inc(v_out, 1)
                for u in range(UNITS):
                    if u + 1 < UNITS:
                        tb_copy(b, u + 1)
                    if u >= 1:
                        logits(b, u - 1)
                logits(b, UNITS - 1)
                dve.wait_ge(logit_out, UNITS * (b + 1))
                dve.tensor_scalar(neg[:], top[:], -1.0, None, ALU.mult).then_inc(neg_ready, 1)

            def weights(b, g):
                dve.wait_ge(exp_done, UNITS * b + 4 * g + 4)
                dve.reciprocal(inv[:, 4 * g:4 * g + 4], tot[:, 4 * g:4 * g + 4]).then_inc(inv_ready, 1)
                dve.wait_ge(inv_ready, UNITS // 4 * b + g + 1)
                for u in range(4 * g, 4 * g + 4):
                    off, J = unit_columns(u)
                    op = dve.tensor_scalar(probs[:, off:off + J], probs[:, off:off + J], inv[:, u:u + 1], None,
                                           ALU.mult)
                op.then_inc(probs_ready, 1)

            def heads_out(b):
                for n, (g, jb) in enumerate(GROUPS):
                    if n % 2 == 1:
                        continue
                    dve.wait_ge(pt_done, NG * b + n + 1)
                    dve.tensor_copy(weights_at(g, jb), hid_ps[n % 2]).then_inc(pt_even, 1)
                for c in range(0, PAIRS, 2):
                    dve.wait_ge(pv_done, PAIRS * b + c + 1)
                    dve.tensor_copy(o[:, c, :], proj_ps[c % 2][:, 0:L]).then_inc(o_even, 1)
                dve.wait_ge(wo_done, b + 1)
                dve.scalar_tensor_tensor(k.x[:, bass.ds(b * L, L)], out_ps[:, 0:L], k.mod[:, 0, 2, bass.ds(b, 1)],
                                         k.x[:, bass.ds(b * L, L)], ALU.mult, ALU.add).then_inc(x_done, 1)

            def whole(b):
                mlp(b)
                scores(b + 1, weights_of=b)
                heads_out(b)

            def last():
                mlp(B - 1)
                for g in range(UNITS // 4):
                    weights(B - 1, g)
                heads_out(B - 1)

            batches(dve, lambda: scores(0, first=True), whole, last)

        @block.tensor
        def _(pe):
            def project(b, n, first):
                if not first or n >= 2:
                    pe.wait_ge(rope_parts, NQ * b + n - 1)
                for a in range(2):
                    mm = pe.matmul(proj_ps[n % 2][:, a * L:(a + 1) * L], w_qk[:, n, a, :], h[:],
                                   start=True, stop=True)
                mm.then_inc(proj_done, 1)

            def score(b, c, first):
                pe.wait_ge(rope_done, NQ * b + 2 * c + 2)
                if c >= 2:
                    pe.wait_ge((s_even, s_odd)[c % 2], PAIRS // 2 * b + c // 2)
                for hh in range(2):
                    r = slice(D0 * hh, D0 * hh + D0)
                    ps = pair_b[c % 2][:, hh, :]
                    pe.matmul(ps[:, 0:L], qk[r, 2 * c + 1, 0:P], qk[r, 2 * c, :], start=True, stop=True)
                    mm = pe.matmul(ps[:, L:L + P], qk[r, 2 * c + 1, P:L], qk[r, 2 * c, P:L], start=True, stop=True)
                mm.then_inc(s_done, 1)

            def scores(b, first=False):
                pe.wait_ge(h_ready, b + 1)
                if not first:
                    since(pe, v_out, 4 * b)
                    since(pe, logit_out, UNITS * b)
                    since(pe, x_done, b - 1)
                for n in range(4):
                    project(b, n, first)
                for c in range(PAIRS):
                    score(b, c, first)
                    for n in range(2 * c + 4, min(2 * c + 6, NQ)):
                        project(b, n, first)

            def transpose(b, u):
                _, J = unit_columns(u)
                if u >= 2:
                    pe.wait_ge(ta_out, UNITS * b + u - 1)
                    pe.wait_ge(tb_out, UNITS * b + u - 1)
                for jb in range(J // P):
                    mm = pe.transpose(t_ps[u % 2][:, P * jb:P * jb + P], score_block(u, jb), k.ident[:])
                mm.then_inc(t_done, 1)

            def score_block(u, jb):
                i0 = IG * u - (P if jb else 0)
                return (s1 if jb else s0)[:, i0:i0 + IG, :].rearrange("p i h -> p (i h)")

            def hidden(b, u):
                off, J = unit_columns(u)
                pe.wait_ge(ta_out, UNITS * b + u + 1)
                pe.wait_ge(tb_out, UNITS * b + u + 1)
                since(pe, gelu_done, UNITS * b + max(u - 1, 0))
                pe.matmul(hid_ps[u % 2][:, 0:J], w1a[:], ta[:, off:off + J], start=True, stop=True)
                pe.matmul(hid_ps[u % 2][:, J:2 * J], w1b[:], tb[:, off:off + J], start=True, stop=True)\
                  .then_inc(hid_done, 1)

            def logits(b, u):
                _, J = unit_columns(u)
                pe.wait_ge(gelu_done, UNITS * b + u + 1)
                since(pe, logit_out, UNITS * b + max(u - 1, 0))
                ps = logit_ps[u % 2]
                for jb in range(J // P):
                    pe.matmul(ps[:, P * jb:P * jb + P], score_block(u, jb), k.ident[:], start=(jb == 0), stop=False,
                              is_transpose=True, skip_group_check=True)
                for half in range(2):
                    mm = pe.matmul(ps[64 * half:64 * half + 64, 0:J], w2[:], hid[:, u % 2, half * J:half * J + J],
                                   start=False, stop=True, skip_group_check=True)
                mm.then_inc(logit_done, 1)

            def mlp(b):
                pe.wait_ge(s_even, PAIRS // 2 * (b + 1))
                pe.wait_ge(s_odd, PAIRS // 2 * (b + 1))
                transpose(b, 0)
                pe.wait_ge(rope_parts, NQ * (b + 1))
                since(pe, o_even, PAIRS // 2 * b)
                since(pe, o_odd, PAIRS // 2 * b)
                since(pe, x_done, b)
                for n in range(4):
                    if n >= 2:
                        since(pe, v_out, 4 * b + n - 1)
                    pe.matmul(proj_ps[n % 2], h[:, P * (n // 2):P * (n // 2) + P],
                              w_v[:, CH * (n % 2):CH * (n % 2 + 1)], start=True, stop=True).then_inc(v_done, 1)
                since(pe, pt_even, NG // 2 * b)
                since(pe, pt_odd, NG // 2 * b)
                for u in range(UNITS):
                    if u + 1 < UNITS:
                        transpose(b, u + 1)
                    hidden(b, u)
                    if u >= 1:
                        logits(b, u - 1)
                logits(b, UNITS - 1)

            def heads(b, nxt):
                for n, (g, jb) in enumerate(GROUPS):
                    pe.wait_ge(probs_ready, UNITS // 4 * b + g + 1)
                    if n >= 2:
                        pe.wait_ge((pt_even, pt_odd)[n % 2], NG // 2 * b + n // 2)
                    for j in range(4):
                        off, _ = unit_columns(4 * g + j)
                        mm = pe.transpose(hid_ps[n % 2][:, P * j:P * j + P], probs[:, off + P * jb:off + P * jb + P],
                                          k.ident[:])
                    mm.then_inc(pt_done, 1)
                pe.wait_ge(pt_even, NG // 2 * (b + 1))
                pe.wait_ge(pt_odd, NG // 2 * (b + 1))
                pe.wait_ge(rope_parts, NQ * nxt)
                pe.wait_ge(v_out, 4 * (b + 1))
                for c in range(PAIRS):
                    if c >= 2:
                        pe.wait_ge((o_even, o_odd)[c % 2], PAIRS // 2 * b + c // 2)
                    for hh in range(2):
                        hd = 2 * c + hh
                        dims = slice(D0 * hd, D0 * hd + D0)
                        pe.matmul(proj_ps[c % 2][D0 * hh:D0 * hh + D0, 0:L], v[:, 0, dims], p0[:, :, hd],
                                  start=True, stop=False, skip_group_check=True)
                        mm = pe.matmul(proj_ps[c % 2][D0 * hh:D0 * hh + D0, P:L], v[:, 1, dims], p1[:, :, hd],
                                       start=False, stop=True, skip_group_check=True)
                    mm.then_inc(pv_done, 1)
                pe.wait_ge(o_even, PAIRS // 2 * (b + 1))
                pe.wait_ge(o_odd, PAIRS // 2 * (b + 1))
                for c in range(PAIRS):
                    mm = pe.matmul(out_ps[:, 0:L], w_o[:, c, :], o[:, c, :], start=(c == 0), stop=(c == PAIRS - 1))
                mm.then_inc(wo_done, 1)

            def first():
                pe.wait_ge(loaded, 16 * 8)
                scores(0, first=True)
                pe.wait_ge(mix_laid, 16 * 4)

            def whole(b):
                mlp(b)
                scores(b + 1)
                heads(b, b + 2)

            def last():
                mlp(B - 1)
                heads(B - 1, B)

            batches(pe, first, whole, last)


class Chain:

    def __init__(self, eng, sem, done=0):
        self.eng, self.sem, self.done = eng, sem, done

    def __call__(self, instruction):
        self.done = self.done + 1
        instruction.then_inc(self.sem, 1)
        self.eng.wait_ge(self.sem, self.done)


class Router:
    PARTS = 5
    STARTS = (0, 2, 5, 10, 16)
    STEPS = 20

    def __init__(self, k, ctx, tag, experts, renormalised):
        nc = k.nc

        def sb(name, shape, dtype=F32):
            return ctx.enter_context(nc.sbuf_tensor(f"{tag}_{name}", shape, dtype))

        def sem(name):
            return ctx.enter_context(nc.semaphore(f"{tag}_{name}"))

        self.E, self.renormalised = experts, renormalised
        wide, narrow = [P, TB, experts], [P, TB, 1]
        self.probs, self.work, self.first, self.second = (sb(n, wide) for n in ("probs", "work", "first", "second"))
        self.shifted, self.comb, self.order = sb("shifted", wide), sb("comb", wide), sb("order", wide)
        self.m, self.m1, self.m2, self.rank = (sb(n, narrow) for n in ("m", "m1", "m2", "rank"))
        self.logits_done, self.link, self.shift_ready, self.exp_done, self.comb_ready = (
            sem("logits_done"), sem("link"), sem("shift_ready"), sem("exp_done"), sem("comb_ready"))

    def route(self, dve, part, logits, bias, l):
        def wide(a):
            return a[:].broadcast_to([P, TB, self.E])

        link = Chain(dve, self.link, self.STEPS * l + self.STARTS[part])
        if part == 0:
            dve.wait_ge(self.logits_done, l + 1)
            if bias is None:
                link(dve.tensor_copy(self.work[:], logits))
            else:
                link(dve.tensor_tensor(self.work[:], logits, bias, ALU.add))
            link(dve.tensor_reduce(self.m[:], self.work[:], AX.X, ALU.max))
            dve.tensor_tensor(self.shifted[:], self.work[:], wide(self.m), ALU.subtract).then_inc(self.shift_ready, 1)
        elif part == 1:
            dve.wait_ge(self.exp_done, l + 1)
            link(dve.tensor_reduce(self.m1[:], self.probs[:], AX.X, ALU.add))
            link(dve.reciprocal(self.m2[:], self.m1[:]))
            link(dve.tensor_tensor(self.probs[:], self.probs[:], wide(self.m2), ALU.mult))
        elif part == 2:
            self.highest(dve, link, self.probs[:], self.m1, self.first)
        elif part == 3:
            link(dve.scalar_tensor_tensor(self.work[:], self.first[:], -2.0, self.probs[:], ALU.mult, ALU.add))
            self.highest(dve, link, self.work[:], self.m2, self.second)
        else:
            link(dve.tensor_tensor(self.first[:], self.first[:], self.second[:], ALU.add))
            if self.renormalised:
                link(dve.tensor_tensor(self.rank[:], self.m1[:], self.m2[:], ALU.add))
                link(dve.reciprocal(self.m[:], self.rank[:]))
                link(dve.tensor_tensor(self.probs[:], self.probs[:], wide(self.m), ALU.mult))
            dve.tensor_tensor(self.comb[:], self.first[:], self.probs[:], ALU.mult).then_inc(self.comb_ready, 1)

    def highest(self, dve, link, values, top, out):
        link(dve.tensor_reduce(top[:], values, AX.X, ALU.max))
        link(dve.tensor_tensor(out[:], values, top[:].broadcast_to([P, TB, self.E]), ALU.is_equal))
        link(dve.tensor_tensor(out[:], out[:], self.order[:], ALU.mult))
        link(dve.tensor_reduce(self.rank[:], out[:], AX.X, ALU.max))
        link(dve.tensor_tensor(out[:], out[:], self.rank[:].broadcast_to([P, TB, self.E]), ALU.is_equal))

    def exps(self, act, l):
        act.wait_ge(self.shift_ready, l + 1)
        act.activation(self.probs[:], self.shifted[:], ACT.Exp).then_inc(self.exp_done, 1)


def products(pe, out, weights, values, start, stop):
    for n, (a, b) in enumerate(((0, 0), (0, 1), (1, 0))):
        mm = pe.matmul(out, weights[a], values[b], start=start and n == 0, stop=stop and n == 2)
    return mm


def experts0_stage(k):
    nc = k.nc
    with ExitStack() as ctx:
        def sb(name, shape, dtype=F32):
            return ctx.enter_context(nc.sbuf_tensor(name, shape, dtype))

        def sem(name):
            return ctx.enter_context(nc.semaphore(name))

        def bank(name):
            return ctx.enter_context(nc.psum_tensor(name, [P, CH], F32))

        r = Router(k, ctx, "r0", E0, renormalised=False)
        NF = E0 * FC0
        FW = FC0 * P
        WE = 3 * FW
        SLOTS = 4
        DOWN = 2
        gate_w = sb("gate_w", [P, E0])
        raw = sb("e0_w_raw", [P, 2, WE])
        w_high, w_rest = sb("e0_w_high", [P, E0, WE], F32R), sb("e0_w_rest", [P, E0, WE], F32R)
        comb = sb("e0_comb", [P, E0, BPC])
        xe = sb("e0_x", [P, 2, CH])
        xe_high, xe_rest = sb("e0_x_high", [P, 2, CH], F32R), sb("e0_x_rest", [P, 2, CH], F32R)
        silu = sb("e0_silu", [P, 2, CH])
        g = sb("e0_gated", [P, 2, CH])
        g_high, g_rest = sb("e0_gated_high", [P, SLOTS, CH], F32R), sb("e0_gated_rest", [P, SLOTS, CH], F32R)
        wide_ps = [bank(f"wide{i}") for i in range(2)]
        a1 = [bank(f"a1_{i}") for i in range(2)]
        a3 = [bank(f"a3_{i}") for i in range(2)]
        y_ps, lg = bank("y0"), bank("lg0")
        small, w_in = sem("e0_small"), sem("e0_w_in")
        high_done, rest_done, comb_laid, wide_done, xe_ready, xe_high_ready, xe_rest_ready = (
            sem(f"e0_{n}") for n in ("w_high", "w_rest", "comb_laid", "wide", "xe", "xe_high", "xe_rest"))
        up_done, silu_done, g_done, g_high_done, g_ready, down_done, x_done = (
            sem(f"e0_{n}") for n in ("up", "silu", "g", "g_high", "g_rest", "down", "x"))
        block = ctx.enter_context(nc.Block())

        def chunks(eng, first, chunk, end):
            first()
            chunk(0)
            with eng.Fori(1, NCH - 1) as n:
                chunk(n)
            chunk(NCH - 1)
            end()

        def last(n):
            return isinstance(n, int) and n == NCH - 1

        def starts(n):
            return isinstance(n, int) and n == 0

        def ahead(step, n, e):
            if e + 1 < E0:
                step(n, e + 1)
            elif not last(n):
                step(n + 1, 0)

        def behind(step, n, f, lag):
            if f >= lag:
                step(n, f - lag)
            elif not starts(n):
                step(n - 1, f - lag + NF)

        @block.sync
        def _(sp):
            load_parts(sp, small, [(gate_w[:], k.d["gate_w"]), (r.order[:], k.d["order0"])])
            for e in range(E0):
                if e >= 2:
                    sp.wait_ge(rest_done, e - 1)
                    sp.wait_ge(w_in, 48 * (e - 1))
                load_parts(sp, w_in, [(raw[:, e % 2, 0:FW], k.d["e0_w1"][:, e, :]),
                                      (raw[:, e % 2, FW:2 * FW], k.d["e0_w3"][:, e, :]),
                                      (raw[:, e % 2, 2 * FW:WE].rearrange("p (c n) -> p c n", c=FC0),
                                       k.d["e0_w2"][:, e, :, :])])
                sp.wait_ge(w_in, 48 * (e + 1))

        @block.gpsimd
        def _(pool):
            def split_rest(e):
                pool.wait_ge(high_done, e + 1)
                pool.tensor_tensor(w_rest[:, e, :], raw[:, e % 2, :], w_high[:, e, :].bitcast(F32), ALU.subtract)\
                    .then_inc(rest_done, 1)

            def x_rest(n, e):
                pool.wait_ge(xe_high_ready, E0 * n + e + 1)
                pool.tensor_tensor(xe_rest[:, e % 2, :], xe[:, e % 2, :], xe_high[:, e % 2, :].bitcast(F32),
                                   ALU.subtract).then_inc(xe_rest_ready, 1)

            def first():
                split_rest(0)
                x_rest(0, 0)

            def chunk(n):
                for e in range(E0):
                    if starts(n) and e + 1 < E0:
                        split_rest(e + 1)
                    ahead(x_rest, n, e)

            chunks(pool, first, chunk, lambda: None)

        @block.scalar
        def _(act):
            def x_high(n, e):
                act.wait_ge(xe_ready, E0 * n + e + 1)
                since(act, up_done, NF * n + FC0 * (e - 1))
                act.activation(xe_high[:, e % 2, :], xe[:, e % 2, :], ACT.Copy).then_inc(xe_high_ready, 1)

            def gated_high(n, f):
                act.wait_ge(g_done, NF * n + f + 1)
                since(act, down_done, NF * n + f + 1 - SLOTS)
                act.activation(g_high[:, f % SLOTS, :], g[:, f % 2, :], ACT.Copy).then_inc(g_high_done, 1)

            def first():
                r.exps(act, 0)
                x_high(0, 0)

            def chunk(n):
                for f in range(NF):
                    if f % FC0 == 1:
                        ahead(x_high, n, f // FC0)
                    act.wait_ge(up_done, NF * n + f + 1)
                    since(act, g_done, NF * n + f - 1)
                    act.activation(silu[:, f % 2, :], a1[f % 2][:], ACT.Silu).then_inc(silu_done, 1)
                    gated_high(n, f)

            chunks(act, first, chunk, lambda: None)

        @block.vector
        def _(dve):
            def split_high(e):
                dve.wait_ge(w_in, 48 * (e + 1))
                dve.tensor_copy(w_high[:, e, :], raw[:, e % 2, :]).then_inc(high_done, 1)

            def lay_comb(n):
                since(dve, wide_done, E0 * n)
                dve.tensor_copy(comb[:], r.comb[:, bass.ds(BPC * n, BPC), :].rearrange("p t e -> p e t"))\
                   .then_inc(comb_laid, 1)

            def scale_x(n, e):
                dve.wait_ge(wide_done, E0 * n + e + 1)
                since(dve, xe_rest_ready, E0 * n + e - 1)
                dve.tensor_tensor(xe[:, e % 2, :], k.xhat[:, bass.ds(n * CH, CH)], wide_ps[e % 2][:], ALU.mult)\
                   .then_inc(xe_ready, 1)

            def gated_rest(n, f):
                dve.wait_ge(g_high_done, NF * n + f + 1)
                dve.tensor_tensor(g_rest[:, f % SLOTS, :], g[:, f % 2, :], g_high[:, f % SLOTS, :].bitcast(F32),
                                  ALU.subtract).then_inc(g_ready, 1)

            def add_x(n):
                dve.wait_ge(down_done, NF * (n + 1))
                for j in range(2):
                    cols = bass.ds(n * CH + j * L, L)
                    op = dve.scalar_tensor_tensor(k.x[:, cols], y_ps[:, j * L:j * L + L],
                                                  k.mod[:, 0, 5, bass.ds(2 * n + j, 1)], k.x[:, cols],
                                                  ALU.mult, ALU.add)
                op.then_inc(x_done, 1)

            def first():
                split_high(0)
                dve.wait_ge(small, 32)
                for part in range(r.PARTS):
                    r.route(dve, part, lg[:, 0:TB * E0].rearrange("p (t e) -> p t e", e=E0), None, 0)
                dve.wait_ge(r.comb_ready, 1)
                lay_comb(0)
                scale_x(0, 0)

            def chunk(n):
                for f in range(NF):
                    e, fc = f // FC0, f % FC0
                    if fc == 0 and starts(n) and e + 1 < E0:
                        split_high(e + 1)
                    if fc == 0:
                        ahead(scale_x, n, e)
                    behind(gated_rest, n, f, 1)
                    dve.wait_ge(silu_done, NF * n + f + 1)
                    dve.tensor_tensor(g[:, f % 2, :], silu[:, f % 2, :], a3[f % 2][:], ALU.mult).then_inc(g_done, 1)
                    if f == NF - FC0 - 2 and not last(n):
                        lay_comb(n + 1)
                    if f == DOWN - 1 and not starts(n):
                        add_x(n - 1)

            def end():
                gated_rest(NCH - 1, NF - 1)
                add_x(NCH - 1)

            chunks(dve, first, chunk, end)

        @block.tensor
        def _(pe):
            def wide(n, e):
                if e == 0:
                    pe.wait_ge(comb_laid, n + 1)
                since(pe, xe_ready, E0 * n + e - 1)
                widen(pe, k, wide_ps[e % 2], comb[:, e, :]).then_inc(wide_done, 1)

            def first():
                pe.wait_ge(small, 32)
                for t in range(TB):
                    mm = pe.matmul(lg[:, t * E0:(t + 1) * E0], k.xhat[:, t * P:(t + 1) * P], gate_w[:],
                                   start=True, stop=True)
                mm.then_inc(r.logits_done, 1)
                wide(0, 0)

            def up(n, f):
                e, fc = f // FC0, f % FC0
                if fc == 0:
                    pe.wait_ge(xe_rest_ready, E0 * n + e + 1)
                    if starts(n):
                        pe.wait_ge(rest_done, e + 1)
                since(pe, g_done, NF * n + f - 1)
                values = (xe_high[:, e % 2, :], xe_rest[:, e % 2, :])
                for out, c0 in ((a1, 0), (a3, FW)):
                    cols = slice(c0 + fc * P, c0 + fc * P + P)
                    mm = products(pe, out[f % 2][:], (w_high[:, e, cols], w_rest[:, e, cols]), values, True, True)
                mm.then_inc(up_done, 1)

            def down(n, f):
                e, fc = f // FC0, f % FC0
                pe.wait_ge(g_ready, NF * n + f + 1)
                if f == 0:
                    since(pe, x_done, n)
                cols = slice(2 * FW + fc * P, 2 * FW + fc * P + P)
                products(pe, y_ps[:], (w_high[:, e, cols], w_rest[:, e, cols]),
                         (g_high[:, f % SLOTS, :], g_rest[:, f % SLOTS, :]), f == 0, f == NF - 1)\
                    .then_inc(down_done, 1)

            def chunk(n):
                for f in range(NF):
                    if f % FC0 == 0:
                        ahead(wide, n, f // FC0)
                    up(n, f)
                    behind(down, n, f, DOWN)

            def end():
                for f in range(NF - DOWN, NF):
                    down(NCH - 1, f)

            chunks(pe, first, chunk, end)


def attention1_stage(k):
    nc = k.nc
    with ExitStack() as ctx:
        def sb(name, shape, dtype=F32):
            return ctx.enter_context(nc.sbuf_tensor(name, shape, dtype))

        def sem(name):
            return ctx.enter_context(nc.semaphore(name))

        def bank(name):
            return ctx.enter_context(nc.psum_tensor(name, [P, CH], F32))

        HEADS = [(r, c) for r in range(R1) for c in range(G1)]
        NH = len(HEADS)
        W = P + L
        BLOCKS = (slice(0, P), slice(P, W))
        SLOTS = 4
        TURN, VALUES, NORM = 3, 5, 1
        Q_AT = 8
        OUT_AT = VALUES + 1
        rope = sb("rope1", [P, 2, L])
        w_q, w_k, w_v, w_o = sb("w_q1", [P, R1, P]), sb("w_k1", [P, P]), sb("w_v1", [P, G1 * D1]), sb("w_o1", [P, R1, P])
        mask = sb("mask1", [P, W])
        xh, xr, part = sb("h1_batch", [P, L]), sb("x_rotated", [P, L]), sb("rope_part", [P, L])
        v = sb("v1", [P, 2, G1, 32])
        rest = sb("rest1", [P, 2])
        q_round, k_round = sb("q1_rounded", [P, R1, L], F32R), sb("k1_rounded", [P, L], F32R)
        q, kk = sb("q1", [P, R1, L], F32R), sb("k1", [P, L], F32R)
        masked = sb("masked", [P, 2, W])
        low, tot, inv = sb("neg_max1", [P, NH, 2]), sb("sum1", [P, NH, 2]), sb("inv1", [P, NH, 2])
        wait_cell = sb("wait_cell1", [P, NH])
        probs, turned = sb("probs1", [P, SLOTS, W]), sb("probs1_t", [P, 2, W])
        o = sb("o1", [P, R1, L])
        s_ps = [bank(f"s1_{i}") for i in range(2)]
        pt_ps = [bank(f"pt1_{i}") for i in range(2)]
        o_ps = [bank(f"o1_{i}") for i in range(2)]
        q_ps = [bank(f"q1_{i}") for i in range(2)]
        loaded, xh_ready, rope_parts, xr_ready, v_zeroed, v_ready = (
            sem(f"a1_{n}") for n in ("loaded", "xh", "rope_parts", "xr", "v_zeroed", "v_ready"))
        q_done, q_rounded, q_low_out, q_high_out, k_done, k_rounded, k_out = (
            sem(f"a1_{n}") for n in ("q", "q_rounded", "q_low_out", "q_high_out", "k", "k_rounded", "k_out"))
        s_done, masked_done, exp_done, inv_ready, normed, pt_done, pt_out, pv_done = (
            sem(f"a1_{n}") for n in ("s", "masked", "exp", "inv", "normed", "pt", "pt_out", "pv"))
        o_low_out, o_high_out, wo_done, x_done = (sem(f"a1_{n}") for n in ("o_low_out", "o_high_out", "wo", "x"))
        block = ctx.enter_context(nc.Block())

        def pair(a, i):
            return a[:, 2 * i:2 * i + 2, :].rearrange("p r i -> p (r i)")

        def batches(eng, first, body, end):
            first()
            body(0)
            with eng.Fori(1, B - 1) as b:
                body(b)
            body(B - 1)
            end()

        def behind(step, b, p, lag):
            if p >= lag:
                step(b, p - lag)
            elif not isinstance(b, int) or b > 0:
                step(b - 1, p - lag + NH)

        def last(b):
            return isinstance(b, int) and b == B - 1

        def starts(b):
            return isinstance(b, int) and b == 0

        @block.sync
        def _(sp):
            load_parts(sp, loaded, [(rope[:], k.d["rope1"]), (w_v[:], k.d["w_v1"]), (w_q[:], k.d["w_q1"]),
                                    (w_k[:], k.d["w_k1"]), (w_o[:], k.d["w_o1"]), (mask[:], k.d["mask1"]),
                                    (rest[:], k.d["rest1"])])

        @block.scalar
        def _(act):
            def round_q(b, i):
                act.wait_ge(q_done, 2 * b + i + 1)
                since(act, (q_low_out, q_high_out)[i], b)
                act.activation(pair(q_round, i), q_ps[i][:], ACT.Copy).then_inc(q_rounded, 1)

            def round_k(b):
                act.wait_ge(k_done, b + 1)
                since(act, k_out, b)
                act.activation(k_round[:], q_ps[0][:, 0:L], ACT.Copy).then_inc(k_rounded, 1)

            def exps(b, p):
                act.wait_ge(masked_done, NH * b + p + 1)
                since(act, pt_done, NH * b + p + 1 - SLOTS)
                for i, cols in enumerate(BLOCKS):
                    op = act.activation(probs[:, p % SLOTS, cols], masked[:, p % 2, cols], ACT.Exp, scale=-1.0,
                                        bias=low[:, p, i:i + 1], accum_out=tot[:, p, i:i + 1])
                op.then_inc(exp_done, 1)

            def turned_copy(b, p):
                act.wait_ge(pt_done, NH * b + p + 1)
                since(act, pv_done, NH * b + p - 1)
                act.activation(turned[:, p % 2, :], pt_ps[p % 2][:, 0:W], ACT.Copy).then_inc(pt_out, 1)

            def o_low(b):
                act.wait_ge(pv_done, NH * b + NH // 2)
                since(act, wo_done, b)
                act.activation(o[:, 0:2, :].rearrange("p r i -> p (r i)"), o_ps[0][:], ACT.Copy).then_inc(o_low_out, 1)

            def o_high(b):
                act.wait_ge(pv_done, NH * (b + 1))
                act.activation(o[:, 2:4, :].rearrange("p r i -> p (r i)"), o_ps[1][:], ACT.Copy).then_inc(o_high_out, 1)

            def first():
                round_q(0, 0)
                round_q(0, 1)
                round_k(0)

            def body(b):
                for p in range(NH):
                    exps(b, p)
                    behind(turned_copy, b, p, TURN)
                    if p == VALUES and not starts(b):
                        o_high(b - 1)
                    if p == 7 + VALUES + 2:
                        o_low(b)
                    if p == Q_AT + 2 and not last(b):
                        round_q(b + 1, 0)
                    if p == Q_AT + 4 and not last(b):
                        round_q(b + 1, 1)
                    if p == Q_AT + 5 and not last(b):
                        round_k(b + 1)

            def end():
                for p in range(NH - TURN, NH):
                    turned_copy(B - 1, p)
                o_high(B - 1)

            batches(act, first, body, end)

        @block.gpsimd
        def _(pool):
            def rotate(b):
                half = P // 2
                pool.wait_ge(xh_ready, b + 1)
                since(pool, k_done, b)
                pool.tensor_tensor(xr[:], xh[:], rope[:, 0, :], ALU.mult).then_inc(rope_parts, 1)
                for n, (lo, to) in enumerate(((0, half), (half, 0))):
                    pool.wait_ge(rope_parts, 3 * b + n + 1)
                    pool.tensor_tensor(part[to:to + half, :], xh[lo:lo + half, :], rope[lo:lo + half, 1, :],
                                       ALU.mult).then_inc(rope_parts, 1)
                pool.wait_ge(rope_parts, 3 * (b + 1))
                pool.tensor_tensor(xr[:], xr[:], part[:], ALU.add).then_inc(xr_ready, 1)

            def first():
                pool.wait_ge(loaded, 16 * 7)
                rotate(0)
                pool.memset(v[:], 0.0).then_inc(v_zeroed, 1)

            def body(b):
                if not last(b):
                    rotate(b + 1)

            batches(pool, first, body, lambda: None)

        @block.vector
        def _(dve):
            def v_copy(b):
                if starts(b):
                    dve.wait_ge(v_zeroed, 1)
                since(dve, pv_done, NH * b)
                dve.tensor_copy(v[:, :, :, 0:D1], q_ps[0][:, L:L + 2 * G1 * D1].rearrange("p (t c d) -> p t c d", t=2, c=G1))\
                   .then_inc(v_ready, 1)

            def take_h(b):
                since(dve, xr_ready, b)
                dve.tensor_copy(xh[:], k.xhat[:, bass.ds(b * L, L)]).then_inc(xh_ready, 1)

            def first():
                take_h(0)
                dve.wait_ge(loaded, 16 * 7)
                split_q(0, 0)
                split_k(0)
                split_q(0, 1)

            def split_q(b, i):
                dve.wait_ge(q_rounded, 2 * b + i + 1)
                since(dve, s_done, (NH * (b - 1) + NH // 2) if i == 0 else NH * b)
                dve.scalar_tensor_tensor(pair(q, i), pair(q_round, i).bitcast(F32), rest[:, 0:1], q_ps[i][:],
                                         ALU.mult, ALU.add).then_inc((q_low_out, q_high_out)[i], 1)

            def split_k(b):
                dve.wait_ge(k_rounded, b + 1)
                since(dve, s_done, NH * b)
                dve.scalar_tensor_tensor(kk[:], k_round[:].bitcast(F32), rest[:, 1:2], q_ps[0][:, 0:L],
                                         ALU.mult, ALU.add).then_inc(k_out, 1)

            def maxima(b, p):
                dve.wait_ge(s_done, NH * b + p + 1)
                since(dve, exp_done, NH * b + p - 1)
                dve.memset(wait_cell[:, p:p + 1], 0.0)
                for i, cols in enumerate(BLOCKS):
                    op = dve.tensor_tensor_reduce(masked[:, p % 2, cols], s_ps[p % 2][:, cols],
                                                  mask[:, P:W - P] if i == 0 else mask[:, 0:L],
                                                  -D1 ** -0.5, -3.0 * NEG,
                                                  ALU.add, ALU.min, low[:, p, i:i + 1])
                op.then_inc(masked_done, 1)

            def normalise(b, p):
                dve.wait_ge(exp_done, NH * b + p + 1)
                dve.reciprocal(inv[:, p, :], tot[:, p, :]).then_inc(inv_ready, 1)
                dve.wait_ge(inv_ready, NH * b + p + 1)
                for i, cols in enumerate(BLOCKS):
                    op = dve.tensor_scalar(probs[:, p % SLOTS, cols], probs[:, p % SLOTS, cols], inv[:, p, i:i + 1],
                                           None, ALU.mult)
                op.then_inc(normed, 1)

            def add_x(b):
                dve.wait_ge(wo_done, b + 1)
                cols = bass.ds(b * L, L)
                dve.scalar_tensor_tensor(k.x[:, cols], q_ps[1][:, 0:L], k.mod[:, 1, 2, bass.ds(b, 1)], k.x[:, cols],
                                         ALU.mult, ALU.add).then_inc(x_done, 1)

            def body(b):
                for p in range(NH):
                    maxima(b, p)
                    if p == 0 and not last(b):
                        take_h(b + 1)
                    if p == NH - 1 and not last(b):
                        split_k(b + 1)
                    behind(normalise, b, p, NORM)
                    if p == VALUES:
                        v_copy(b)
                    if p == OUT_AT + R1 and not starts(b):
                        add_x(b - 1)
                    if p == Q_AT + 3 and not last(b):
                        split_q(b + 1, 0)
                if not last(b):
                    split_q(b + 1, 1)

            def end():
                for p in range(NH - NORM, NH):
                    normalise(B - 1, p)
                add_x(B - 1)

            batches(dve, first, body, end)

        @block.tensor
        def _(pe):
            def project_q(b, r):
                if r == 0:
                    pe.wait_ge(xr_ready, b + 1)
                    since(pe, v_ready, b)
                    since(pe, k_out, b)
                if r == R1 // 2:
                    since(pe, q_high_out, b)
                    since(pe, x_done, b - 1)
                mm = pe.matmul(q_ps[r // 2][:, L * (r % 2):L * (r % 2) + L], w_q[:, r, :], xr[:], start=True, stop=True)
                if r % 2 == 1:
                    mm.then_inc(q_done, 1)

            def project_kv(b):
                pe.wait_ge(q_low_out, b + 1)
                pe.matmul(q_ps[0][:, 0:L], w_k[:], xr[:], start=True, stop=True)
                for t in range(2):
                    c0 = L + t * G1 * D1
                    mm = pe.matmul(q_ps[0][:, c0:c0 + G1 * D1], xr[:, P * t:P * t + P], w_v[:], start=True, stop=True)
                mm.then_inc(k_done, 1)

            def first():
                pe.wait_ge(loaded, 16 * 7)
                for r in range(R1):
                    project_q(0, r)
                project_kv(0)

            def scores(b, p):
                r, c = HEADS[p]
                if p == 0:
                    pe.wait_ge(k_out, b + 1)
                if p == NH // 2:
                    pe.wait_ge(q_high_out, b + 1)
                since(pe, masked_done, NH * b + p - 1)
                rows = slice(32 * c, 32 * c + 3 * D1)
                for i, cols in enumerate(BLOCKS):
                    mm = pe.matmul(s_ps[p % 2][:, cols], q[rows, r, P * i:P * i + P], kk[rows, 0:P * (i + 1)],
                                   start=True, stop=True)
                mm.then_inc(s_done, 1)

            def turn(b, p):
                pe.wait_ge(normed, NH * b + p + 1)
                since(pe, pt_out, NH * b + p - 1)
                for i in range(W // P):
                    mm = pe.transpose(pt_ps[p % 2][:, P * i:P * i + P], probs[:, p % SLOTS, P * i:P * i + P], k.ident[:])
                mm.then_inc(pt_done, 1)

            def values(b, p):
                r, c = HEADS[p]
                if p == 0:
                    pe.wait_ge(v_ready, b + 1)
                    since(pe, o_low_out, b)
                if p == NH // 2:
                    since(pe, o_high_out, b)
                pe.wait_ge(pt_out, NH * b + p + 1)
                out = o_ps[r // 2][32 * c:32 * c + 32, L * (r % 2):L * (r % 2) + L]
                pe.matmul(out, v[:, 0, c, :], turned[:, p % 2, 0:L], start=True, stop=False, skip_group_check=True,
                          tile_position=(0, 32 * c))
                pe.matmul(out[:, P:L], v[:, 1, c, :], turned[:, p % 2, L:W], start=False, stop=True,
                          skip_group_check=True, tile_position=(0, 32 * c)).then_inc(pv_done, 1)

            def project_out(b, r):
                if r == 0:
                    pe.wait_ge(o_low_out, b + 1)
                    pe.wait_ge(o_high_out, b + 1)
                mm = pe.matmul(q_ps[1][:, 0:L], w_o[:, r, :], o[:, r, :], start=(r == 0), stop=(r == R1 - 1))
                if r == R1 - 1:
                    mm.then_inc(wo_done, 1)

            def body(b):
                for p in range(NH):
                    scores(b, p)
                    behind(turn, b, p, TURN)
                    behind(values, b, p, VALUES)
                    if OUT_AT <= p < OUT_AT + R1 and not starts(b):
                        if p == OUT_AT:
                            pe.wait_ge(q_high_out, b + 1)
                        project_out(b - 1, p - OUT_AT)
                    if Q_AT <= p < Q_AT + R1 and not last(b):
                        project_q(b + 1, p - Q_AT)
                    if p == Q_AT + R1 and not last(b):
                        project_kv(b + 1)

            def end():
                for p in range(NH, NH + VALUES):
                    if p - TURN < NH:
                        turn(B - 1, p - TURN)
                    values(B - 1, p - VALUES)
                for r in range(R1):
                    project_out(B - 1, r)

            batches(pe, first, body, end)


def experts1_stage(k):
    nc = k.nc
    with ExitStack() as ctx:
        def sb(name, shape, dtype=F32):
            return ctx.enter_context(nc.sbuf_tensor(name, shape, dtype))

        def sem(name):
            return ctx.enter_context(nc.semaphore(name))

        def bank(name):
            return ctx.enter_context(nc.psum_tensor(name, [P, CH], F32))

        ITEMS = [(e, n) for e in range(E1) for n in range(NCH)]
        NI = len(ITEMS)
        NF = NI * FC1
        SLOTS = 4
        LATE = [(3, 3), (4, 1), (4, 3), (5, 1), (5, 3)]
        ROUTE = [7, 10, 11, 12, 13]
        BY_DVE = FC1 - 1
        DOWN = 2
        WE = F1 + FC1 * P
        r = Router(k, ctx, "r1", E1, renormalised=True)
        hs = k.xhat
        xn, acc = sb("x_normed", [P, T]), sb("acc", [P, T])
        pars = sb("pars", [P, LY, NPAR])
        b1 = sb("e1_b1", [P, E1 * FC1])
        raw = sb("e1_w_raw", [P, 2, WE])
        w_high, w_rest = sb("e1_w_high", [P, E1, WE], F32R), sb("e1_w_rest", [P, E1, WE], F32R)
        xe = sb("e1_x", [P, 2, CH])
        xe_high, xe_rest = sb("e1_x_high", [P, 2, CH], F32R), sb("e1_x_rest", [P, 2, CH], F32R)
        hid = sb("e1_hidden", [P, SLOTS, CH])
        hid_high, hid_rest = sb("e1_hidden_high", [P, SLOTS, CH], F32R), sb("e1_hidden_rest", [P, SLOTS, CH], F32R)
        t, tw = sb("e1_sum", [P, 4, CH]), sb("e1_weighted", [P, 2, CH])
        HB = 2
        h_ps, y_ps = [bank(f"h1_{i}") for i in range(HB)], [bank(f"y1_{i}") for i in range(2)]
        comb_ps, mean_ps, wide_ps, small_ps = bank("e1_comb_ps"), bank("mean1"), bank("e1_wide"), bank("e1_small_ps")
        logits_ps = comb_ps[:, 0:TB * E1].rearrange("p (t e) -> p t e", e=E1)
        norm = Norm(k, ctx, "n1", [mean_ps], [wide_ps], small_ps[:, CH - TB:CH])
        small, w_in = sem("e1_small"), [sem(f"e1_w_in{e}") for e in range(E1)]
        high_done, rest_done, xe_ready, xe_high_ready, xe_rest_ready, h_done, gelu_done, hid_ready, down_done = (
            sem(f"e1_{n}") for n in ("w_high", "w_rest", "xe", "xe_high", "xe_rest", "h", "gelu", "hid", "down"))
        comb_done, t_done, tw_done, added, final, hid_high_done, x_done, stored = (
            sem(f"e1_{n}") for n in ("comb", "t", "tw", "added", "final", "hid_high", "x", "stored"))
        block = ctx.enter_context(nc.Block())

        def par(l, i):
            return pars[:, bass.ds(l, 1), i:i + 1].rearrange("p l n -> p (l n)")

        def layers(eng, first, layer):
            first()
            layer(0)
            with eng.Fori(1, LY - 1) as l:
                layer(l)
            layer(LY - 1)

        def last(l):
            return isinstance(l, int) and l == LY - 1

        def starts(l):
            return isinstance(l, int) and l == 0

        def ahead(step, l, i):
            if i + 1 < NI:
                step(l, i + 1)
            elif not last(l):
                step(l + 1, 0)

        def norm_steps(l, i, delay):
            n = i - delay - (NI - NCH + 2)
            if n >= 0:
                if not last(l):
                    return l + 1, n
            elif n + NI < NCH and not (starts(l) and n + NI < 2 - delay):
                return l, n + NI
            return None

        def ready_early(l, i):
            return not norm_steps(l, i, 1)

        SPLITS = {2: (0, 3), 6: (1, 0), 10: (1, 1), 13: (1, 2)}
        FIRST_SPLITS = {2: (0, 1), 4: (0, 2), 7: (0, 3), 9: (1, 0), 11: (1, 1), 13: (1, 2)}

        def split_of(l, i):
            later, e = (FIRST_SPLITS if starts(l) else SPLITS).get(i, (0, None))
            if e is None or (later and last(l)):
                return None
            return l + later, e

        @block.sync
        def _(sp):
            load_parts(sp, small, [(pars[:], k.d["pars"]), (r.order[:], k.d["order1"])])

            def layer(l):
                for e in range(E1):
                    since(sp, rest_done, E1 * l + e - 1)
                    sp.dma_start(raw[:, e % 2, 0:F1], k.d["e1_w1"][:, bass.ds(l, 1), e, :].rearrange("p l f -> p (l f)"))\
                      .then_inc(w_in[e], 16)
                    sp.dma_start(raw[:, e % 2, F1:WE], k.d["e1_w2"][:, bass.ds(l, 1), e, :].rearrange("p l f -> p (l f)"))\
                      .then_inc(w_in[e], 16)

            layers(sp, lambda: None, layer)
            for n in range(NCH):
                cols = slice(n * CH, n * CH + CH)
                sp.wait_ge(x_done, n + 1)
                sp.dma_start(k.out[:, cols], k.x[:, cols]).then_inc(stored, 16)
            sp.wait_ge(stored, 16 * NCH)

        @block.gpsimd
        def _(pool):
            def split_rest(l, e):
                pool.wait_ge(high_done, E1 * l + e + 1)
                pool.tensor_tensor(w_rest[:, e, :], raw[:, e % 2, :], w_high[:, e, :].bitcast(F32), ALU.subtract)\
                    .then_inc(rest_done, 1)

            def x_rest(l, i):
                pool.wait_ge(xe_high_ready, NI * l + i + 1)
                pool.tensor_tensor(xe_rest[:, i % 2, :], xe[:, i % 2, :], xe_high[:, i % 2, :].bitcast(F32),
                                   ALU.subtract).then_inc(xe_rest_ready, 1)

            def add(l, i):
                e, n = ITEMS[i]
                cols = slice(n * CH, (n + 1) * CH)
                pool.wait_ge(tw_done, NI * l + i + 1)
                since(pool, added, NADD * l + i + 1 - 2 * NCH)
                pool.tensor_tensor(acc[:, cols], acc[:, cols], tw[:, i % 2, :], ALU.add).then_inc(added, 1)

            def first():
                norm.pool_root(pool, 0, 0)
                x_rest(0, 0)

            def layer(l):
                for i in range(NI):
                    end = norm_steps(l, i, 1)
                    if end:
                        norm.pool_root(pool, end[1], NCH * end[0] + end[1])
                    ahead(x_rest, l, i)
                    if 1 <= ITEMS[i - 1][0] < E1 - 1 and i >= 1:
                        add(l, i - 1)
                    at = split_of(l, i)
                    if at:
                        split_rest(*at)

            layers(pool, first, layer)

        @block.scalar
        def _(act):
            def x_high(l, i):
                act.wait_ge(xe_ready, NI * l + i + 1)
                since(act, h_done, NF * l + FC1 * (i - 1))
                act.activation(xe_high[:, i % 2, :], xe[:, i % 2, :], ACT.Copy).then_inc(xe_high_ready, 1)

            def gelu(l, f):
                i, fc = f // FC1, f % FC1
                act.wait_ge(h_done, NF * l + f + 1)
                since(act, down_done, NF * l + f + 1 - SLOTS)
                c = FC1 * ITEMS[i][0] + fc
                op = act.activation(hid[:, f % SLOTS, :], h_ps[f % HB][:], ACT.Gelu, bias=b1[:, c:c + 1])
                if fc != BY_DVE:
                    op = act.activation(hid_high[:, f % SLOTS, :], h_ps[f % HB][:], ACT.Gelu, bias=b1[:, c:c + 1])
                op.then_inc(gelu_done, 1)

            def first():
                norm.act_square(act, xn, 0, 0)
                norm.act_square(act, xn, 1, 1)
                act.wait_ge(small, 32)
                x_high(0, 0)

            def layer(l):
                for f in range(NF):
                    i, fc = f // FC1, f % FC1
                    at = norm_steps(l, i, 0)
                    if fc == 2 and at:
                        norm.act_square(act, xn, at[1], NCH * at[0] + at[1])
                    if fc == (2 if ready_early(l, i) else 3):
                        ahead(x_high, l, i)
                    gelu(l, f)
                    if f == ROUTE[1] - 1:
                        r.exps(act, l)

            layers(act, first, layer)

        @block.vector
        def _(dve):
            def split_high(l, e):
                dve.wait_ge(w_in[e], 32 * (l + 1))
                since(dve, down_done, NF * (l - 1) + NCH * FC1 * (e + 1))
                c = FC1 * e
                dve.tensor_copy(b1[:, c:c + FC1], pars[:, bass.ds(l, 1), 3 * E1 + c:3 * E1 + c + FC1]
                                .rearrange("p l n -> p (l n)"))
                dve.tensor_copy(w_high[:, e, :], raw[:, e % 2, :]).then_inc(high_done, 1)

            def scale_x(l, i):
                e, n = ITEMS[i]
                dve.wait_ge(norm.normed, norm.base + NCH * l + n + 1)
                since(dve, xe_rest_ready, NI * l + i - 1)
                dve.tensor_scalar(xe[:, i % 2, :], xn[:, n * CH:(n + 1) * CH], par(l, e), par(l, E1 + e),
                                  ALU.mult, ALU.add).then_inc(xe_ready, 1)

            def hid_split(l, f):
                dve.wait_ge(gelu_done, NF * l + f + 1)
                if f % FC1 == BY_DVE:
                    dve.tensor_copy(hid_high[:, f % SLOTS, :], hid[:, f % SLOTS, :]).then_inc(hid_high_done, 1)
                    dve.wait_ge(hid_high_done, NI * l + f // FC1 + 1)
                dve.tensor_tensor(hid_rest[:, f % SLOTS, :], hid[:, f % SLOTS, :],
                                  hid_high[:, f % SLOTS, :].bitcast(F32), ALU.subtract).then_inc(hid_ready, 1)

            def expert_out(l, i):
                e, n = ITEMS[i]
                dve.wait_ge(down_done, NF * l + FC1 * (i + 1))
                since(dve, tw_done, NI * l + i - 3)
                dve.scalar_tensor_tensor(t[:, i % 4, :], y_ps[i % 2][:], par(l, 2 * E1 + e),
                                         hs[:, n * CH:(n + 1) * CH], ALU.add, ALU.add).then_inc(t_done, 1)

            def weighted(l, i):
                e, n = ITEMS[i]
                dve.wait_ge(t_done, NI * l + i + 1)
                dve.wait_ge(comb_done, NI * l + i + 1)
                if e > 0:
                    since(dve, added, NADD * l + min(i - NCH - 1, NADD))
                out = acc[:, n * CH:(n + 1) * CH] if e == 0 else tw[:, i % 2, :]
                dve.tensor_tensor(out, t[:, i % 4, :], comb_ps[:], ALU.mult).then_inc(tw_done, 1)
                if e == E1 - 1:
                    dve.wait_ge(tw_done, NI * l + i + 1)
                    dve.tensor_tensor(hs[:, n * CH:(n + 1) * CH], acc[:, n * CH:(n + 1) * CH], tw[:, i % 2, :],
                                      ALU.add).then_inc(final, 1)

            def first():
                dve.wait_ge(small, 32)
                norm.dve_center(dve, hs, xn, 0, 0)
                split_high(0, 0)
                norm.dve_add_eps(dve, 0, 0)
                dve.wait_ge(high_done, 1)
                dve.tensor_tensor(w_rest[:, 0, :], raw[:, 0, :], w_high[:, 0, :].bitcast(F32), ALU.subtract)\
                   .then_inc(rest_done, 1)
                norm.dve_center(dve, hs, xn, 1, 1)
                norm.dve_scale(dve, xn, 0, 0)
                scale_x(0, 0)

            def layer(l):
                for f in range(NF):
                    i, fc = f // FC1, f % FC1
                    at, end = norm_steps(l, i, 0), norm_steps(l, i, 1)
                    if fc == 0 and end:
                        norm.dve_add_eps(dve, end[1], NCH * end[0] + end[1])
                    if fc == 1 and at:
                        norm.dve_center(dve, hs, xn, at[1], NCH * at[0] + at[1])
                    if fc == 2 and end:
                        norm.dve_scale(dve, xn, end[1], NCH * end[0] + end[1])
                    if fc == (0 if ready_early(l, i) else 2):
                        ahead(scale_x, l, i)
                    hid_split(l, f)
                    if f in ROUTE:
                        r.route(dve, ROUTE.index(f), logits_ps,
                                pars[:, bass.ds(l, 1), NPAR - TB * E1:NPAR].rearrange("p l (t e) -> p (l t) e", e=E1), l)
                    if (i, fc) in LATE:
                        weighted(l, LATE.index((i, fc)))
                    if fc == 1:
                        if i >= 1:
                            expert_out(l, i - 1)
                            if i > len(LATE):
                                weighted(l, i - 1)
                        elif not starts(l):
                            expert_out(l - 1, NI - 1)
                            weighted(l - 1, NI - 1)
                    at = split_of(l, i)
                    if fc == 3 and at:
                        split_high(*at)
                    if fc == 3 and last(l) and i >= NI - 2:
                        add_x(i - (NI - 2))

            def add_x(n):
                dve.wait_ge(final, NCH * (LY - 1) + n + 1)
                for b in range(2 * n, 2 * n + 2):
                    cols = slice(b * L, b * L + L)
                    op = dve.scalar_tensor_tensor(k.x[:, cols], hs[:, cols], k.mod[:, 1, 5, b:b + 1], k.x[:, cols],
                                                  ALU.mult, ALU.add)
                op.then_inc(x_done, 1)

            layers(dve, first, layer)
            expert_out(LY - 1, NI - 1)
            weighted(LY - 1, NI - 1)
            for n in range(NCH - 2, NCH):
                add_x(n)

        @block.tensor
        def _(pe):
            def up(l, f):
                i, fc = f // FC1, f % FC1
                e, n = ITEMS[i]
                if fc == 0:
                    if n == 0:
                        pe.wait_ge(rest_done, E1 * l + e + 1)
                    pe.wait_ge(xe_rest_ready, NI * l + i + 1)
                since(pe, gelu_done, NF * l + f + 1 - HB)
                cols = slice(fc * P, fc * P + P)
                products(pe, h_ps[f % HB][:], (w_high[:, e, cols], w_rest[:, e, cols]),
                         (xe_high[:, i % 2, :], xe_rest[:, i % 2, :]), True, True).then_inc(h_done, 1)

            def down(l, f):
                i, fc = f // FC1, f % FC1
                e = ITEMS[i][0]
                pe.wait_ge(hid_ready, NF * l + f + 1)
                if fc == 0:
                    since(pe, t_done, NI * l + i - 1)
                cols = slice(F1 + fc * P, F1 + fc * P + P)
                products(pe, y_ps[i % 2][:], (w_high[:, e, cols], w_rest[:, e, cols]),
                         (hid_high[:, f % SLOTS, :], hid_rest[:, f % SLOTS, :]), fc == 0, fc == FC1 - 1)\
                    .then_inc(down_done, 1)

            def comb(l, i):
                e, n = ITEMS[i]
                pe.wait_ge(r.comb_ready, l + 1)
                since(pe, tw_done, NI * l + i)
                blocks = slice(BPC * n, BPC * n + BPC)
                widen(pe, k, comb_ps, r.comb[:, blocks, e]).then_inc(comb_done, 1)

            def logits(l):
                since(pe, final, NCH * l)
                since(pe, tw_done, NI * l)
                for tb in range(TB):
                    mm = pe.matmul(logits_ps[:, tb, :], hs[:, tb * P:(tb + 1) * P],
                                   pars[:, bass.ds(l, 1), ROUTER:ROUTER + E1].rearrange("p l e -> p (l e)"),
                                   start=True, stop=True)
                mm.then_inc(r.logits_done, 1)

            def mean(l, n):
                since(pe, final, NCH * l - (NCH - 1 - n))
                norm.pe_mean(pe, hs, n, NCH * l + n)

            def first():
                mean(0, 0)
                norm.pe_var(pe, 0, 0)
                mean(0, 1)
                norm.pe_wide(pe, 0, 0)
                norm.pe_var(pe, 1, 1)
                pe.wait_ge(small, 32)

            def layer(l):
                for f in range(NF):
                    i, fc = f // FC1, f % FC1
                    up(l, f)
                    at, end = norm_steps(l, i, 0), norm_steps(l, i, 1)
                    if fc == 0 and at:
                        mean(*at)
                    if fc == 1 and end:
                        norm.pe_wide(pe, end[1], NCH * end[0] + end[1])
                    if fc == 3 and at:
                        norm.pe_var(pe, at[1], NCH * at[0] + at[1])
                    if (i, fc) == (1, 2):
                        logits(l)
                    if (i, fc) in LATE:
                        comb(l, LATE.index((i, fc)))
                    if fc == 1 and i > len(LATE):
                        comb(l, i - 1)
                    if fc == 1 and i == 0 and not starts(l):
                        comb(l - 1, NI - 1)
                    if f >= DOWN:
                        down(l, f - DOWN)
                    elif not starts(l):
                        down(l - 1, f - DOWN + NF)

            layers(pe, first, layer)
            for f in range(NF - DOWN, NF):
                down(LY - 1, f)
            comb(LY - 1, NI - 1)


def build(nc, k):
    with ExitStack() as ctx:
        def sb(name, shape):
            return ctx.enter_context(nc.sbuf_tensor(name, shape, F32))

        k.x = sb("x", [P, T])
        k.xhat = sb("xhat", [P, T])
        k.ident = sb("ident", [P, P])
        k.mean_mat = sb("mean_mat", [P, P])
        k.mod = sb("mod", [P, 2, 6, B])
        k.neg_half = sb("neg_half", [P, 1])
        k.norm_semaphores = [ctx.enter_context(nc.semaphore(f"norm_{n}")) for n in Norm.SEMAPHORES]
        k.chunks_normed = 0
        with ExitStack() as inputs:
            loads = attention0_inputs(k, inputs)
            setup_stage(k, loads, k.attention0_inputs[-1])
            norm_stage(k, "n0a")
            attention0_stage(k)
        norm_stage(k, "n0b", 0, 3)
        experts0_stage(k)
        norm_stage(k, "n1a", 1, 0)
        attention1_stage(k)
        norm_stage(k, "n1b", 1, 3)
        experts1_stage(k)



def constants():
    f = np.float32
    inv = (f(1.0) / np.power(f(10000.0), np.arange(0, D0, 2, dtype=f) / f(D0))).astype(f)
    ang = np.outer(np.arange(L, dtype=f), inv).astype(f)
    cos, sin = np.cos(ang).astype(f).T, np.sin(ang).astype(f).T
    rope0 = np.stack([np.tile(cos, (4, 1)), np.concatenate([-sin, sin, -sin, sin], 0)], 1)
    t = np.arange(SPAN)[None, :] - (L - IG)
    row = np.arange(P)[:, None] // H0
    signed = row - t
    swapped = (row + IG // 2) % IG - t
    dist = np.stack([np.abs(signed), np.abs(swapped), np.where(signed < 0, NEG, 0.0)], 1).astype(f)
    return {"rope0": rope0, **more_constants(), "dist": dist, "ident": np.eye(P, dtype=f), "mean_mat": np.full((P, P), 1.0 / P, f)}


def more_constants():
    f = np.float32
    half = P // 2
    theta = (f(1.0) / np.power(f(10000.0), np.arange(half, dtype=f) / f(half))).astype(f)
    ang = (np.arange(L, dtype=f)[:, None] * theta[None, :]).astype(f)
    cos, sin = np.cos(ang).astype(f).T, np.sin(ang).astype(f).T
    rope1 = np.stack([np.concatenate([cos, cos], 0), np.concatenate([sin, -sin], 0)], 1)
    future = np.arange(P + L)[None, :] - P > np.arange(P)[:, None]
    part = np.arange(P) % 32 // D1
    out = {"rope1": rope1, "mask1": np.where(future, -1.0e9, 0.0).astype(f),
           "rest1": np.stack([-1.0 * (part == 1), -1.0 * (part == 2)], 1).astype(f)}
    for n, e in (("0", E0), ("1", E1)):
        out["order" + n] = np.ascontiguousarray(np.broadcast_to(np.arange(e, 0, -1).astype(f), (P, TB, e)))
    return out


EVEN_FIRST = np.concatenate([np.arange(0, P, 2), np.arange(1, P, 2)])


def laid_out(i):
    a = {n: np.asarray(v) for n, v in i.items()}
    f = np.float32
    ch = EVEN_FIRST
    w = a["L0_attn_w_qkv"][ch].reshape(P, 3, H0, D0)
    rotated = np.concatenate([w[..., D0 // 2:], w[..., :D0 // 2]], -1)
    w_qk = np.stack([w[:, 0:2], rotated[:, 0:2]], 0)
    w_qk = w_qk.reshape(2, P, 2, PAIRS, P).transpose(1, 3, 2, 0, 4).reshape(P, 2 * PAIRS, 2, P)
    w1 = a["L0_attn_w1"]
    w1a, w1b, w2 = np.zeros((P, P), f), np.zeros((P, P), f), np.zeros((P, 64), f)
    for q in range(4):
        m = slice(32 * q, 32 * q + 32)
        lo, hi = slice(16 * q, 16 * q + 16), slice(64 + 16 * q, 80 + 16 * q)
        w1a[lo, m], w1a[hi, m] = w1[:H0], w1[H0:]
        w1b[lo, m], w1b[hi, m] = w1[H0:], w1[:H0]
        w2[m, lo] = a["L0_attn_w2"]
    cols = np.stack([np.tile(a["L0_attn_log_p"].reshape(-1), IG), np.tile(a["L0_attn_log_a"].reshape(-1), IG),
                     np.tile(a["L0_attn_b2"], IG), np.tile(a["L0_attn_b1"], 4)], 1)
    w_q = np.zeros((P, R1, P), f)
    w_k = np.zeros((P, P), f)
    w_o = np.zeros((P, R1, P), f)
    for c in range(G1):
        w_k[:, 32 * c:32 * c + 3 * D1] = np.tile(a["L1_attn_W_k"][D1 * c:D1 * c + D1].T, (1, 3))
        for r in range(R1):
            hd = R1 * c + r
            w_q[:, r, 32 * c:32 * c + 3 * D1] = np.tile(a["L1_attn_W_q"][D1 * hd:D1 * hd + D1].T, (1, 3))
            w_o[32 * c:32 * c + D1, r, :] = a["L1_attn_W_o"][ch, D1 * hd:D1 * hd + D1].T
    wide = FC0 * P
    e0_w1, e0_w3, e0_w2 = np.zeros((P, E0, wide), f), np.zeros((P, E0, wide), f), np.zeros((E0, wide, P), f)
    e0_w1[:, :, :F0] = a["L0_ffn_w1"].transpose(1, 0, 2)[ch]
    e0_w3[:, :, :F0] = a["L0_ffn_w3"].transpose(1, 0, 2)[ch]
    e0_w2[:, :F0] = a["L0_ffn_w2"][:, :, ch]
    lg, lb, l2 = (a[n][:, :, ch].transpose(2, 0, 1) for n in ("L1_ffn_ln_g", "L1_ffn_ln_b", "L1_ffn_b2"))
    b1 = a["L1_ffn_b1"].reshape(LY, E1, FC1, P).transpose(3, 0, 1, 2).reshape(P, LY, E1 * FC1)
    rw = a["L1_ffn_router_w"][:, ch].transpose(1, 0, 2)
    rb = np.broadcast_to(np.tile(a["L1_ffn_router_b"], (1, TB))[None], (P, LY, TB * E1))
    d = {
        "x": a["L0_attn_x"].reshape(T, P).T[ch],
        "c": np.stack([a["L0_c"].T, a["L1_c"].T], 1),
        "wmod": np.stack([a["L0_wmod"].reshape(P, 6, P)[:, :, ch], a["L1_wmod"].reshape(P, 6, P)[:, :, ch]], 1),
        "w_qk": w_qk, "w_v": w[:, 2].reshape(P, H0 * D0),
        "w_o0": a["L0_attn_w_o"].reshape(PAIRS, P, P).transpose(1, 0, 2)[:, :, ch],
        "w1a": w1a, "w1b": w1b, "w2": w2, "head_cols": cols,
        "gate_w": a["L0_ffn_gate_w"].T[ch], "e0_w1": e0_w1, "e0_w3": e0_w3,
        "e0_w2": e0_w2.reshape(E0, FC0, P, P).transpose(2, 0, 1, 3),
        "w_q1": w_q, "w_k1": w_k, "w_v1": a["L1_attn_W_v"].T, "w_o1": w_o,
        "pars": np.concatenate([lg, lb, l2, b1, rw, rb], 2),
        "e1_w1": a["L1_ffn_w1"].transpose(2, 0, 1, 3)[ch],
        "e1_w2": a["L1_ffn_w2"][:, :, :, ch].reshape(LY, E1, FC1, P, P).transpose(3, 0, 1, 2, 4)
                 .reshape(P, LY, E1, FC1 * P),
    }
    d.update(constants())
    return {n: np.ascontiguousarray(v) for n, v in d.items()}


def kernel(**inputs):
    import concourse.bacc as bacc
    from concourse.bass_utils import run_bass_kernel_spmd

    nc = bacc.Bacc("TRN2", target_bir_lowering=False, num_devices=1)
    k = Kit()
    k.nc, k.d = nc, {}
    arrays = {}
    for name, a in laid_out(inputs).items():
        arrays[f"in_{name}"] = a
        k.d[name] = nc.dram_tensor(f"in_{name}", a.shape, mybir.dt.from_np(a.dtype), kind="ExternalInput").ap()
    k.out = nc.dram_tensor("out_x", (P, T), F32, kind="ExternalOutput").ap()
    build(nc, k)
    r = run_bass_kernel_spmd(nc, [arrays], core_ids=[0])
    return np.ascontiguousarray(r.results[0]["out_x"][np.argsort(EVEN_FIRST)].T).reshape(B, L, P)
```
